# Optimizing a Trainium2 kernel written in Bass

```python
import numpy as np
import jax
import jax.numpy as jnp

def _softmax(x, axis=-1):
    return jax.nn.softmax(x, axis=axis)

def _gelu(x):
    return jax.nn.gelu(x, approximate=True)

def _silu(x):
    return jax.nn.silu(x)

def _sigmoid(x):
    return jax.nn.sigmoid(x)

def _layernorm(x, axis=-1, eps=1e-05):
    m = jnp.mean(x, axis=axis, keepdims=True)
    v = jnp.var(x, axis=axis, keepdims=True)
    return (x - m) / jnp.sqrt(v + eps)

def _scatter_add(tgt, idx, src, axis=0):
    return tgt.at[idx].add(src)

def _segment_sum(src, seg, n):
    return jax.ops.segment_sum(src, seg, n)
kernel_name = 'mk_adaln_d2_jaxref_r4_5487fd'

def setup_inputs(seed: int=0):
    np.random.seed(seed)
    _w = jnp.asarray

    def _L0_attn_setup():
        import jax, jax.numpy as jnp
        import numpy as np
        NUM_HEADS = 16
        WINDOW = 64
        key = jax.random.key(seed)
        ks = jax.random.split(key, 6)
        b, l, d = (2, 512, 256)
        s = 1.0 / np.sqrt(d)
        return {'x': jax.random.normal(ks[0], (b, l, d), dtype=jnp.float32), 'Wq': jax.random.normal(ks[1], (d, d), dtype=jnp.float32) * s, 'Wk': jax.random.normal(ks[2], (d, d), dtype=jnp.float32) * s, 'Wv': jax.random.normal(ks[3], (d, d), dtype=jnp.float32) * s, 'Wo': jax.random.normal(ks[4], (d, d), dtype=jnp.float32) * s, 'bo': jax.random.normal(ks[5], (d,), dtype=jnp.float32) * 0.01}
    _L0_attn_in = _L0_attn_setup()

    def _L0_ffn_setup():
        import jax, jax.numpy as jnp
        import numpy as np
        B, T, C = (2, 512, 256)
        H, D = (16, 64)
        CR = 8
        R = C // CR
        ROPE = D // 2
        NOPE = D - ROPE
        E, K, I, S = (8, 2, 128, 1)
        THETA = 100000.0
        EPS = 1e-05

        def _rmsnorm(x, w):
            rms = jnp.sqrt(jnp.mean(x * x, axis=-1, keepdims=True) + EPS)
            return w * (x / rms)

        def _rope(xh):
            d = xh.shape[-1]
            t = jnp.arange(xh.shape[2], dtype=jnp.float32)
            freqs = 1.0 / THETA ** (jnp.arange(0, d, 2, dtype=jnp.float32) / d)
            ang = jnp.outer(t, freqs)
            cos, sin = (jnp.cos(ang), jnp.sin(ang))
            xr = xh.reshape(xh.shape[:-1] + (d // 2, 2))
            x0, x1 = (xr[..., 0], xr[..., 1])
            rot = jnp.stack([x0 * cos - x1 * sin, x0 * sin + x1 * cos], axis=-1)
            return rot.reshape(xh.shape)

        def _attention(x, Wq, Wkva, Wkvb, Wo):
            b, t, _ = x.shape
            q = (x @ Wq).reshape(b, t, H, D).transpose(0, 2, 1, 3)
            ckv = x @ Wkva
            kv_latent, k_rope = (ckv[:, :, :R], ckv[:, :, R:])
            kv = (kv_latent @ Wkvb).reshape(b, t, H, NOPE).transpose(0, 2, 1, 3)
            k_rope = jnp.broadcast_to(k_rope[:, None, :, :], (b, H, t, ROPE))
            q_nope, q_rope = (q[..., :NOPE], q[..., NOPE:])
            q = jnp.concatenate([q_nope, _rope(q_rope)], axis=-1)
            k = jnp.concatenate([kv, _rope(k_rope)], axis=-1)
            v = jnp.concatenate([kv, jnp.zeros_like(k_rope)], axis=-1)
            att = jnp.einsum('bhqd,bhkd->bhqk', q, k) / jnp.sqrt(jnp.float32(D))
            mask = jnp.tril(jnp.ones((t, t), dtype=bool))
            att = jnp.where(mask, att, jnp.float32(-jnp.inf))
            att = jax.nn.softmax(att, axis=-1)
            y = jnp.einsum('bhqk,bhkd->bhqd', att, v)
            y = y.transpose(0, 2, 1, 3).reshape(b, t, H * D)
            return y @ Wo

        def _experts(x_flat, Wg, Wu, Wd):
            g = jax.nn.silu(jnp.einsum('nc,eci->nei', x_flat, Wg))
            u = jnp.einsum('nc,eci->nei', x_flat, Wu)
            return jnp.einsum('nei,eic->nec', g * u, Wd)

        def _moe(x, Wgate, expert_bias, Wg, Wu, Wd, sWg, sWu, sWd):
            b, t, c = x.shape
            xf = x.reshape(-1, c)
            shared = jnp.mean(_experts(xf, sWg, sWu, sWd), axis=1)
            logits = xf @ Wgate + expert_bias
            probs = jax.nn.softmax(logits, axis=-1)
            topk_p, topk_i = jax.lax.top_k(probs, K)
            topk_p = topk_p / jnp.sum(topk_p, axis=-1, keepdims=True)
            comb = jnp.sum(jax.nn.one_hot(topk_i, E, dtype=xf.dtype) * topk_p[..., None], axis=1)
            routed = jnp.einsum('ne,nec->nc', comb, _experts(xf, Wg, Wu, Wd))
            return (shared + routed).reshape(b, t, c)
        key = jax.random.key(seed)
        ks = jax.random.split(key, 16)
        w = lambda k, shp: jax.random.normal(k, shp, dtype=jnp.float32) * 0.02
        return {'x': jax.random.normal(ks[0], (B, T, C), dtype=jnp.float32), 'w_ln1': jnp.ones((C,), jnp.float32), 'Wq': w(ks[1], (C, H * D)), 'Wkva': w(ks[2], (C, R + ROPE)), 'Wkvb': w(ks[3], (R, H * NOPE)), 'Wo': w(ks[4], (H * D, C)), 'w_ln2': jnp.ones((C,), jnp.float32), 'Wgate': w(ks[5], (C, E)), 'expert_bias': jnp.zeros((E,), jnp.float32), 'Wg': w(ks[6], (E, C, I)), 'Wu': w(ks[7], (E, C, I)), 'Wd': w(ks[8], (E, I, C)), 'sWg': w(ks[9], (S, C, I)), 'sWu': w(ks[10], (S, C, I)), 'sWd': w(ks[11], (S, I, C))}
    _L0_ffn_in = _L0_ffn_setup()
    _L0_c = _w((lambda *s: np.random.randn(*s).astype(np.float32) * 0.05)(4, 256))
    _L0_wmod = _w((lambda *s: np.random.randn(*s).astype(np.float32) * 0.05)(256, 6 * 256) * 256 ** (-0.5))

    def _L1_attn_setup():
        import jax, jax.numpy as jnp
        import numpy as np
        DIM = 256
        SEQ = 1024
        BATCH = 4
        ROPE_BASE = 10000.0

        def rotate_half(x):
            x_even = x[..., 0::2]
            x_odd = x[..., 1::2]
            return jnp.stack((-x_odd, x_even), axis=-1).reshape(x.shape)

        def rope_tables(seq_len, dim, base=ROPE_BASE, dtype=jnp.float32):
            pos = jnp.arange(seq_len, dtype=jnp.float32)[:, None]
            inv_freq = 1.0 / base ** (jnp.arange(0, dim, 2, dtype=jnp.float32) / dim)
            freqs = pos * inv_freq
            cos = jnp.repeat(jnp.cos(freqs), 2, axis=-1).astype(dtype)
            sin = jnp.repeat(jnp.sin(freqs), 2, axis=-1).astype(dtype)
            return (cos, sin)
        key = jax.random.key(seed)
        kx, kq, kk, kv = jax.random.split(key, 4)
        s = 1.0 / np.sqrt(DIM)
        return {'x': jax.random.normal(kx, (BATCH, SEQ, DIM), dtype=jnp.float32), 'wq': jax.random.normal(kq, (DIM, DIM), dtype=jnp.float32) * s, 'wk': jax.random.normal(kk, (DIM, DIM), dtype=jnp.float32) * s, 'wv': jax.random.normal(kv, (DIM, DIM), dtype=jnp.float32) * s}
    _L1_attn_in = _L1_attn_setup()

    def _L1_ffn_setup():
        import jax, jax.numpy as jnp
        import numpy as np
        E = 16
        G = 4
        EPG = E // G
        K = 4
        TOPK_GROUP = 2
        PER_GROUP_K = K // TOPK_GROUP

        def _route(xf, router_w, correction_bias):
            S = xf.shape[0]
            logits = xf @ router_w.T
            scores = jax.nn.sigmoid(logits)
            sb = scores + correction_bias
            grp_top = jax.lax.top_k(sb.reshape(S, G, EPG), PER_GROUP_K)[0]
            group_scores = grp_top.sum(axis=-1)
            _, group_idx = jax.lax.top_k(group_scores, TOPK_GROUP)
            group_mask = jnp.zeros((S, G), sb.dtype).at[jnp.arange(S)[:, None], group_idx].set(1.0)
            score_mask = jnp.broadcast_to(group_mask[:, :, None], (S, G, EPG)).reshape(S, E)
            masked = jnp.where(score_mask > 0, sb, -jnp.inf)
            _, topk_idx = jax.lax.top_k(masked, K)
            w = jnp.take_along_axis(scores, topk_idx, axis=1)
            w = w / (w.sum(axis=-1, keepdims=True) + 1e-20)
            return (topk_idx, w, scores)
        key = jax.random.key(seed)
        ks = jax.random.split(key, 9)
        B, T, C, H, HS = (2, 256, 256, 64, 512)
        std = 0.02
        return {'x': jax.random.normal(ks[0], (B, T, C), jnp.float32), 'router_w': jax.random.normal(ks[1], (E, C), jnp.float32) * std, 'correction_bias': jnp.zeros((E,), jnp.float32), 'gate_w': jax.random.normal(ks[2], (E, C, H), jnp.float32) * std, 'up_w': jax.random.normal(ks[3], (E, C, H), jnp.float32) * std, 'down_w': jax.random.normal(ks[4], (E, H, C), jnp.float32) * std, 'shared_gate_w': jax.random.normal(ks[5], (HS, C), jnp.float32) * std, 'shared_up_w': jax.random.normal(ks[6], (HS, C), jnp.float32) * std, 'shared_down_w': jax.random.normal(ks[7], (C, HS), jnp.float32) * std}
    _L1_ffn_in = _L1_ffn_setup()
    _L1_c = _w((lambda *s: np.random.randn(*s).astype(np.float32) * 0.05)(4, 256))
    _L1_wmod = _w((lambda *s: np.random.randn(*s).astype(np.float32) * 0.05)(256, 6 * 256) * 256 ** (-0.5))
    _d = {'L0_attn_x': _L0_attn_in['x'], 'L0_attn_Wq': _L0_attn_in['Wq'], 'L0_attn_Wk': _L0_attn_in['Wk'], 'L0_attn_Wv': _L0_attn_in['Wv'], 'L0_attn_Wo': _L0_attn_in['Wo'], 'L0_attn_bo': _L0_attn_in['bo'], 'L0_ffn_w_ln1': _L0_ffn_in['w_ln1'], 'L0_ffn_Wq': _L0_ffn_in['Wq'], 'L0_ffn_Wkva': _L0_ffn_in['Wkva'], 'L0_ffn_Wkvb': _L0_ffn_in['Wkvb'], 'L0_ffn_Wo': _L0_ffn_in['Wo'], 'L0_ffn_w_ln2': _L0_ffn_in['w_ln2'], 'L0_ffn_Wgate': _L0_ffn_in['Wgate'], 'L0_ffn_expert_bias': _L0_ffn_in['expert_bias'], 'L0_ffn_Wg': _L0_ffn_in['Wg'], 'L0_ffn_Wu': _L0_ffn_in['Wu'], 'L0_ffn_Wd': _L0_ffn_in['Wd'], 'L0_ffn_sWg': _L0_ffn_in['sWg'], 'L0_ffn_sWu': _L0_ffn_in['sWu'], 'L0_ffn_sWd': _L0_ffn_in['sWd'], 'L0_c': _L0_c, 'L0_wmod': _L0_wmod, 'L1_attn_wq': _L1_attn_in['wq'], 'L1_attn_wk': _L1_attn_in['wk'], 'L1_attn_wv': _L1_attn_in['wv'], 'L1_ffn_router_w': _L1_ffn_in['router_w'], 'L1_ffn_correction_bias': _L1_ffn_in['correction_bias'], 'L1_ffn_gate_w': _L1_ffn_in['gate_w'], 'L1_ffn_up_w': _L1_ffn_in['up_w'], 'L1_ffn_down_w': _L1_ffn_in['down_w'], 'L1_ffn_shared_gate_w': _L1_ffn_in['shared_gate_w'], 'L1_ffn_shared_up_w': _L1_ffn_in['shared_up_w'], 'L1_ffn_shared_down_w': _L1_ffn_in['shared_down_w'], 'L1_c': _L1_c, 'L1_wmod': _L1_wmod}
    _x0 = _d['L0_attn_x']
    _d['L0_attn_x'] = jax.random.normal(jax.random.fold_in(jax.random.key(seed), 1), (4, 1024, 256), dtype=_x0.dtype)
    del _x0
    return _d

def reference(L0_attn_x, L0_attn_Wq, L0_attn_Wk, L0_attn_Wv, L0_attn_Wo, L0_attn_bo, L0_ffn_w_ln1, L0_ffn_Wq, L0_ffn_Wkva, L0_ffn_Wkvb, L0_ffn_Wo, L0_ffn_w_ln2, L0_ffn_Wgate, L0_ffn_expert_bias, L0_ffn_Wg, L0_ffn_Wu, L0_ffn_Wd, L0_ffn_sWg, L0_ffn_sWu, L0_ffn_sWd, L0_c, L0_wmod, L1_attn_wq, L1_attn_wk, L1_attn_wv, L1_ffn_router_w, L1_ffn_correction_bias, L1_ffn_gate_w, L1_ffn_up_w, L1_ffn_down_w, L1_ffn_shared_gate_w, L1_ffn_shared_up_w, L1_ffn_shared_down_w, L1_c, L1_wmod):

    def _L0_attn_ref(x, Wq, Wk, Wv, Wo, bo):
        import jax, jax.numpy as jnp
        import numpy as np
        NUM_HEADS = 16
        WINDOW = 64
        b, l, d = x.shape
        h, w = (NUM_HEADS, WINDOW)
        dh = d // h
        p = w // 2
        q = (x @ Wq.T).reshape(b, l, h, dh)
        xp = jnp.pad(x, ((0, 0), (p, p), (0, 0)))
        k = (xp @ Wk.T).reshape(b, l + 2 * p, h, dh)
        v = (xp @ Wv.T).reshape(b, l + 2 * p, h, dh)
        win_idx = jnp.arange(l)[:, None] + jnp.arange(w)[None, :]
        kw = k[:, win_idx]
        vw = v[:, win_idx]
        scale = 1.0 / np.float32(np.sqrt(dh))
        scores = jnp.einsum('blhd,blwhd->blhw', q, kw) * scale
        attn = jax.nn.softmax(scores, axis=-1)
        out = jnp.einsum('blhw,blwhd->blhd', attn, vw).reshape(b, l, d)
        return out @ Wo.T + bo

    def _L0_ffn_ref(x, w_ln1, Wq, Wkva, Wkvb, Wo, w_ln2, Wgate, expert_bias, Wg, Wu, Wd, sWg, sWu, sWd):
        import jax, jax.numpy as jnp
        import numpy as np
        B, T, C = (2, 512, 256)
        H, D = (16, 64)
        CR = 8
        R = C // CR
        ROPE = D // 2
        NOPE = D - ROPE
        E, K, I, S = (8, 2, 128, 1)
        THETA = 100000.0
        EPS = 1e-05

        def _rmsnorm(x, w):
            rms = jnp.sqrt(jnp.mean(x * x, axis=-1, keepdims=True) + EPS)
            return w * (x / rms)

        def _rope(xh):
            d = xh.shape[-1]
            t = jnp.arange(xh.shape[2], dtype=jnp.float32)
            freqs = 1.0 / THETA ** (jnp.arange(0, d, 2, dtype=jnp.float32) / d)
            ang = jnp.outer(t, freqs)
            cos, sin = (jnp.cos(ang), jnp.sin(ang))
            xr = xh.reshape(xh.shape[:-1] + (d // 2, 2))
            x0, x1 = (xr[..., 0], xr[..., 1])
            rot = jnp.stack([x0 * cos - x1 * sin, x0 * sin + x1 * cos], axis=-1)
            return rot.reshape(xh.shape)

        def _attention(x, Wq, Wkva, Wkvb, Wo):
            b, t, _ = x.shape
            q = (x @ Wq).reshape(b, t, H, D).transpose(0, 2, 1, 3)
            ckv = x @ Wkva
            kv_latent, k_rope = (ckv[:, :, :R], ckv[:, :, R:])
            kv = (kv_latent @ Wkvb).reshape(b, t, H, NOPE).transpose(0, 2, 1, 3)
            k_rope = jnp.broadcast_to(k_rope[:, None, :, :], (b, H, t, ROPE))
            q_nope, q_rope = (q[..., :NOPE], q[..., NOPE:])
            q = jnp.concatenate([q_nope, _rope(q_rope)], axis=-1)
            k = jnp.concatenate([kv, _rope(k_rope)], axis=-1)
            v = jnp.concatenate([kv, jnp.zeros_like(k_rope)], axis=-1)
            att = jnp.einsum('bhqd,bhkd->bhqk', q, k) / jnp.sqrt(jnp.float32(D))
            mask = jnp.tril(jnp.ones((t, t), dtype=bool))
            att = jnp.where(mask, att, jnp.float32(-jnp.inf))
            att = jax.nn.softmax(att, axis=-1)
            y = jnp.einsum('bhqk,bhkd->bhqd', att, v)
            y = y.transpose(0, 2, 1, 3).reshape(b, t, H * D)
            return y @ Wo

        def _experts(x_flat, Wg, Wu, Wd):
            g = jax.nn.silu(jnp.einsum('nc,eci->nei', x_flat, Wg))
            u = jnp.einsum('nc,eci->nei', x_flat, Wu)
            return jnp.einsum('nei,eic->nec', g * u, Wd)

        def _moe(x, Wgate, expert_bias, Wg, Wu, Wd, sWg, sWu, sWd):
            b, t, c = x.shape
            xf = x.reshape(-1, c)
            shared = jnp.mean(_experts(xf, sWg, sWu, sWd), axis=1)
            logits = xf @ Wgate + expert_bias
            probs = jax.nn.softmax(logits, axis=-1)
            topk_p, topk_i = jax.lax.top_k(probs, K)
            topk_p = topk_p / jnp.sum(topk_p, axis=-1, keepdims=True)
            comb = jnp.sum(jax.nn.one_hot(topk_i, E, dtype=xf.dtype) * topk_p[..., None], axis=1)
            routed = jnp.einsum('ne,nec->nc', comb, _experts(xf, Wg, Wu, Wd))
            return (shared + routed).reshape(b, t, c)
        x = x + _attention(_rmsnorm(x, w_ln1), Wq, Wkva, Wkvb, Wo)
        residual = x
        xn = _rmsnorm(x, w_ln2)
        x_out = _moe(xn, Wgate, expert_bias, Wg, Wu, Wd, sWg, sWu, sWd)
        return residual + x_out

    def _L1_attn_ref(x, wq, wk, wv):
        import jax, jax.numpy as jnp
        import numpy as np
        DIM = 256
        SEQ = 1024
        BATCH = 4
        ROPE_BASE = 10000.0

        def rotate_half(x):
            x_even = x[..., 0::2]
            x_odd = x[..., 1::2]
            return jnp.stack((-x_odd, x_even), axis=-1).reshape(x.shape)

        def rope_tables(seq_len, dim, base=ROPE_BASE, dtype=jnp.float32):
            pos = jnp.arange(seq_len, dtype=jnp.float32)[:, None]
            inv_freq = 1.0 / base ** (jnp.arange(0, dim, 2, dtype=jnp.float32) / dim)
            freqs = pos * inv_freq
            cos = jnp.repeat(jnp.cos(freqs), 2, axis=-1).astype(dtype)
            sin = jnp.repeat(jnp.sin(freqs), 2, axis=-1).astype(dtype)
            return (cos, sin)
        q = jnp.einsum('bsd,ed->bse', x, wq)
        k = jnp.einsum('bsd,ed->bse', x, wk)
        v = jnp.einsum('bsd,ed->bse', x, wv)
        seq_len, dim = (q.shape[-2], q.shape[-1])
        cos, sin = rope_tables(seq_len, dim, dtype=q.dtype)
        q = q * cos + rotate_half(q) * sin
        k = k * cos + rotate_half(k) * sin
        scale = 1.0 / jnp.sqrt(jnp.asarray(dim, dtype=q.dtype))
        scores = jnp.einsum('bqd,bkd->bqk', q, k) * scale
        mask = jnp.triu(jnp.ones((seq_len, seq_len), dtype=bool), k=1)
        scores = jnp.where(mask, jnp.asarray(-jnp.inf, dtype=scores.dtype), scores)
        weights = jax.nn.softmax(scores, axis=-1)
        return jnp.einsum('bqk,bkd->bqd', weights, v)

    def _L1_ffn_ref(x, router_w, correction_bias, gate_w, up_w, down_w, shared_gate_w, shared_up_w, shared_down_w):
        import jax, jax.numpy as jnp
        import numpy as np
        E = 16
        G = 4
        EPG = E // G
        K = 4
        TOPK_GROUP = 2
        PER_GROUP_K = K // TOPK_GROUP

        def _route(xf, router_w, correction_bias):
            S = xf.shape[0]
            logits = xf @ router_w.T
            scores = jax.nn.sigmoid(logits)
            sb = scores + correction_bias
            grp_top = jax.lax.top_k(sb.reshape(S, G, EPG), PER_GROUP_K)[0]
            group_scores = grp_top.sum(axis=-1)
            _, group_idx = jax.lax.top_k(group_scores, TOPK_GROUP)
            group_mask = jnp.zeros((S, G), sb.dtype).at[jnp.arange(S)[:, None], group_idx].set(1.0)
            score_mask = jnp.broadcast_to(group_mask[:, :, None], (S, G, EPG)).reshape(S, E)
            masked = jnp.where(score_mask > 0, sb, -jnp.inf)
            _, topk_idx = jax.lax.top_k(masked, K)
            w = jnp.take_along_axis(scores, topk_idx, axis=1)
            w = w / (w.sum(axis=-1, keepdims=True) + 1e-20)
            return (topk_idx, w, scores)
        B, T, C = x.shape
        S = B * T
        xf = x.reshape(S, C)
        sg = xf @ shared_gate_w.T
        su = xf @ shared_up_w.T
        shared_out = jax.nn.silu(sg) * su @ shared_down_w.T
        topk_idx, w, _scores = _route(xf, router_w, correction_bias)
        combine = jnp.zeros((S, E), xf.dtype).at[jnp.arange(S)[:, None], topk_idx].add(w)
        g = jnp.einsum('sc,ech->esh', xf, gate_w)
        u = jnp.einsum('sc,ech->esh', xf, up_w)
        h = jax.nn.silu(g) * u
        hw = h * combine.T[:, :, None]
        routed = jnp.einsum('esh,ehc->sc', hw, down_w)
        return (shared_out + routed).reshape(B, T, C)
    x = L0_attn_x
    mod = (_silu(L0_c) @ L0_wmod).reshape(L0_c.shape[0], 6, 1, -1)
    sa, ca, ga, sb, cb, gb = (mod[:, 0], mod[:, 1], mod[:, 2], mod[:, 3], mod[:, 4], mod[:, 5])
    ga = (2 * (ga >= 0) - 1) * jnp.maximum(jnp.abs(ga), 0.25)
    gb = (2 * (gb >= 0) - 1) * jnp.maximum(jnp.abs(gb), 0.25)
    h = _layernorm(x, axis=-1) * (1 + ca) + sa
    x = x + ga * _L0_attn_ref(h, L0_attn_Wq, L0_attn_Wk, L0_attn_Wv, L0_attn_Wo, L0_attn_bo)
    h = _layernorm(x, axis=-1) * (1 + cb) + sb
    x = x + gb * _L0_ffn_ref(h, L0_ffn_w_ln1, L0_ffn_Wq, L0_ffn_Wkva, L0_ffn_Wkvb, L0_ffn_Wo, L0_ffn_w_ln2, L0_ffn_Wgate, L0_ffn_expert_bias, L0_ffn_Wg, L0_ffn_Wu, L0_ffn_Wd, L0_ffn_sWg, L0_ffn_sWu, L0_ffn_sWd)
    mod = (_silu(L1_c) @ L1_wmod).reshape(L1_c.shape[0], 6, 1, -1)
    sa, ca, ga, sb, cb, gb = (mod[:, 0], mod[:, 1], mod[:, 2], mod[:, 3], mod[:, 4], mod[:, 5])
    ga = (2 * (ga >= 0) - 1) * jnp.maximum(jnp.abs(ga), 0.25)
    gb = (2 * (gb >= 0) - 1) * jnp.maximum(jnp.abs(gb), 0.25)
    h = _layernorm(x, axis=-1) * (1 + ca) + sa
    x = x + ga * _L1_attn_ref(h, L1_attn_wq, L1_attn_wk, L1_attn_wv)
    h = _layernorm(x, axis=-1) * (1 + cb) + sb
    x = x + gb * _L1_ffn_ref(h, L1_ffn_router_w, L1_ffn_correction_bias, L1_ffn_gate_w, L1_ffn_up_w, L1_ffn_down_w, L1_ffn_shared_gate_w, L1_ffn_shared_up_w, L1_ffn_shared_down_w)
    return x

_drawn_inputs = setup_inputs


def setup_inputs(seed=0):
    import zlib

    import numpy as np

    out = dict(_drawn_inputs(seed))
    spreads = {'L0_ffn_w_ln1': (1.0, 0.6),
     'L0_ffn_w_ln2': (1.0, 0.6),
     'L0_ffn_expert_bias': (0.0, 0.8),
     'L1_ffn_correction_bias': (0.0, 0.8)}
    factors = {'L0_attn_bo': 8.0,
     'L0_ffn_Wq': 8.0,
     'L0_ffn_Wkva': 8.0,
     'L0_ffn_Wkvb': 8.0,
     'L0_ffn_Wo': 8.0,
     'L0_ffn_Wgate': 8.0,
     'L0_ffn_Wg': 8.0,
     'L0_ffn_Wu': 8.0,
     'L0_ffn_Wd': 8.0,
     'L0_ffn_sWg': 8.0,
     'L0_ffn_sWu': 8.0,
     'L0_ffn_sWd': 8.0,
     'L1_ffn_router_w': 8.0,
     'L1_ffn_gate_w': 8.0,
     'L1_ffn_up_w': 8.0,
     'L1_ffn_down_w': 8.0,
     'L1_ffn_shared_gate_w': 8.0,
     'L1_ffn_shared_up_w': 8.0,
     'L1_ffn_shared_down_w': 8.0,
     'L1_attn_wq': 8.0,
     'L1_attn_wk': 8.0,
     'L1_attn_wv': 6.776}
    for name, (base, spread) in spreads.items():
        noise = np.random.default_rng([zlib.crc32(name.encode()), seed]).standard_normal(out[name].shape)
        drawn = base * np.exp(spread * noise) if base else spread * noise
        out[name] = jnp.asarray(drawn.astype(out[name].dtype))
    for name, factor in factors.items():
        out[name] = (out[name] * factor).astype(out[name].dtype)
    return out
```

```python
from contextlib import ExitStack, contextmanager

import numpy as np

import concourse.bass as bass
from concourse import mybir

F32 = mybir.dt.float32
BF16 = mybir.dt.bfloat16
ALU = mybir.AluOpType
ACT = mybir.ActivationFunctionType
AX = mybir.AxisListType

P = 128
B, T, C = 4, 1024, 256
TT = T // P
KC = C // P
HALF = 512
NH = T // HALF
EPS = 1e-5
MASKED = -1e30
SA, CA, GA, SB, CB, GB = range(6)

A_HEADS, WINDOW = 16, 64
A_DH = C // A_HEADS
PAD = WINDOW // 2
NWIN = T // WINDOW
PAIRS = A_HEADS // 2

L_HEADS, L_D, LATENT, ROPE = 16, 64, 32, 32
NOPE = L_D - ROPE
L_PAIRS = L_HEADS // 2
YT_TILES = L_HEADS * NOPE // P

MOE0 = dict(experts=8, shared=1, routed=8)
MOE1 = dict(experts=16, shared=4, routed=8)


class Signal:

    def __init__(self, ctx, nc, name, per, credit=1):
        self.sem = ctx.enter_context(nc.semaphore(name))
        self.per, self.credit = per, credit

    def at(self, turn, n):
        return turn * self.per + (self.credit + n)

    def open(self, engine):
        if self.credit:
            engine.sem_inc(self.sem, self.credit)


def signals(ctx, nc, phase, table):
    return {name: Signal(ctx, nc, f"{phase}_{name}", *((v,) if isinstance(v, int) else v))
            for name, v in table.items()}


@contextmanager
def cleared_after(nc, used):
    yield
    with nc.Block() as block:
        @block.sync
        def _(sp):
            for sem in used:
                sp.sem_clear(sem)



LN_SIGNALS = dict(stats=2 * TT, std=1, rstd=1, xn=TT, turned=2 * KC, hT=2 * KC)


def ln_vector(v, turn, S, src, st, mv, std, rstd, xn, free, rms=False):
    for t in range(TT):
        v.bn_stats(st[:, t, :], src[:, t, :]).then_inc(S["stats"].sem, 1)
    v.wait_ge(S["stats"].sem, S["stats"].at(turn, TT))
    v.memset(std[:, 0:1], 0.0)
    for t in range(TT):
        v.bn_aggr(mv[:, t, :], st[:, t, :]).then_inc(S["stats"].sem, 1)
    if rms:
        v.wait_ge(S["stats"].sem, S["stats"].at(turn, 2 * TT))
        v.tensor_tensor(st[:, :, 0], mv[:, :, 0], mv[:, :, 0], ALU.mult).then_inc(S["sq"].sem, 1)
        v.wait_ge(S["sq"].sem, S["sq"].at(turn, 1))
        v.tensor_tensor(mv[:, :, 1], mv[:, :, 1], st[:, :, 0], ALU.add).then_inc(S["sq"].sem, 1)
    v.wait_ge(S["std"].sem, S["std"].at(turn, 1))
    v.reciprocal(rstd[:, :], std[:, :]).then_inc(S["rstd"].sem, 1)
    v.wait_ge(S["rstd"].sem, S["rstd"].at(turn, 1))
    v.wait_ge(free.sem, free.at(turn, 0))
    for t in range(TT):
        if rms:
            v.tensor_scalar(xn[:, t, :], src[:, t, :], rstd[:, t:t + 1], None, ALU.mult)\
                .then_inc(S["xn"].sem, 1)
        else:
            v.tensor_scalar(xn[:, t, :], src[:, t, :], mv[:, t, 0:1], rstd[:, t:t + 1],
                            ALU.subtract, ALU.mult).then_inc(S["xn"].sem, 1)


def ln_scalar_std(a, turn, S, mv, std, eps, rms=False):
    if rms:
        a.wait_ge(S["sq"].sem, S["sq"].at(turn, 2))
    else:
        a.wait_ge(S["stats"].sem, S["stats"].at(turn, 2 * TT))
    a.activation(std[:, :], mv[:, :, 1], ACT.Sqrt, bias=eps[:, 0:1]).then_inc(S["std"].sem, 1)


def ln_tensor(pe, turn, S, xn, ident, banks):
    for u in range(2 * KC):
        k, half = u // 2, u % 2
        if k == 0:
            pe.wait_ge(S["xn"].sem, S["xn"].at(turn, 4 * half + 4))
        for i in range(4):
            mm = pe.transpose(banks[u][:, i * P:(i + 1) * P],
                              xn[:, 4 * half + i, k * P:(k + 1) * P], ident[:, :])
        mm.then_inc(S["turned"].sem, 1)


def ln_scalar_out(a, turn, S, hT, off, banks, scale, shift):
    for u in range(2 * KC):
        k, half = u // 2, u % 2
        a.wait_ge(S["turned"].sem, S["turned"].at(turn, u + 1))
        out = hT[:, k, off + half * HALF:off + (half + 1) * HALF]
        if shift is None:
            a.activation(out, banks[u][:, :], ACT.Copy, scale=scale(k)).then_inc(S["hT"].sem, 1)
        else:
            a.activation(out, banks[u][:, :], ACT.Identity, scale=scale(k), bias=shift(k))\
                .then_inc(S["hT"].sem, 1)



def attention_signals(J):
    return dict(score=J, negmax=J, exp=J, turnedP=(J, 2), evac=J, evac2=(J // 2, 1),
                pv=(J, 2), recip=J, norm=(J, 2))


def keys(j):
    return (j % TT + 1) * P


def att_tensor(pe, turn, S, J, q_of, k_of, v_of, W, vcols, ident, identb, causal, S2, TR, O, Pt, PT):
    def score(j):
        n, qt = keys(j), j % TT
        if j >= 2:
            pe.wait_ge(S["exp"].sem, S["exp"].at(turn, j - 1))
        for n0 in range(0, n, HALF):
            n1 = min(n, n0 + HALF)
            diagonal = n1 == n
            if diagonal:
                pe.matmul(S2[j % 2][:, n - P:n], identb[:, :], causal[:, :], start=True, stop=False,
                          skip_group_check=True)
            for k in range(W):
                mm = pe.matmul(S2[j % 2][:, n0:n1], q_of(j, k, qt), k_of(j, k, n0, n1),
                               start=(k == 0 and not diagonal), stop=(k == W - 1),
                               skip_group_check=diagonal)
        mm.then_inc(S["score"].sem, 1)

    def turn_p(j):
        n = keys(j)
        pe.wait_ge(S["exp"].sem, S["exp"].at(turn, j + 1))
        for i in range(n // P):
            mm = pe.transpose(TR[i // 4][:, (i % 4) * P:(i % 4 + 1) * P],
                              Pt[:, j % 2, i * P:(i + 1) * P], ident[:, :])
        mm.then_inc(S["turnedP"].sem, 1)

    def pv(j):
        n = keys(j)
        pe.wait_ge(S["evac"].sem, S["evac"].at(turn, j + 1))
        if n > HALF:
            big = (j // TT) * (TT // 2) + (j % TT - TT // 2) + 1
            pe.wait_ge(S["evac2"].sem, S["evac2"].at(turn, big))
        pe.wait_ge(S["norm"].sem, S["norm"].at(turn, j - 1))
        for i in range(n // P):
            mm = pe.matmul(O[j % 2][:, 0:vcols], PT[:, j % 2, i, :], v_of(j, i),
                           start=(i == 0), stop=(i == n // P - 1))
        mm.then_inc(S["pv"].sem, 1)

    score(0)
    for j in range(J):
        if j + 1 < J:
            score(j + 1)
        if j >= 1:
            pv(j - 1)
        turn_p(j)
    pv(J - 1)


def att_scalar(a, turn, S, J, S2, TR, Pt, PT, negmax, sums):
    def exp(j):
        n = keys(j)
        a.wait_ge(S["negmax"].sem, S["negmax"].at(turn, j + 1))
        a.wait_ge(S["turnedP"].sem, S["turnedP"].at(turn, j - 1))
        a.activation(Pt[:, j % 2, 0:n], S2[j % 2][:, 0:n], ACT.Exp, bias=negmax[:, j:j + 1],
                     accum_out=sums[:, j:j + 1]).then_inc(S["exp"].sem, 1)

    def evac(j):
        n = min(keys(j), HALF)
        a.wait_ge(S["turnedP"].sem, S["turnedP"].at(turn, j + 1))
        a.wait_ge(S["pv"].sem, S["pv"].at(turn, j - 1))
        a.activation(PT[:, j % 2, 0:n // P, :], TR[0][:, 0:n].rearrange("p (i q) -> p i q", q=P),
                     ACT.Copy).then_inc(S["evac"].sem, 1)

    a.wait_ge(S["norm"].sem, S["norm"].at(turn, 0))
    exp(0)
    for j in range(J):
        if j + 1 < J:
            exp(j + 1)
        evac(j)


def att_vector(v, turn, S, J, S2, TR, PT, O, negmax, sums, rs, vcols, y_of):
    def rowmax(j):
        v.wait_ge(S["score"].sem, S["score"].at(turn, j + 1))
        v.tensor_reduce(negmax[:, j:j + 1], S2[j % 2][:, 0:keys(j)], AX.X, ALU.max, negate=True)\
            .then_inc(S["negmax"].sem, 1)

    def evac2(j):
        n = keys(j)
        if n > HALF:
            v.wait_ge(S["turnedP"].sem, S["turnedP"].at(turn, j + 1))
            v.wait_ge(S["pv"].sem, S["pv"].at(turn, j - 1))
            v.tensor_copy(PT[:, j % 2, 4:n // P, :],
                          TR[1][:, 0:n - HALF].rearrange("p (i q) -> p i q", q=P))\
                .then_inc(S["evac2"].sem, 1)

    def norm(j):
        v.wait_ge(S["exp"].sem, S["exp"].at(turn, j + 1))
        v.reciprocal(rs[:, j:j + 1], sums[:, j:j + 1]).then_inc(S["recip"].sem, 1)
        v.wait_ge(S["recip"].sem, S["recip"].at(turn, j + 1))
        v.wait_ge(S["pv"].sem, S["pv"].at(turn, j + 1))
        v.tensor_scalar(y_of(j), O[j % 2][:, 0:vcols], rs[:, j:j + 1], None, ALU.mult)\
            .then_inc(S["norm"].sem, 1)

    rowmax(0)
    for j in range(J):
        if j + 1 < J:
            rowmax(j + 1)
        evac2(j)
        if j >= 1:
            norm(j - 1)
    norm(J - 1)


def modulation(nc, cT, wmod, MODT, ROWS):
    rows = [(0, GA), (0, GB), (0, CB), (0, SB), (1, GA), (1, GB)]
    with ExitStack() as sems, ExitStack() as ctx:
        c_sb = ctx.enter_context(nc.sbuf_tensor("m_c", [P, 2, KC, B], F32))
        sc = ctx.enter_context(nc.sbuf_tensor("m_silu", [P, 2, KC, B], F32))
        wm = ctx.enter_context(nc.sbuf_tensor("m_w", [P, 2, KC, 6 * C], F32))
        scb = ctx.enter_context(nc.sbuf_tensor("m_silub", [P, 2, KC, B, P], F32))
        sign = ctx.enter_context(nc.sbuf_tensor("m_sign", [P, 4 * B * C], F32))
        mag = ctx.enter_context(nc.sbuf_tensor("m_mag", [P, 4 * B * C], F32))
        banks = [ctx.enter_context(nc.psum_tensor(f"m_ps{i}", [P, HALF], F32)) for i in range(4)]
        loaded = sems.enter_context(nc.semaphore("m_loaded"))
        silu = sems.enter_context(nc.semaphore("m_silu_ready"))
        spread = sems.enter_context(nc.semaphore("m_spread"))
        product = sems.enter_context(nc.semaphore("m_product"))
        copied = sems.enter_context(nc.semaphore("m_copied"))
        chain = sems.enter_context(nc.semaphore("m_chain"))
        used = (loaded, silu, spread, product, copied, chain)
        ctx.enter_context(cleared_after(nc, used))
        block = ctx.enter_context(nc.Block())
        njobs = 2 + len(rows) * 2

        @block.sync
        def _(sp):
            for l in range(2):
                sp.dma_start(c_sb[:, l], cT[l]).then_inc(loaded, 16)
                sp.dma_start(wm[:, l], wmod[l]).then_inc(loaded, 16)

        @block.scalar
        def _(a):
            a.wait_ge(loaded, 64)
            a.activation(sc[:, :, :, :], c_sb[:, :, :, :], ACT.Silu).then_inc(silu, 1)

        @block.tensor
        def _(pe):
            pe.wait_ge(silu, 1)
            for l in range(2):
                for j in range(12):
                    for k in range(KC):
                        mm = pe.matmul(banks[l][:, j * B:(j + 1) * B], wm[:, l, k, j * P:(j + 1) * P],
                                       sc[:, l, k, :], start=(k == 0), stop=(k == KC - 1))
                mm.then_inc(product, 1)
            pe.wait_ge(spread, 1)
            for n in range(len(rows) * 2):
                l, r = rows[n // 2]
                pe.wait_ge(copied, n + 1)
                for i in range(2):
                    b = 2 * (n % 2) + i
                    for k in range(KC):
                        mm = pe.matmul(banks[2 + n % 2][:, i * C:(i + 1) * C], scb[:, l, k, b, :],
                                       wm[:, l, k, r * C:(r + 1) * C], start=(k == 0), stop=(k == KC - 1))
                mm.then_inc(product, 1)

        @block.vector
        def _(v):
            v.wait_ge(silu, 1)
            v.tensor_copy(scb[:, :, :, :, :].rearrange("p l k b m -> p (l k b) m"),
                          sc[:, :, :, :].rearrange("p l k b -> p (l k b)")[:, :, None]
                          .broadcast_to([P, 2 * KC * B, P])).then_inc(spread, 1)
            for l in range(2):
                v.wait_ge(product, l + 1)
                v.tensor_copy(MODT[:, l, :, :], banks[l][:, 0:12 * B].rearrange("p (j b) -> p b j", b=B))\
                    .then_inc(copied, 1)
            for n in range(len(rows) * 2):
                r, half = n // 2, n % 2
                v.wait_ge(product, n + 3)
                v.tensor_copy(ROWS[:, r, 2 * half:2 * half + 2, :],
                              banks[2 + n % 2][:, :].rearrange("p (b c) -> p b c", b=2)).then_inc(copied, 1)
            v.wait_ge(copied, njobs)
            for n, j in enumerate((CA, CB)):
                v.tensor_scalar(MODT[:, :, :, 2 * j:2 * j + 2], MODT[:, :, :, 2 * j:2 * j + 2], 1.0,
                                None, ALU.add).then_inc(chain, 1)
            v.tensor_scalar(ROWS[:, 2], ROWS[:, 2], 1.0, None, ALU.add).then_inc(chain, 1)
            at = 3
            for lo in (0, 4):
                n = 2 * B * C
                g = ROWS[:, lo:lo + 2].rearrange("p r b c -> p (r b c)")
                if at > 3:
                    v.wait_ge(chain, at)
                v.tensor_scalar(sign[:, 0:n], g, 0.0, 2.0, ALU.is_ge, ALU.mult).then_inc(chain, 1)
                v.tensor_scalar(mag[:, 0:n], g, -1.0, None, ALU.mult).then_inc(chain, 1)
                v.wait_ge(chain, at + 2)
                v.tensor_tensor(mag[:, 0:n], mag[:, 0:n], g, ALU.max).then_inc(chain, 1)
                v.wait_ge(chain, at + 3)
                v.tensor_scalar(mag[:, 0:n], mag[:, 0:n], 0.25, None, ALU.max).then_inc(chain, 1)
                v.wait_ge(chain, at + 4)
                v.scalar_tensor_tensor(g, sign[:, 0:n], -1.0, mag[:, 0:n], ALU.add, ALU.mult)\
                    .then_inc(chain, 1)
                at += 5


def windowed_attention(nc, sems, X, MODT, ROWS, ident, identb, eps, W, K):
    with ExitStack() as ctx:
        def sb(name, shape, dt=F32):
            return ctx.enter_context(nc.sbuf_tensor("w_" + name, shape, dt))

        wq, wk, wv, wo = (sb(n, [P, KC, C]) for n in ("wq", "wk", "wv", "wo"))
        bo = sb("bo", [P, C])
        band = sb("band", [P, P])
        bandb = sb("bandb", [P, P], BF16)
        hmask = sb("hmask", [P, A_HEADS])
        own = sb("own", [P, 2])
        sel = sb("sel", [P, WINDOW])
        xb = sb("xb", [P, TT, C])
        mod = sb("mod", [P, 12])
        gate = sb("gate", [P, C])
        xn = sb("xn", [P, TT, C])
        st, mv = sb("st", [P, TT, 6]), sb("mv", [P, TT, 2])
        std, rstd = sb("std", [P, TT]), sb("rstd", [P, TT])
        hT = sb("hT", [P, KC, T + 2 * PAD])
        qT = sb("qT", [P, KC, T])
        kT = sb("kT", [P, KC, T + 2 * PAD])
        qm = sb("qm", [P, NWIN, A_HEADS, WINDOW])
        V = sb("V", [P, NWIN, PAIRS, 34])
        D = qT
        PTs = sb("PT", [P, 2, PAIRS * P])
        m = sb("m", [P, 2, PAIRS])
        r = sb("r", [P, 2, PAIRS])
        rm = sb("rm", [P, 2, PAIRS, 2])
        Yn = sb("Yn", [P, 2, PAIRS, 2, A_DH])
        yT = xn[:, :, :].rearrange("p t c -> p (t c)").rearrange("p (k t) -> p k t", k=KC)
        tmp = sb("tmp", [P, 2, C])
        banks = [ctx.enter_context(nc.psum_tensor(f"w_ps{i}", [P, HALF], F32)) for i in range(8)]
        S = signals(sems, nc, "w", dict(LN_SIGNALS) | dict(
            qk=8, qkout=8, qm=A_HEADS, vproj=8, vout=8, score=2 * NWIN, max=2 * NWIN,
            sub=2 * NWIN, exp=NWIN, turnedP=(2 * NWIN, 3), ptout=2 * NWIN, pv=(NWIN, 2),
            recip=2 * NWIN, yn=NWIN, ymm=(NWIN, 2), yout=NWIN, proj=TT, biased=TT,
            mul=TT, added=(TT, 2)))
        wload = sems.enter_context(nc.semaphore("w_wload"))
        consts = sems.enter_context(nc.semaphore("w_consts"))
        xload = sems.enter_context(nc.semaphore("w_xload"))
        xstore = sems.enter_context(nc.semaphore("w_xstore"))
        block = ctx.enter_context(nc.Block())

        @block.sync
        def _(sp):
            for dst, src in ((wq, W["a_wq"]), (wk, W["a_wk"]), (wv, W["a_wv"]), (wo, W["a_wo"])):
                sp.dma_start(dst[:, :, :], src).then_inc(wload, 16)
            sp.dma_start(bo[:, :], W["a_bo"].partition_broadcast(P)).then_inc(wload, 16)
            for dst, src in ((band, K["band"]), (hmask, K["hmask"]), (own, K["own"]), (sel, K["sel64"])):
                sp.dma_start(dst[:, :], src).then_inc(wload, 16)
            with sp.Fori(0, B) as b:
                sp.wait_ge(S["added"].sem, S["added"].at(b, 0))
                sp.wait_ge(xstore, b * 16 + 1)
                sp.dma_start(xb[:, :, :], X[:, bass.ds(b * TT, TT), :]).then_inc(xload, 16)
                sp.dma_start(mod[:, :], MODT[:, 0, bass.ds(b, 1), :]).then_inc(xload, 16)
                sp.dma_start(gate[:, :], ROWS[:, 0, bass.ds(b, 1), :]).then_inc(xload, 16)
                sp.wait_ge(S["added"].sem, S["added"].at(b, TT))
                sp.dma_start(X[:, bass.ds(b * TT, TT), :], xb[:, :, :]).then_inc(xstore, 16)
            sp.wait_ge(xstore, B * 16 + 1)

        @block.vector
        def _(v):
            for name in ("stats", "rstd", "xn", "qm", "max", "sub", "recip", "yn", "yout", "biased"):
                S[name].open(v)
            v.wait_ge(wload, 9 * 16)
            v.tensor_copy(bandb[:, :], band[:, :]).then_inc(consts, 1)
            for buf in (hT, kT):
                v.memset(buf[:, :, 0:PAD], 0.0).then_inc(consts, 1)
                v.memset(buf[:, :, PAD + T:], 0.0).then_inc(consts, 1)
            v.memset(V[:, :, :, 32:34], 1.0).then_inc(consts, 1)
            with v.Fori(0, B) as b:
                v.wait_ge(xload, b * 48 + 48)
                ln_vector(v, b, S, xb, st, mv, std, rstd, xn, S["turned"])
                for n in range(KC):
                    v.wait_ge(S["qkout"].sem, S["qkout"].at(b, 2 * n + 2))
                    for h in range(n * A_HEADS // KC, (n + 1) * A_HEADS // KC):
                        v.tensor_scalar(qm[:, :, h, :], qT[:, n, :].rearrange("p (w q) -> p w q", q=WINDOW),
                                        hmask[:, h:h + 1], None, ALU.mult)\
                            .then_inc(S["qm"].sem, 1)

                def softmax(w):
                    for g in range(2):
                        u = 2 * w + g
                        v.wait_ge(S["score"].sem, S["score"].at(b, u + 1))
                        s3 = banks[2 * (w % 2) + g][:, :].rearrange("p (n k) -> p n k", k=P)
                        mx = m[:, w % 2, 4 * g:4 * g + 4]
                        v.tensor_reduce(mx, s3, AX.X, ALU.max).then_inc(S["max"].sem, 1)
                        v.wait_ge(S["max"].sem, S["max"].at(b, u + 1))
                        v.wait_ge(S["turnedP"].sem, S["turnedP"].at(b, 2 * w - 2))
                        v.tensor_tensor(
                            D[:, w % 2, g * HALF:(g + 1) * HALF].rearrange("p (n k) -> p n k", k=P),
                            s3, mx[:, :, None].broadcast_to([P, 4, P]), ALU.subtract)\
                            .then_inc(S["sub"].sem, 1)

                def weigh(w):
                    o3 = banks[6][:, 0:PAIRS * 34].rearrange("p (n d) -> p n d", d=34)
                    v.wait_ge(S["pv"].sem, S["pv"].at(b, w + 1))
                    v.reciprocal(r[:, w % 2, :], o3[:, :, 32]).then_inc(S["recip"].sem, 1)
                    v.wait_ge(S["recip"].sem, S["recip"].at(b, 2 * w + 1))
                    v.tensor_tensor(rm[:, w % 2], r[:, w % 2, :, None].broadcast_to([P, PAIRS, 2]),
                                    own[:, None, :].broadcast_to([P, PAIRS, 2]), ALU.mult)\
                        .then_inc(S["recip"].sem, 1)
                    v.wait_ge(S["recip"].sem, S["recip"].at(b, 2 * w + 2))
                    v.wait_ge(S["ymm"].sem, S["ymm"].at(b, w - 1))
                    v.tensor_tensor(
                        Yn[:, w % 2], o3[:, :, 0:32].rearrange("p n (h d) -> p n h d", h=2),
                        rm[:, w % 2, :, :, None].broadcast_to([P, PAIRS, 2, A_DH]), ALU.mult)\
                        .then_inc(S["yn"].sem, 1)

                def y_out(w):
                    v.wait_ge(S["ymm"].sem, S["ymm"].at(b, w + 1))
                    v.tensor_copy(yT[:, :, w * WINDOW:(w + 1) * WINDOW],
                                  banks[7][:, 0:KC * WINDOW].rearrange("p (k q) -> p k q", k=KC))\
                        .then_inc(S["yout"].sem, 1)

                softmax(0)
                for w in range(NWIN):
                    if w + 1 < NWIN:
                        softmax(w + 1)
                    weigh(w)
                    y_out(w)
                for t in range(TT):
                    v.wait_ge(S["proj"].sem, S["proj"].at(b, t + 1))
                    v.wait_ge(S["added"].sem, S["added"].at(b, t - 1))
                    v.tensor_tensor(tmp[:, t % 2, :], banks[t % 2][:, 0:C], bo[:, :], ALU.add)\
                        .then_inc(S["biased"].sem, 1)

        @block.gpsimd
        def _(g):
            for name in ("mul", "added"):
                S[name].open(g)
            g.sem_inc(xstore, 1)
            with g.Fori(0, B) as b:
                for t in range(TT):
                    g.wait_ge(S["biased"].sem, S["biased"].at(b, t + 1))
                    g.tensor_tensor(tmp[:, t % 2, :], tmp[:, t % 2, :], gate[:, :], ALU.mult)\
                        .then_inc(S["mul"].sem, 1)
                    g.wait_ge(S["mul"].sem, S["mul"].at(b, t + 1))
                    g.tensor_tensor(xb[:, t, :], xb[:, t, :], tmp[:, t % 2, :], ALU.add)\
                        .then_inc(S["added"].sem, 1)

        @block.scalar
        def _(a):
            for name in ("std", "hT", "qkout", "vout", "exp", "ptout"):
                S[name].open(a)
            a.wait_ge(consts, 6)
            with a.Fori(0, B) as b:
                ln_scalar_std(a, b, S, mv, std, eps)
                ln_scalar_out(a, b, S, hT, PAD, banks, lambda k: mod[:, 2 * CA + k:2 * CA + k + 1],
                              lambda k: mod[:, 2 * SA + k:2 * SA + k + 1])
                for u in range(8):
                    et, half = (u % 4) // 2, u % 2
                    dst = qT[:, et, half * HALF:(half + 1) * HALF] if u < 4 else \
                        kT[:, et, PAD + half * HALF:PAD + (half + 1) * HALF]
                    a.wait_ge(S["qk"].sem, S["qk"].at(b, u + 1))
                    a.activation(dst, banks[u][:, :], ACT.Copy).then_inc(S["qkout"].sem, 1)
                for u in range(NWIN // 2):
                    a.wait_ge(S["vproj"].sem, S["vproj"].at(b, u + 1))
                    a.activation(V[:, 2 * u:2 * u + 2, :, 0:32],
                                 banks[u][:, :].rearrange("p (w n d) -> p w n d", w=2, d=32), ACT.Copy)\
                        .then_inc(S["vout"].sem, 1)

                def exp(w):
                    a.wait_ge(S["sub"].sem, S["sub"].at(b, 2 * w + 2))
                    a.activation(D[:, w % 2, :], D[:, w % 2, :], ACT.Exp, scale=A_DH ** -0.5)\
                        .then_inc(S["exp"].sem, 1)

                exp(0)
                for w in range(NWIN):
                    if w + 1 < NWIN:
                        exp(w + 1)
                    for g in range(2):
                        a.wait_ge(S["turnedP"].sem, S["turnedP"].at(b, 2 * w + g + 1))
                        if g == 0:
                            a.wait_ge(S["pv"].sem, S["pv"].at(b, w - 1))
                        a.activation(PTs[:, w % 2, g * HALF:(g + 1) * HALF], banks[4 + g][:, :], ACT.Copy)\
                            .then_inc(S["ptout"].sem, 1)

        @block.tensor
        def _(pe):
            for name in ("turned", "qk", "vproj", "score", "turnedP", "pv", "ymm", "proj"):
                S[name].open(pe)
            pe.wait_ge(consts, 6)
            with pe.Fori(0, B) as b:
                pe.wait_ge(S["biased"].sem, S["biased"].at(b, 0))
                ln_tensor(pe, b, S, xn, ident, banks)
                pe.wait_ge(S["hT"].sem, S["hT"].at(b, 2 * KC))
                for u in range(8):
                    w, et, half = (wq, wk)[u // 4], (u % 4) // 2, u % 2
                    for k in range(KC):
                        mm = pe.matmul(banks[u][:, :], w[:, k, et * P:(et + 1) * P],
                                       hT[:, k, PAD + half * HALF:PAD + (half + 1) * HALF],
                                       start=(k == 0), stop=(k == KC - 1))
                    mm.then_inc(S["qk"].sem, 1)
                for u in range(NWIN // 2):
                    pe.wait_ge(S["qkout"].sem, S["qkout"].at(b, u + 1))
                    for i in range(2):
                        w0 = (2 * u + i) * WINDOW
                        for k in range(KC):
                            mm = pe.matmul(banks[u][:, i * C:(i + 1) * C], hT[:, k, w0:w0 + P],
                                           wv[:, k, :], start=(k == 0), stop=(k == KC - 1))
                    mm.then_inc(S["vproj"].sem, 1)

                def score(w):
                    if w >= 2:
                        pe.wait_ge(S["sub"].sem, S["sub"].at(b, 2 * w - 2))
                    for g in range(2):
                        bank = banks[2 * (w % 2) + g]
                        pe.matmul(bank[:, :].rearrange("p (n k) -> p n k", k=P), identb[:, :],
                                  bandb[:, None, :].broadcast_to([P, 4, P]), start=True, stop=False,
                                  skip_group_check=True)
                        for i in range(4):
                            h = 2 * (4 * g + i)
                            mm = pe.matmul(bank[:, i * P:(i + 1) * P],
                                           qm[:, w, h:h + 2, :].rearrange("p h q -> p (h q)"),
                                           kT[:, g, w * WINDOW:w * WINDOW + P],
                                           start=False, stop=(i == 3), skip_group_check=True)
                        mm.then_inc(S["score"].sem, 1)

                def turn_p(w):
                    pe.wait_ge(S["exp"].sem, S["exp"].at(b, w + 1))
                    for g in range(2):
                        if w >= 1:
                            pe.wait_ge(S["ptout"].sem, S["ptout"].at(b, 2 * w - 1 + g))
                        for i in range(4):
                            n = 4 * g + i
                            mm = pe.transpose(banks[4 + g][:, i * P:(i + 1) * P],
                                              D[:, w % 2, n * P:(n + 1) * P], ident[:, :])
                        mm.then_inc(S["turnedP"].sem, 1)

                def pv(w):
                    pe.wait_ge(S["ptout"].sem, S["ptout"].at(b, 2 * w + 2))
                    if w >= 1:
                        pe.wait_ge(S["yn"].sem, S["yn"].at(b, w))
                    for n in range(PAIRS):
                        mm = pe.matmul(banks[6][:, n * 34:(n + 1) * 34], PTs[:, w % 2, n * P:(n + 1) * P],
                                       V[:, w, n, :], start=True, stop=True)
                    mm.then_inc(S["pv"].sem, 1)

                def y_mm(w):
                    pe.wait_ge(S["yn"].sem, S["yn"].at(b, w + 1))
                    if w >= 1:
                        pe.wait_ge(S["yout"].sem, S["yout"].at(b, w))
                    for k in range(KC):
                        mm = pe.matmul(banks[7][:, k * WINDOW:(k + 1) * WINDOW],
                                       Yn[:, w % 2, 4 * k:4 * k + 4].rearrange("p n h d -> p (n h d)"),
                                       sel[:, :], start=True, stop=True)
                    mm.then_inc(S["ymm"].sem, 1)

                pe.wait_ge(S["qm"].sem, S["qm"].at(b, A_HEADS))
                pe.wait_ge(S["qkout"].sem, S["qkout"].at(b, 8))
                pe.wait_ge(S["vout"].sem, S["vout"].at(b, 8))
                score(0)
                for w in range(NWIN):
                    if w + 1 < NWIN:
                        score(w + 1)
                    turn_p(w)
                    if w >= 1:
                        y_mm(w - 1)
                    pv(w)
                y_mm(NWIN - 1)
                pe.wait_ge(S["yout"].sem, S["yout"].at(b, NWIN))
                for t in range(TT):
                    if t >= 2:
                        pe.wait_ge(S["biased"].sem, S["biased"].at(b, t - 1))
                    for k in range(KC):
                        mm = pe.matmul(banks[t % 2][:, 0:C], yT[:, k, t * P:(t + 1) * P], wo[:, k, :],
                                       start=(k == 0), stop=(k == KC - 1))
                    mm.then_inc(S["proj"].sem, 1)


def latent_attention(nc, sems, X, U, ROWS, ident, identb, causal, eps, W, K):
    J = 2 * TT
    with ExitStack() as ctx:
        def sb(name, shape, dt=F32):
            return ctx.enter_context(nc.sbuf_tensor("l_" + name, shape, dt))

        wkva, wkvb, wo = sb("wkva", [P, KC, 64]), sb("wkvb", [LATENT, 512]), sb("wo", [P, YT_TILES, C])
        wq, wkp = sb("wq", [P, KC, P]), sb("wkp", [64, P])
        w_ln = sb("w_ln", [P, KC])
        qcos, qsin = sb("qcos", [P, T]), sb("qsin", [P, T])
        kcos, ksin = sb("kcos", [64, T]), sb("ksin", [64, T])
        xx, ub = sb("xx", [P, 2 * TT, C]), sb("ub", [P, TT, C])
        xb, xn = xx[:, 0:TT, :], xx[:, TT:, :]
        Y = xx[:, :, :].rearrange("p t c -> p (t c)").rearrange("p (t y) -> p t y", t=TT)
        cb, sbias = sb("cb", [P, C]), sb("sb", [P, C])
        st, mv = sb("st", [P, TT, 6]), sb("mv", [P, TT, 2])
        std, rstd = sb("std", [P, TT]), sb("rstd", [P, TT])
        rT = sb("rT", [P, KC, T])
        kvr = sb("kvr", [64, T])
        shuf = sb("shuf", [P, T])
        V = sb("V", [P, TT, 512])
        qT, kT = sb("qT", [P, T]), sb("kT", [P, T])
        Pt, PT = sb("Pt", [P, 2, T]), sb("PT", [P, 2, TT, P])
        negmax, sums, rs = sb("negmax", [P, J]), sb("sums", [P, J]), sb("rs", [P, J])
        YT = V[:, :, :].rearrange("p t c -> p (t c)").rearrange("p (k t) -> p k t", k=YT_TILES)
        S2 = [ctx.enter_context(nc.psum_tensor(f"l_s{i}", [P, 2 * HALF], F32)) for i in range(2)]
        TR = [ctx.enter_context(nc.psum_tensor(f"l_t{i}", [P, HALF], F32)) for i in range(2)]
        O = [ctx.enter_context(nc.psum_tensor(f"l_o{i}", [P, HALF], F32)) for i in range(2)]
        banks = [S2[0][:, 0:HALF], S2[0][:, HALF:], S2[1][:, 0:HALF], S2[1][:, HALF:],
                 TR[0][:, :], TR[1][:, :], O[0][:, :], O[1][:, :]]
        N1 = signals(sems, nc, "l_n1", dict(stats=2 * TT, std=1, rstd=1, xn=TT))
        S = signals(sems, nc, "l", dict(LN_SIGNALS) | dict(
            sq=2, scaled=TT, u=TT, ckv=1, shufk=1, ropek=3, vproj=TT, vout=TT,
            turnedY=8, ytout=8, proj=TT, added=TT))
        A = signals(sems, nc, "la", attention_signals(J) | dict(
            qproj=1, kproj=1, shufq=1, cosq=1, sinq=1, ropeq=1, kout=1))
        wload = sems.enter_context(nc.semaphore("l_wload"))
        pload = sems.enter_context(nc.semaphore("l_pload"))
        xload = sems.enter_context(nc.semaphore("l_xload"))
        ustore = sems.enter_context(nc.semaphore("l_ustore"))
        block = ctx.enter_context(nc.Block())

        @block.sync
        def _(sp):
            for dst, src in ((wkva, W["l_wkva"]), (wo, W["l_wo"])):
                sp.dma_start(dst[:, :, :], src).then_inc(wload, 16)
            for dst, src in ((wkvb, W["l_wkvb"]), (w_ln, W["l_ln1"]), (qcos, K["qcos"]),
                             (qsin, K["qsin"]), (kcos, K["kcos"]), (ksin, K["ksin"])):
                sp.dma_start(dst[:, :], src).then_inc(wload, 16)
            sp.dma_start(wq[:, :, :], W["l_wq"][0:1]).then_inc(pload, 16)
            sp.dma_start(wkp[:, :], W["l_wkp"][0:1]).then_inc(pload, 16)
            with sp.Fori(0, B) as b:
                sp.wait_ge(S["added"].sem, S["added"].at(b, 0))
                sp.wait_ge(ustore, b * 16 + 1)
                sp.dma_start(xb[:, :, :], X[:, bass.ds(b * TT, TT), :]).then_inc(xload, 16)
                sp.dma_start(cb[:, :], ROWS[:, 2, bass.ds(b, 1), :]).then_inc(xload, 16)
                sp.dma_start(sbias[:, :], ROWS[:, 3, bass.ds(b, 1), :]).then_inc(xload, 16)
            sp.wait_ge(ustore, B * 16 + 1)
            sp.wait_ge(pload, (B * L_PAIRS + 1) * 32)

        @block.vector
        def _(v):
            for sig in (N1["stats"], N1["rstd"], N1["xn"]):
                sig.open(v)
            for name in ("stats", "sq", "rstd", "xn", "shufk", "ropek", "added"):
                S[name].open(v)
            for name in ("negmax", "evac2", "recip", "norm", "shufq", "cosq"):
                A[name].open(v)
            v.wait_ge(wload, 8 * 16)
            swap = [i ^ 1 for i in range(32)]
            with v.Fori(0, B) as b:
                v.wait_ge(xload, b * 48 + 48)
                v.wait_ge(S["turned"].sem, S["turned"].at(b, 0))
                ln_vector(v, b, N1, xb, st, mv, std, rstd, xn, S["u"])
                v.wait_ge(S["u"].sem, S["u"].at(b, TT))
                ln_vector(v, b, S, ub, st, mv, std, rstd, xn, S["turned"], rms=True)
                v.wait_ge(S["ckv"].sem, S["ckv"].at(b, 1))
                v.wait_ge(A["ropeq"].sem, A["ropeq"].at(b * L_PAIRS, 0))
                v.tensor_tensor(kvr[:, :], S2[0][0:64, :], kcos[:, :], ALU.mult).then_inc(S["ropek"].sem, 1)
                v.stream_shuffle(shuf[0:64, :], S2[0][0:64, :], swap).then_inc(S["shufk"].sem, 1)
                v.wait_ge(S["shufk"].sem, S["shufk"].at(b, 1))
                v.tensor_tensor(shuf[0:64, :], shuf[0:64, :], ksin[:, :], ALU.mult)\
                    .then_inc(S["ropek"].sem, 1)
                v.wait_ge(S["ropek"].sem, S["ropek"].at(b, 2))
                v.tensor_tensor(kvr[:, :], kvr[:, :], shuf[0:64, :], ALU.add).then_inc(S["ropek"].sem, 1)
                with v.Fori(0, L_PAIRS) as hp:
                    turn = b * L_PAIRS + hp
                    v.wait_ge(S["ropek"].sem, S["ropek"].at(b, 3))
                    v.wait_ge(A["qproj"].sem, A["qproj"].at(turn, 1))
                    v.wait_ge(A["ropeq"].sem, A["ropeq"].at(turn, 0))
                    v.tensor_tensor(qT[:, :], S2[0][:, :], qcos[:, :], ALU.mult).then_inc(A["cosq"].sem, 1)
                    v.stream_shuffle(shuf[:, :], S2[0][:, :], swap).then_inc(A["shufq"].sem, 1)
                    att_vector(v, turn, A, J, S2, TR, PT, O, negmax, sums, rs, 32,
                               lambda j: Y[:, j % TT, bass.ds(hp * 64 + (j // TT) * 32, 32)])
                for t in range(TT):
                    v.wait_ge(S["proj"].sem, S["proj"].at(b, t + 1))
                    v.tensor_tensor(ub[:, t, :], ub[:, t, :], banks[t % 4][:, 0:C], ALU.add)\
                        .then_inc(S["added"].sem, 1)

        @block.gpsimd
        def _(g):
            for name in ("scaled", "u"):
                S[name].open(g)
            for name in ("sinq", "ropeq"):
                A[name].open(g)
            g.sem_inc(ustore, 1)
            with g.Fori(0, B) as b:
                g.wait_ge(ustore, b * 16 + 1)
                for t in range(TT):
                    g.wait_ge(N1["xn"].sem, N1["xn"].at(b, t + 1))
                    g.tensor_tensor(ub[:, t, :], xn[:, t, :], cb[:, :], ALU.mult)\
                        .then_inc(S["scaled"].sem, 1)
                    g.wait_ge(S["scaled"].sem, S["scaled"].at(b, t + 1))
                    g.tensor_tensor(ub[:, t, :], ub[:, t, :], sbias[:, :], ALU.add)\
                        .then_inc(S["u"].sem, 1)
                with g.Fori(0, L_PAIRS) as hp:
                    turn = b * L_PAIRS + hp
                    g.wait_ge(A["shufq"].sem, A["shufq"].at(turn, 1))
                    g.tensor_tensor(shuf[:, :], shuf[:, :], qsin[:, :], ALU.mult).then_inc(A["sinq"].sem, 1)
                    g.wait_ge(A["sinq"].sem, A["sinq"].at(turn, 1))
                    g.wait_ge(A["cosq"].sem, A["cosq"].at(turn, 1))
                    g.tensor_tensor(qT[:, :], qT[:, :], shuf[:, :], ALU.add).then_inc(A["ropeq"].sem, 1)

        @block.scalar
        def _(a):
            for sig in (N1["std"], S["std"], S["hT"], S["vout"], S["ytout"], A["exp"], A["evac"], A["kout"]):
                sig.open(a)
            with a.Fori(0, B) as b:
                ln_scalar_std(a, b, N1, mv, std, eps)
                ln_scalar_std(a, b, S, mv, std, eps, rms=True)
                ln_scalar_out(a, b, S, rT, 0, [banks[4], banks[5], banks[6], banks[7]],
                              lambda k: w_ln[:, k:k + 1], None)
                for t in range(TT):
                    a.wait_ge(S["vproj"].sem, S["vproj"].at(b, t + 1))
                    a.activation(V[:, t, :], banks[(t + 2) % 8], ACT.Copy).then_inc(S["vout"].sem, 1)
                with a.Fori(0, L_PAIRS) as hp:
                    turn = b * L_PAIRS + hp
                    a.wait_ge(A["kproj"].sem, A["kproj"].at(turn, 1))
                    a.activation(kT[:, :], S2[1][:, :], ACT.Copy).then_inc(A["kout"].sem, 1)
                    a.dma_start(wq[:, :, :], W["l_wq"][bass.ds(hp + 1, 1)]).then_inc(pload, 16)
                    a.dma_start(wkp[:, :], W["l_wkp"][bass.ds(hp + 1, 1)]).then_inc(pload, 16)
                    att_scalar(a, turn, A, J, S2, TR, Pt, PT, negmax, sums)
                for u in range(8):
                    a.wait_ge(S["turnedY"].sem, S["turnedY"].at(b, u + 1))
                    a.activation(YT[:, u // 2, (u % 2) * HALF:(u % 2 + 1) * HALF], banks[u], ACT.Copy)\
                        .then_inc(S["ytout"].sem, 1)
                a.wait_ge(S["added"].sem, S["added"].at(b, TT))
                a.dma_start(U[:, bass.ds(b * TT, TT), :], ub[:, :, :]).then_inc(ustore, 16)

        @block.tensor
        def _(pe):
            for name in ("turned", "ckv", "vproj", "turnedY", "proj"):
                S[name].open(pe)
            for name in ("qproj", "kproj", "score", "turnedP", "pv"):
                A[name].open(pe)
            pe.wait_ge(wload, 8 * 16)
            with pe.Fori(0, B) as b:
                pe.wait_ge(S["added"].sem, S["added"].at(b, 0))
                ln_tensor(pe, b, S, xn, ident, [banks[4], banks[5], banks[6], banks[7]])
                pe.wait_ge(S["hT"].sem, S["hT"].at(b, 2 * KC))
                for half in range(NH):
                    for k in range(KC):
                        mm = pe.matmul(S2[0][0:64, half * HALF:(half + 1) * HALF], wkva[:, k, :],
                                       rT[:, k, half * HALF:(half + 1) * HALF],
                                       start=(k == 0), stop=(k == KC - 1))
                mm.then_inc(S["ckv"].sem, 1)
                pe.wait_ge(S["ropek"].sem, S["ropek"].at(b, 3))
                for t in range(TT):
                    pe.matmul(banks[(t + 2) % 8], kvr[0:LATENT, t * P:(t + 1) * P], wkvb[:, :],
                              start=True, stop=True).then_inc(S["vproj"].sem, 1)
                with pe.Fori(0, L_PAIRS) as hp:
                    turn = b * L_PAIRS + hp
                    pe.wait_ge(S["vout"].sem, S["vout"].at(b, TT))
                    pe.wait_ge(A["exp"].sem, A["exp"].at(turn, 0))
                    pe.wait_ge(A["shufq"].sem, A["shufq"].at(turn, 0))
                    pe.wait_ge(pload, turn * 32 + 32)
                    for half in range(NH):
                        for k in range(KC):
                            mm = pe.matmul(S2[0][:, half * HALF:(half + 1) * HALF], wq[:, k, :],
                                           rT[:, k, half * HALF:(half + 1) * HALF],
                                           start=(k == 0), stop=(k == KC - 1))
                    mm.then_inc(A["qproj"].sem, 1)
                    for half in range(NH):
                        mm = pe.matmul(S2[1][:, half * HALF:(half + 1) * HALF], wkp[:, :],
                                       kvr[:, half * HALF:(half + 1) * HALF], start=True, stop=True)
                    mm.then_inc(A["kproj"].sem, 1)
                    pe.wait_ge(A["ropeq"].sem, A["ropeq"].at(turn, 1))
                    pe.wait_ge(A["kout"].sem, A["kout"].at(turn, 1))

                    def rows(j):
                        return slice(64 * (j // TT), 64 * (j // TT) + 64)

                    att_tensor(pe, turn, A, J,
                               lambda j, k, qt: qT[rows(j), qt * P:(qt + 1) * P],
                               lambda j, k, n0, n1: kT[rows(j), n0:n1],
                               lambda j, i: V[:, i, bass.ds(hp * 64 + (j // TT) * 32, 32)],
                               1, 32, ident, identb, causal, S2, TR, O, Pt, PT)
                pe.wait_ge(A["norm"].sem, A["norm"].at(b * L_PAIRS + (L_PAIRS - 1), J))
                for u in range(8):
                    for i in range(4):
                        t = 4 * (u % 2) + i
                        mm = pe.transpose(banks[u][:, i * P:(i + 1) * P],
                                          Y[:, t, (u // 2) * P:(u // 2 + 1) * P], ident[:, :])
                    mm.then_inc(S["turnedY"].sem, 1)
                pe.wait_ge(S["ytout"].sem, S["ytout"].at(b, 8))
                for t in range(TT):
                    if t >= 4:
                        pe.wait_ge(S["added"].sem, S["added"].at(b, t - 3))
                    for k in range(YT_TILES):
                        mm = pe.matmul(banks[t % 4][:, 0:C], YT[:, k, t * P:(t + 1) * P], wo[:, k, :],
                                       start=(k == 0), stop=(k == YT_TILES - 1))
                    mm.then_inc(S["proj"].sem, 1)


def rope_attention(nc, sems, X, MODT, ROWS, ident, identb, causal, eps, W, K):
    J = TT
    with ExitStack() as ctx:
        def sb(name, shape, dt=F32):
            return ctx.enter_context(nc.sbuf_tensor("r_" + name, shape, dt))

        wq, wk, wv = (sb(n, [P, KC, C]) for n in ("wq", "wk", "wv"))
        cos, sin = sb("cos", [P, KC, T]), sb("sin", [P, KC, T])
        xb = sb("xb", [P, TT, C])
        mod, gate = sb("mod", [P, 12]), sb("gate", [P, C])
        xn = sb("xn", [P, TT, C])
        st, mv = sb("st", [P, TT, 6]), sb("mv", [P, TT, 2])
        std, rstd = sb("std", [P, TT]), sb("rstd", [P, TT])
        hT = sb("hT", [P, KC, T])
        shuf = sb("shuf", [P, 2 * KC, T])
        qk = sb("qk", [P, 2 * KC, T])
        V = sb("V", [P, TT, C])
        Pt, PT = sb("Pt", [P, 2, T]), sb("PT", [P, 2, TT, P])
        negmax, sums, rs = sb("negmax", [P, J]), sb("sums", [P, J]), sb("rs", [P, J])
        tmp = sb("tmp", [P, TT, C])
        S2 = [ctx.enter_context(nc.psum_tensor(f"r_s{i}", [P, 2 * HALF], F32)) for i in range(2)]
        TR = [ctx.enter_context(nc.psum_tensor(f"r_t{i}", [P, HALF], F32)) for i in range(2)]
        O = [ctx.enter_context(nc.psum_tensor(f"r_o{i}", [P, HALF], F32)) for i in range(2)]
        banks = [TR[0][:, :], TR[1][:, :], O[0][:, :], O[1][:, :]]
        S = signals(sems, nc, "r", dict(LN_SIGNALS) | attention_signals(J) | dict(
            proj=4, shufd=4, cosd=4, sind=4, rope=4, vproj=4, vout=4, gated=TT, added=TT))
        wload = sems.enter_context(nc.semaphore("r_wload"))
        xload = sems.enter_context(nc.semaphore("r_xload"))
        xstore = sems.enter_context(nc.semaphore("r_xstore"))
        block = ctx.enter_context(nc.Block())

        @block.sync
        def _(sp):
            for dst, src in ((wq, W["r_wq"]), (wk, W["r_wk"]), (wv, W["r_wv"]), (cos, K["rcos"]),
                             (sin, K["rsin"])):
                sp.dma_start(dst[:, :, :], src).then_inc(wload, 16)
            with sp.Fori(0, B) as b:
                sp.wait_ge(S["added"].sem, S["added"].at(b, 0))
                sp.wait_ge(xstore, b * 16 + 1)
                sp.dma_start(xb[:, :, :], X[:, bass.ds(b * TT, TT), :]).then_inc(xload, 16)
                sp.dma_start(mod[:, :], MODT[:, 1, bass.ds(b, 1), :]).then_inc(xload, 16)
                sp.dma_start(gate[:, :], ROWS[:, 4, bass.ds(b, 1), :]).then_inc(xload, 16)
                sp.wait_ge(S["added"].sem, S["added"].at(b, TT))
                sp.dma_start(X[:, bass.ds(b * TT, TT), :], xb[:, :, :]).then_inc(xstore, 16)
            sp.wait_ge(xstore, B * 16 + 1)

        @block.vector
        def _(v):
            for name in ("stats", "rstd", "xn", "shufd", "cosd", "negmax", "evac2", "recip", "norm"):
                S[name].open(v)
            v.wait_ge(wload, 5 * 16)
            swap = [i ^ 1 for i in range(32)]
            with v.Fori(0, B) as b:
                v.wait_ge(xload, b * 48 + 48)
                ln_vector(v, b, S, xb, st, mv, std, rstd, xn, S["turned"])
                for u in range(4):
                    v.wait_ge(S["proj"].sem, S["proj"].at(b, u + 1))
                    v.tensor_tensor(qk[:, u, :], S2[u % 2][:, :], cos[:, u % KC, :], ALU.mult)\
                        .then_inc(S["cosd"].sem, 1)
                    v.stream_shuffle(shuf[:, u, :], S2[u % 2][:, :], swap).then_inc(S["shufd"].sem, 1)
                att_vector(v, b, S, J, S2, TR, PT, O, negmax, sums, rs, C, lambda j: tmp[:, j, :])

        @block.gpsimd
        def _(g):
            for name in ("sind", "rope", "gated", "added"):
                S[name].open(g)
            g.sem_inc(xstore, 1)
            with g.Fori(0, B) as b:
                for u in range(4):
                    g.wait_ge(S["shufd"].sem, S["shufd"].at(b, u + 1))
                    g.tensor_tensor(shuf[:, u, :], shuf[:, u, :], sin[:, u % KC, :], ALU.mult)\
                        .then_inc(S["sind"].sem, 1)
                    g.wait_ge(S["sind"].sem, S["sind"].at(b, u + 1))
                    g.wait_ge(S["cosd"].sem, S["cosd"].at(b, u + 1))
                    g.tensor_tensor(qk[:, u, :], qk[:, u, :], shuf[:, u, :], ALU.add)\
                        .then_inc(S["rope"].sem, 1)
                for t in range(TT):
                    g.wait_ge(S["norm"].sem, S["norm"].at(b, t + 1))
                    g.tensor_tensor(tmp[:, t, :], tmp[:, t, :], gate[:, :], ALU.mult)\
                        .then_inc(S["gated"].sem, 1)
                    g.wait_ge(S["gated"].sem, S["gated"].at(b, t + 1))
                    g.tensor_tensor(xb[:, t, :], xb[:, t, :], tmp[:, t, :], ALU.add)\
                        .then_inc(S["added"].sem, 1)

        @block.scalar
        def _(a):
            for name in ("std", "hT", "vout", "exp", "evac"):
                S[name].open(a)
            with a.Fori(0, B) as b:
                ln_scalar_std(a, b, S, mv, std, eps)
                ln_scalar_out(a, b, S, hT, 0, banks, lambda k: mod[:, 2 * CA + k:2 * CA + k + 1],
                              lambda k: mod[:, 2 * SA + k:2 * SA + k + 1])
                for u in range(4):
                    a.wait_ge(S["vproj"].sem, S["vproj"].at(b, u + 1))
                    a.activation(V[:, 2 * u:2 * u + 2, :],
                                 banks[u].rearrange("p (t c) -> p t c", t=2), ACT.Copy)\
                        .then_inc(S["vout"].sem, 1)
                att_scalar(a, b, S, J, S2, TR, Pt, PT, negmax, sums)

        @block.tensor
        def _(pe):
            for name in ("turned", "proj", "vproj", "score", "turnedP", "pv"):
                S[name].open(pe)
            pe.wait_ge(wload, 5 * 16)
            with pe.Fori(0, B) as b:
                pe.wait_ge(S["norm"].sem, S["norm"].at(b, 0))
                ln_tensor(pe, b, S, xn, ident, banks)
                pe.wait_ge(S["hT"].sem, S["hT"].at(b, 2 * KC))
                for u in range(4):
                    w, et = (wq, wk)[u // KC], u % KC
                    if u >= 2:
                        pe.wait_ge(S["shufd"].sem, S["shufd"].at(b, u - 1))
                    for half in range(NH):
                        for k in range(KC):
                            mm = pe.matmul(S2[u % 2][:, half * HALF:(half + 1) * HALF],
                                           w[:, k, et * P:(et + 1) * P],
                                           hT[:, k, half * HALF:(half + 1) * HALF],
                                           start=(k == 0), stop=(k == KC - 1))
                    mm.then_inc(S["proj"].sem, 1)
                for u in range(4):
                    for i in range(2):
                        t = 2 * u + i
                        for k in range(KC):
                            mm = pe.matmul(banks[u][:, i * C:(i + 1) * C], hT[:, k, t * P:(t + 1) * P],
                                           wv[:, k, :], start=(k == 0), stop=(k == KC - 1))
                    mm.then_inc(S["vproj"].sem, 1)
                pe.wait_ge(S["rope"].sem, S["rope"].at(b, 4))
                pe.wait_ge(S["vout"].sem, S["vout"].at(b, 4))
                att_tensor(pe, b, S, J,
                           lambda j, k, qt: qk[:, k, qt * P:(qt + 1) * P],
                           lambda j, k, n0, n1: qk[:, KC + k, n0:n1],
                           lambda j, i: V[:, i, :],
                           KC, C, ident, identb, causal, S2, TR, O, Pt, PT)


def experts(nc, sems, name, X, U, MODT, ROWS, ident, identb, eps, W, K, out):
    first = U is not None
    M = MOE0 if first else MOE1
    E, NS = M["experts"], M["shared"]
    NT = NS + M["routed"]
    G = 4
    with ExitStack() as ctx:
        def sb(nm, shape, dt=F32):
            return ctx.enter_context(nc.sbuf_tensor(f"{name}_{nm}", shape, dt))

        wg, wu = sb("wg", [P, NT, KC, P]), sb("wu", [P, NT, KC, P])
        wd = sb("wd", [P, NT, C])
        wr = sb("wr", [P, KC, E])
        rbias = sb("rbias", [P, E])
        lower = sb("lower", [P, E, E])
        selb = sb("selb", [P, M["routed"], P], BF16)
        w_ln = sb("w_ln", [P, KC])
        xb = sb("xb", [P, TT, C])
        ub = sb("ub", [P, TT, C]) if first else None
        mod, gate = sb("mod", [P, 12]), sb("gate", [P, C])
        xn = sb("xn", [P, TT, C])
        st, mv = sb("st", [P, TT, 6]), sb("mv", [P, TT, 2])
        std, rstd = sb("std", [P, TT]), sb("rstd", [P, TT])
        hT = sb("hT", [P, KC, T])
        score, key = sb("score", [P, TT, E]), sb("key", [P, TT, E])
        red = sb("red", [P, TT])
        r1, r2 = sb("r1", [P, TT * E * E]), sb("r2", [P, TT * E * E])
        rank, comb = sb("rank", [P, TT, E]), sb("comb", [P, TT, E])
        gA, gB, gC, gD = (sb(n, [P, TT * G]) for n in ("gA", "gB", "gC", "gD"))
        comb3 = sb("comb3", [P, TT, P], BF16)
        combT = sb("combT", [P, T], BF16)
        sg, hid = sb("sg", [P, 2, HALF]), sb("hid", [P, 2, HALF])
        tmp = sb("tmp", [P, 2, C])
        Gb = [ctx.enter_context(nc.psum_tensor(f"{name}_g{i}", [P, HALF], F32)) for i in range(2)]
        Ub = [ctx.enter_context(nc.psum_tensor(f"{name}_u{i}", [P, HALF], F32)) for i in range(2)]
        Cb = [ctx.enter_context(nc.psum_tensor(f"{name}_c{i}", [P, HALF], F32)) for i in range(2)]
        acc = [ctx.enter_context(nc.psum_tensor(f"{name}_a{i}", [P, HALF], F32)) for i in range(2)]
        CHAIN = 17 if first else 33
        NJ = NH * NT
        NR = NH * M["routed"]
        S = signals(sems, nc, name, dict(LN_SIGNALS) | dict(
            sq=2, logits=1, act=1, chain=(CHAIN, 0), comb=1, combP=1, combT=1, gate=NJ, up=NJ, cb=NR, silu=NJ,
            mul=NJ, hid=NR, down=(NJ, 2), y=TT, gated=TT, added=(TT, 2)))
        wload = sems.enter_context(nc.semaphore(name + "_wload"))
        xload = sems.enter_context(nc.semaphore(name + "_xload"))
        xstore = sems.enter_context(nc.semaphore(name + "_xstore"))
        consts = sems.enter_context(nc.semaphore(name + "_consts"))
        block = ctx.enter_context(nc.Block())
        loads = 48 + 16 * first

        def routed(n):
            return n // NT * M["routed"] + max(0, n % NT - NS)

        @block.sync
        def _(sp):
            sp.dma_start(wr[:, :, :], W[name + "_wr"]).then_inc(wload, 16)
            sp.dma_start(rbias[:, :], W[name + "_rb"].partition_broadcast(P)).then_inc(wload, 16)
            sp.dma_start(lower[:, :, :], K[name + "_lower"]).then_inc(wload, 16)
            sp.dma_start(w_ln[:, :], W["m0_ln"]).then_inc(wload, 16)
            sp.dma_start(r1[:, 0:M["routed"] * P].rearrange("p (j m) -> p j m", m=P) if not first else
                         wg[:, 0:4].rearrange("p a k m -> p (a k) m"), K[name + "_sel"]).then_inc(wload, 16)
            sp.wait_ge(consts, 2)
            for dst, src in ((wg, W[name + "_wg"]), (wu, W[name + "_wu"])):
                sp.dma_start(dst[:, :, :, :], src).then_inc(wload, 16)
            sp.dma_start(wd[:, :, :], W[name + "_wd"]).then_inc(wload, 16)
            with sp.Fori(0, B) as b:
                sp.wait_ge(S["added"].sem, S["added"].at(b, 0))
                sp.wait_ge(xstore, b * 16 + 1)
                sp.dma_start(xb[:, :, :], X[:, bass.ds(b * TT, TT), :]).then_inc(xload, 16)
                if first:
                    sp.dma_start(ub[:, :, :], U[:, bass.ds(b * TT, TT), :]).then_inc(xload, 16)
                sp.dma_start(mod[:, :], MODT[:, 1, bass.ds(b, 1), :]).then_inc(xload, 16)
                sp.dma_start(gate[:, :], ROWS[:, 1 if first else 5, bass.ds(b, 1), :]).then_inc(xload, 16)
                sp.wait_ge(S["added"].sem, S["added"].at(b, TT))
                if first:
                    sp.dma_start(X[:, bass.ds(b * TT, TT), :], xb[:, :, :]).then_inc(xstore, 16)
                else:
                    sp.dma_start(out[bass.ds(b, 1)].rearrange("b (t p) c -> p (b t) c", p=P), xb[:, :, :])\
                        .then_inc(xstore, 16)
            sp.wait_ge(xstore, B * 16 + 1)

        @block.vector
        def _(v):
            for nm in ("stats", "sq", "rstd", "xn", "comb", "combT", "mul", "hid", "y"):
                S[nm].open(v)
            v.wait_ge(wload, 5 * 16)
            v.tensor_copy(selb[:, :, :], (wg[:, 0:4].rearrange("p a k m -> p (a k) m") if first else
                          r1[:, 0:M["routed"] * P].rearrange("p (j m) -> p j m", m=P))).then_inc(consts, 1)
            v.memset(comb3[:, :, :], 0.0).then_inc(consts, 1)
            v.wait_ge(consts, 2)
            with v.Fori(0, B) as b:
                v.wait_ge(xload, b * loads + loads)
                ln_vector(v, b, S, ub if first else xb, st, mv, std, rstd, xn, S["turned"], rms=first)

                steps = [0]

                def link(ins):
                    steps[0] += 1
                    ins.then_inc(S["chain"].sem, 1)
                    v.wait_ge(S["chain"].sem, b * CHAIN + steps[0])

                def over(x):
                    return x[:, :, None].broadcast_to([P, TT, E])

                lg = Gb[0][:, 0:TT * E].rearrange("p (t e) -> p t e", e=E)
                bias = rbias[:, None, :].broadcast_to([P, TT, E])

                def ranks(x, n, e, low, dst):
                    size = n * e * e
                    a3 = r1[:, 0:size].rearrange("p (t i j) -> p t i j", i=e, j=e)
                    b3 = r2[:, 0:size].rearrange("p (t i j) -> p t i j", i=e, j=e)
                    other = x[:, :, None, :].broadcast_to([P, n, e, e])
                    mine = x[:, :, :, None].broadcast_to([P, n, e, e])
                    link(v.tensor_tensor(a3, other, mine, ALU.is_gt))
                    link(v.tensor_tensor(b3, other, mine, ALU.is_equal))
                    link(v.tensor_tensor(b3, b3, low[:, None, :, :].broadcast_to([P, n, e, e]), ALU.mult))
                    link(v.tensor_tensor(r1[:, 0:size], r1[:, 0:size], r2[:, 0:size], ALU.add))
                    link(v.tensor_reduce(dst, r1[:, 0:size].rearrange("p (t j) -> p t j", j=e), AX.X, ALU.add))

                v.wait_ge(S["logits"].sem, S["logits"].at(b, 1))
                if first:
                    link(v.tensor_tensor(key[:, :, :], lg, bias, ALU.add))
                    link(v.tensor_reduce(red[:, :], key[:, :, :], AX.X, ALU.max))
                    v.tensor_tensor(key[:, :, :], key[:, :, :], over(red), ALU.subtract)\
                        .then_inc(S["comb"].sem, 1)
                    v.wait_ge(S["act"].sem, S["act"].at(b, 1))
                    ranks(score[:, :, :], TT, E, lower[:, :, :], rank[:, :, :].rearrange("p t e -> p (t e)"))
                    keep = 2
                else:
                    v.wait_ge(S["act"].sem, S["act"].at(b, 1))
                    link(v.tensor_tensor(key[:, :, :], score[:, :, :], bias, ALU.add))
                    g4 = key[:, :, :].rearrange("p t (g i) -> p (t g) i", i=4)
                    link(v.tensor_tensor(gA[:, :], g4[:, :, 0], g4[:, :, 1], ALU.max))
                    link(v.tensor_tensor(gB[:, :], g4[:, :, 0], g4[:, :, 1], ALU.min))
                    link(v.tensor_tensor(gC[:, :], g4[:, :, 2], g4[:, :, 3], ALU.max))
                    link(v.tensor_tensor(gD[:, :], g4[:, :, 2], g4[:, :, 3], ALU.min))
                    link(v.tensor_tensor(gB[:, :], gB[:, :], gD[:, :], ALU.max))
                    link(v.tensor_tensor(gD[:, :], gA[:, :], gC[:, :], ALU.min))
                    link(v.tensor_tensor(gB[:, :], gB[:, :], gD[:, :], ALU.max))
                    link(v.tensor_tensor(gA[:, :], gA[:, :], gC[:, :], ALU.max))
                    link(v.tensor_tensor(gA[:, :], gA[:, :], gB[:, :], ALU.add))
                    ranks(gA[:, :].rearrange("p (t g) -> p t g", g=G), TT, G, lower[:, 0:G, 0:G], gC[:, :])
                    link(v.tensor_scalar(gC[:, :], gC[:, :], 2.0, MASKED, ALU.is_ge, ALU.mult))
                    link(v.tensor_tensor(g4, g4, gC[:, :, None].broadcast_to([P, TT * G, 4]), ALU.add))
                    ranks(key[:, :, :], TT, E, lower[:, :, :], rank[:, :, :].rearrange("p t e -> p (t e)"))
                    keep = 4
                link(v.tensor_scalar(rank[:, :, :], rank[:, :, :], float(keep), None, ALU.is_lt))
                link(v.tensor_tensor(comb[:, :, :], score[:, :, :], rank[:, :, :], ALU.mult))
                link(v.tensor_reduce(red[:, :], comb[:, :, :], AX.X, ALU.add))
                if not first:
                    link(v.tensor_scalar(red[:, :], red[:, :], 1e-20, None, ALU.add))
                link(v.reciprocal(red[:, :], red[:, :]))
                link(v.tensor_tensor(comb[:, :, :], comb[:, :, :], over(red), ALU.mult))
                v.wait_ge(S["combP"].sem, S["combP"].at(b, 0))
                for s in range(3):
                    link(v.tensor_copy(comb3[:, :, s * E:(s + 1) * E], comb[:, :, :]))
                    if s < 2:
                        link(v.tensor_tensor(comb[:, :, :], comb[:, :, :], comb3[:, :, s * E:(s + 1) * E],
                                             ALU.subtract))
                assert steps[0] == CHAIN

                def hidden(c, j):
                    n = c * NT + j
                    v.wait_ge(S["silu"].sem, S["silu"].at(b, n + 1))
                    v.wait_ge(S["up"].sem, S["up"].at(b, n + 1))
                    v.wait_ge(S["down"].sem, S["down"].at(b, n - 1))
                    v.tensor_tensor(hid[:, n % 2, :], Ub[n % 2][:, :], sg[:, n % 2, :], ALU.mult)\
                        .then_inc(S["mul"].sem, 1)
                    if j >= NS:
                        v.wait_ge(S["mul"].sem, S["mul"].at(b, n + 1))
                        v.wait_ge(S["cb"].sem, S["cb"].at(b, routed(n + 1)))
                        v.tensor_tensor(hid[:, n % 2, :], hid[:, n % 2, :], Cb[n % 2][:, :], ALU.mult)\
                            .then_inc(S["hid"].sem, 1)

                def split():
                    v.wait_ge(S["combP"].sem, S["combP"].at(b, 1))
                    v.tensor_copy(combT[:, :], Cb[1][:, :].bitcast(BF16)).then_inc(S["combT"].sem, 1)

                split()
                for c in range(NH):
                    for j in range(NT):
                        hidden(c, j)
                    for i in range(4):
                        t = 4 * c + i
                        v.wait_ge(S["down"].sem, S["down"].at(b, (c + 1) * NT))
                        v.wait_ge(S["added"].sem, S["added"].at(b, t - 1))
                        src = acc[i // 2][:, (i % 2) * C:(i % 2 + 1) * C]
                        v.tensor_tensor(tmp[:, t % 2, :], src, ub[:, t, :] if first else gate[:, :],
                                        ALU.add if first else ALU.mult).then_inc(S["y"].sem, 1)

        @block.gpsimd
        def _(g):
            for nm in ("gated", "added"):
                S[nm].open(g)
            g.sem_inc(xstore, 1)
            with g.Fori(0, B) as b:
                for t in range(TT):
                    g.wait_ge(S["y"].sem, S["y"].at(b, t + 1))
                    if first:
                        g.tensor_tensor(tmp[:, t % 2, :], tmp[:, t % 2, :], gate[:, :], ALU.mult)\
                            .then_inc(S["gated"].sem, 1)
                        g.wait_ge(S["gated"].sem, S["gated"].at(b, t + 1))
                    g.tensor_tensor(xb[:, t, :], xb[:, t, :], tmp[:, t % 2, :], ALU.add)\
                        .then_inc(S["added"].sem, 1)

        @block.scalar
        def _(a):
            for nm in ("std", "hT", "act", "silu"):
                S[nm].open(a)
            with a.Fori(0, B) as b:
                ln_scalar_std(a, b, S, mv, std, eps, rms=first)
                banks = [Ub[0][:, :], Ub[1][:, :], acc[0][:, :], acc[1][:, :]]
                if first:
                    ln_scalar_out(a, b, S, hT, 0, banks, lambda k: w_ln[:, k:k + 1], None)
                    a.wait_ge(S["comb"].sem, S["comb"].at(b, 1))
                    a.activation(score[:, :, :], key[:, :, :], ACT.Exp).then_inc(S["act"].sem, 1)
                else:
                    ln_scalar_out(a, b, S, hT, 0, banks, lambda k: mod[:, 2 * CB + k:2 * CB + k + 1],
                                  lambda k: mod[:, 2 * SB + k:2 * SB + k + 1])
                    a.wait_ge(S["logits"].sem, S["logits"].at(b, 1))
                    a.activation(score[:, :, :], Gb[0][:, 0:TT * E].rearrange("p (t e) -> p t e", e=E),
                                 ACT.Sigmoid).then_inc(S["act"].sem, 1)
                for n in range(NJ):
                    a.wait_ge(S["gate"].sem, S["gate"].at(b, n + 1))
                    if n >= 2:
                        a.wait_ge(S["mul"].sem, S["mul"].at(b, n - 1))
                    a.activation(sg[:, n % 2, :], Gb[n % 2][:, :], ACT.Silu).then_inc(S["silu"].sem, 1)

        @block.tensor
        def _(pe):
            for nm in ("turned", "logits", "combP", "gate", "up", "cb", "down"):
                S[nm].open(pe)
            pe.wait_ge(wload, 8 * 16)
            with pe.Fori(0, B) as b:
                pe.wait_ge(S["y"].sem, S["y"].at(b, 0))
                ln_tensor(pe, b, S, xn, ident, [Ub[0][:, :], Ub[1][:, :], acc[0][:, :], acc[1][:, :]])
                pe.wait_ge(S["hT"].sem, S["hT"].at(b, 2 * KC))
                for t in range(TT):
                    for k in range(KC):
                        mm = pe.matmul(Gb[0][:, t * E:(t + 1) * E], hT[:, k, t * P:(t + 1) * P],
                                       wr[:, k, :], start=(k == 0), stop=(k == KC - 1))
                mm.then_inc(S["logits"].sem, 1)
                pe.wait_ge(S["chain"].sem, b * CHAIN + CHAIN)
                for t in range(TT):
                    mm = pe.transpose(Cb[1][:, :].bitcast(BF16)[:, t * P:(t + 1) * P], comb3[:, t, :],
                                      identb[:, :])
                mm.then_inc(S["combP"].sem, 1)
                pe.wait_ge(S["combT"].sem, S["combT"].at(b, 1))

                def up(c, j):
                    n = c * NT + j
                    cols = slice(c * HALF, (c + 1) * HALF)
                    if n >= 2:
                        pe.wait_ge(S["silu"].sem, S["silu"].at(b, n - 1))
                    for k in range(KC):
                        mm = pe.matmul(Gb[n % 2][:, :], wg[:, j, k, :], hT[:, k, cols],
                                       start=(k == 0), stop=(k == KC - 1))
                    mm.then_inc(S["gate"].sem, 1)
                    if n >= 2:
                        pe.wait_ge(S["mul"].sem, S["mul"].at(b, n - 1))
                        if routed(n - 1):
                            pe.wait_ge(S["hid"].sem, S["hid"].at(b, routed(n - 1)))
                    for k in range(KC):
                        mm = pe.matmul(Ub[n % 2][:, :], wu[:, j, k, :], hT[:, k, cols],
                                       start=(k == 0), stop=(k == KC - 1))
                    mm.then_inc(S["up"].sem, 1)
                    if j >= NS:
                        pe.matmul(Cb[n % 2][:, :], selb[:, j - NS, :], combT[:, cols],
                                  start=True, stop=True).then_inc(S["cb"].sem, 1)

                def down(c, j):
                    n = c * NT + j
                    if j < NS:
                        pe.wait_ge(S["mul"].sem, S["mul"].at(b, n + 1))
                    else:
                        pe.wait_ge(S["hid"].sem, S["hid"].at(b, routed(n + 1)))
                    if c >= 1 and j == 0:
                        pe.wait_ge(S["y"].sem, S["y"].at(b, 4 * c))
                    for i in range(4):
                        mm = pe.matmul(acc[i // 2][:, (i % 2) * C:(i % 2 + 1) * C],
                                       hid[:, n % 2, i * P:(i + 1) * P], wd[:, j, :],
                                       start=(j == 0 and i % 2 == 0), stop=(j == NT - 1),
                                       skip_group_check=True)
                    mm.then_inc(S["down"].sem, 1)

                order = [(c, j) for c in range(NH) for j in range(NT)]
                up(*order[0])
                for n, cj in enumerate(order):
                    if n + 1 < len(order):
                        up(*order[n + 1])
                    down(*cj)


def build(nc, w, k, out, upto=5):
    with ExitStack() as ctx:
        def sb(name, shape, dt=F32):
            return ctx.enter_context(nc.sbuf_tensor(name, shape, dt))

        X = sb("X", [P, B * TT, C])
        MODT, ROWS = sb("MODT", [P, 2, B, 12]), sb("ROWS", [P, 6, B, C])
        ident, identb = sb("ident", [P, P]), sb("identb", [P, P], BF16)
        causal, eps = sb("causal", [P, P], BF16), sb("eps", [P, 1])
        mask = sb("mask", [P, P])
        loaded = ctx.enter_context(nc.semaphore("loaded"))
        ready = ctx.enter_context(nc.semaphore("ready"))
        with nc.Block() as block:
            @block.sync
            def _(sp):
                sp.dma_start(ident[:, :], k["ident"]).then_inc(loaded, 16)
                sp.dma_start(mask[:, :], k["causal"]).then_inc(loaded, 16)
                for b in range(B):
                    sp.dma_start(X[:, b * TT:(b + 1) * TT, :],
                                 w["x"][b].rearrange("(t p) c -> p t c", p=P)).then_inc(loaded, 16)
                sp.wait_ge(loaded, (2 + B) * 16)

            @block.vector
            def _(v):
                v.memset(eps[:, :], EPS).then_inc(ready, 1)
                v.wait_ge(loaded, (2 + B) * 16)
                v.tensor_copy(identb[:, :], ident[:, :]).then_inc(ready, 1)
                v.tensor_copy(causal[:, :], mask[:, :]).then_inc(ready, 1)

        modulation(nc, w["cT"], w["wmod"], MODT, ROWS)
        if upto >= 1:
            windowed_attention(nc, ctx, X, MODT, ROWS, ident, identb, eps, w, k)
        U = sb("U", [P, B * TT, C])
        if upto >= 2:
            latent_attention(nc, ctx, X, U, ROWS, ident, identb, causal, eps, w, k)
        if upto >= 3:
            experts(nc, ctx, "m0", X, U, MODT, ROWS, ident, identb, eps, w, k, None)
        if upto >= 4:
            rope_attention(nc, ctx, X, MODT, ROWS, ident, identb, causal, eps, w, k)
        if upto >= 5:
            experts(nc, ctx, "m1", X, None, MODT, ROWS, ident, identb, eps, w, k, out)
        else:
            st = ctx.enter_context(nc.semaphore("dbg"))
            with nc.Block() as block:
                @block.sync
                def _(sp):
                    for b in range(B):
                        sp.dma_start(out[b].rearrange("(t p) c -> p t c", p=P),
                                     (U if upto == 2 else X)[:, b * TT:(b + 1) * TT, :]).then_inc(st, 16)
                    sp.wait_ge(st, 16 * B)


def tables():
    f = np.float32
    i = np.arange(P)
    k = {"ident": np.eye(P, dtype=f)}
    k["causal"] = np.where(i[None, :] <= i[:, None], 0, MASKED).astype(f)
    q = i % WINDOW
    off = i[None, :] - q[:, None]
    k["band"] = np.where((off >= 0) & (off < WINDOW), 0, MASKED).astype(f)
    heads = np.arange(A_HEADS)
    k["hmask"] = (i[:, None] // A_DH == heads[None, :] % (P // A_DH)).astype(f)
    k["own"] = (i[:, None] // WINDOW == np.arange(2)[None, :]).astype(f)
    k["sel64"] = (q[:, None] == np.arange(WINDOW)[None, :]).astype(f)
    t = np.arange(T, dtype=f)

    def angles(theta, d):
        freqs = (1.0 / f(theta) ** (np.arange(0, d, 2, dtype=f) / f(d))).astype(f)
        a = np.repeat(freqs, 2)[:, None] * t[None, :]
        sign = np.where(np.arange(d) % 2 == 0, -1, 1)[:, None]
        return np.cos(a.astype(np.float64)), np.sin(a.astype(np.float64)) * sign

    c, s = angles(100000.0, ROPE)
    kc = np.concatenate([np.ones((NOPE, T)), c])
    ks = np.concatenate([np.zeros((NOPE, T)), s])
    k["kcos"], k["ksin"] = kc.astype(f), ks.astype(f)
    scale = L_D ** -0.5
    k["qcos"], k["qsin"] = (np.tile(kc, (2, 1)) * scale).astype(f), (np.tile(ks, (2, 1)) * scale).astype(f)
    c, s = angles(10000.0, C)
    scale = C ** -0.25
    km = lambda a: np.ascontiguousarray((a * scale).astype(f).reshape(KC, P, T).transpose(1, 0, 2))
    k["rcos"], k["rsin"] = km(c), km(s)
    for name, M in (("m0", MOE0), ("m1", MOE1)):
        E, R = M["experts"], M["routed"]
        e = np.arange(E)
        k[name + "_lower"] = np.broadcast_to((e[None, :] < e[:, None]).astype(f), (P, E, E)).copy()
        sel = np.zeros((P, R, P), f)
        for part in range(3):
            for j in range(R):
                for m in range(P):
                    sel[part * E + (j if E == R else 2 * j + m // 64), j, m] = 1
        k[name + "_sel"] = sel
    return k


def layouts(a):
    def km(w):
        return w.reshape(-1, P, w.shape[-1]).transpose(1, 0, 2)

    w = {"x": a["L0_attn_x"]}
    w["cT"] = np.stack([km(a[f"L{l}_c"].T) for l in range(2)])
    w["wmod"] = np.stack([km(a[f"L{l}_wmod"]) for l in range(2)])
    for n in "qkvo":
        w["a_w" + n] = km(a["L0_attn_W" + n].T)
    w["a_bo"] = a["L0_attn_bo"]
    w["l_wkva"] = km(a["L0_ffn_Wkva"])
    w["l_wkvb"] = a["L0_ffn_Wkvb"]
    w["l_wq"] = a["L0_ffn_Wq"].reshape(KC, P, L_PAIRS, P).transpose(2, 1, 0, 3)
    w["l_wq"] = np.concatenate([w["l_wq"], w["l_wq"][0:1]])
    wkp = np.zeros((L_PAIRS, 64, 2, 64), np.float32)
    wkp[:, 0:32, :, 0:32] = a["L0_ffn_Wkvb"].reshape(32, L_PAIRS, 2, 32).transpose(1, 0, 2, 3)
    wkp[:, 32:64, :, 32:64] = np.eye(32, dtype=np.float32)[:, None, :]
    wkp = wkp.reshape(L_PAIRS, 64, P)
    w["l_wkp"] = np.concatenate([wkp, wkp[0:1]])
    w["l_wo"] = km(a["L0_ffn_Wo"].reshape(L_HEADS, L_D, C)[:, :NOPE].reshape(-1, C))
    w["l_ln1"] = a["L0_ffn_w_ln1"].reshape(KC, P).T
    w["m0_ln"] = a["L0_ffn_w_ln2"].reshape(KC, P).T

    def up(shared, each):
        return np.concatenate([shared, each]).reshape(-1, KC, P, P).transpose(2, 0, 1, 3)

    w["m0_wg"] = up(a["L0_ffn_sWg"], a["L0_ffn_Wg"])
    w["m0_wu"] = up(a["L0_ffn_sWu"], a["L0_ffn_Wu"])
    w["m0_wd"] = np.concatenate([a["L0_ffn_sWd"], a["L0_ffn_Wd"]]).transpose(1, 0, 2)
    w["m0_wr"] = km(a["L0_ffn_Wgate"])
    w["m0_rb"] = a["L0_ffn_expert_bias"]
    for n in "qkv":
        w["r_w" + n] = km(a["L1_attn_w" + n].T)
    two = lambda x: x.reshape(8, 2, C, 64).transpose(0, 2, 1, 3).reshape(8, C, P)
    tiles = lambda x: x.T.reshape(C, 4, P).transpose(1, 0, 2)
    w["m1_wg"] = up(tiles(a["L1_ffn_shared_gate_w"]), two(a["L1_ffn_gate_w"]))
    w["m1_wu"] = up(tiles(a["L1_ffn_shared_up_w"]), two(a["L1_ffn_up_w"]))
    w["m1_wd"] = np.concatenate([a["L1_ffn_shared_down_w"].T.reshape(4, P, C),
                                 a["L1_ffn_down_w"].reshape(8, P, C)]).transpose(1, 0, 2)
    w["m1_wr"] = km(a["L1_ffn_router_w"].T)
    w["m1_rb"] = a["L1_ffn_correction_bias"]
    return {n: np.ascontiguousarray(x) for n, x in w.items()}


def kernel(**inputs):
    import concourse.bacc as bacc
    from concourse.bass_utils import run_bass_kernel_spmd

    nc = bacc.Bacc("TRN2", target_bir_lowering=False, num_devices=1)
    arrays = {n: np.asarray(a) for n, a in inputs.items()}
    w, k = layouts(arrays), tables()
    feed = {}

    def declare(group):
        aps = {}
        for n, a in group.items():
            feed["in_" + n] = a
            aps[n] = nc.dram_tensor("in_" + n, a.shape, F32, kind="ExternalInput").ap()
        return aps

    out = nc.dram_tensor("out", (B, T, C), F32, kind="ExternalOutput").ap()
    build(nc, declare(w), declare(k), out)
    r = run_bass_kernel_spmd(nc, [feed], core_ids=[0])
    return r.results[0]["out"]
```

```python
from contextlib import ExitStack, contextmanager

import numpy as np

import concourse.bass as bass
from concourse import mybir

F32 = mybir.dt.float32
BF16 = mybir.dt.bfloat16
F32R = mybir.dt.float32r
ALU = mybir.AluOpType
ACT = mybir.ActivationFunctionType
AX = mybir.AxisListType

P = 128
B, T, C = 4, 1024, 256
TT = T // P
KC = C // P
HALF = 512
NH = T // HALF
EPS = 1e-5
MASKED = -1e30
SA, CA, GA, SB, CB, GB = range(6)

A_HEADS, WINDOW = 16, 64
A_DH = C // A_HEADS
PAD = WINDOW // 2
NWIN = T // WINDOW
PAIRS = A_HEADS // 2

L_HEADS, L_D, LATENT, ROPE = 16, 64, 32, 32
NOPE = L_D - ROPE
L_PAIRS = L_HEADS // 2

MOE0 = dict(experts=8, shared=1, routed=8)
MOE1 = dict(experts=16, shared=4, routed=8)


class Signal:

    def __init__(self, ctx, nc, name, per, credit=1):
        self.sem = ctx.enter_context(nc.semaphore(name))
        self.per, self.credit = per, credit

    def at(self, turn, n):
        return turn * self.per + (self.credit + n)

    def open(self, engine):
        if self.credit:
            engine.sem_inc(self.sem, self.credit)


def signals(ctx, nc, phase, table):
    return {name: Signal(ctx, nc, f"{phase}_{name}", *((v,) if isinstance(v, int) else v))
            for name, v in table.items()}


@contextmanager
def cleared_after(nc, used):
    yield
    with nc.Block() as block:
        @block.sync
        def _(sp):
            for sem in used:
                sp.sem_clear(sem)



LN_SIGNALS = dict(stats=2 * TT, std=1, rstd=1, xn=TT, turned=2 * KC, hT=2 * KC)


def ln_vector(v, turn, S, src, st, mv, std, rstd, xn, free, rms=False):
    for t in range(TT):
        v.bn_stats(st[:, t, :], src[:, t, :]).then_inc(S["stats"].sem, 1)
    v.wait_ge(S["stats"].sem, S["stats"].at(turn, TT))
    v.memset(std[:, 0:1], 0.0)
    for t in range(TT):
        v.bn_aggr(mv[:, t, :], st[:, t, :]).then_inc(S["stats"].sem, 1)
    if rms:
        v.wait_ge(S["stats"].sem, S["stats"].at(turn, 2 * TT))
        v.tensor_tensor(st[:, :, 0], mv[:, :, 0], mv[:, :, 0], ALU.mult).then_inc(S["sq"].sem, 1)
        v.wait_ge(S["sq"].sem, S["sq"].at(turn, 1))
        v.tensor_tensor(mv[:, :, 1], mv[:, :, 1], st[:, :, 0], ALU.add).then_inc(S["sq"].sem, 1)
    v.wait_ge(S["std"].sem, S["std"].at(turn, 1))
    v.reciprocal(rstd[:, :], std[:, :]).then_inc(S["rstd"].sem, 1)
    v.wait_ge(S["rstd"].sem, S["rstd"].at(turn, 1))
    v.wait_ge(free.sem, free.at(turn, 0))
    for t in range(TT):
        if rms:
            v.tensor_scalar(xn[:, t, :], src[:, t, :], rstd[:, t:t + 1], None, ALU.mult)\
                .then_inc(S["xn"].sem, 1)
        else:
            v.tensor_scalar(xn[:, t, :], src[:, t, :], mv[:, t, 0:1], rstd[:, t:t + 1],
                            ALU.subtract, ALU.mult).then_inc(S["xn"].sem, 1)


def ln_scalar_std(a, turn, S, mv, std, eps, rms=False):
    if rms:
        a.wait_ge(S["sq"].sem, S["sq"].at(turn, 2))
    else:
        a.wait_ge(S["stats"].sem, S["stats"].at(turn, 2 * TT))
    a.activation(std[:, :], mv[:, :, 1], ACT.Sqrt, bias=eps[:, 0:1]).then_inc(S["std"].sem, 1)


def ln_tensor(pe, turn, S, xn, ident, banks):
    for u in range(2 * KC):
        k, half = u // 2, u % 2
        if k == 0:
            pe.wait_ge(S["xn"].sem, S["xn"].at(turn, 4 * half + 4))
        for i in range(4):
            mm = pe.transpose(banks[u][:, i * P:(i + 1) * P],
                              xn[:, 4 * half + i, k * P:(k + 1) * P], ident[:, :])
        mm.then_inc(S["turned"].sem, 1)


def ln_scalar_out(a, turn, S, hT, off, banks, scale, shift):
    for u in range(2 * KC):
        k, half = u // 2, u % 2
        a.wait_ge(S["turned"].sem, S["turned"].at(turn, u + 1))
        out = hT[:, k, off + half * HALF:off + (half + 1) * HALF]
        if shift is None:
            a.activation(out, banks[u][:, :], ACT.Copy, scale=scale(k)).then_inc(S["hT"].sem, 1)
        else:
            a.activation(out, banks[u][:, :], ACT.Identity, scale=scale(k), bias=shift(k))\
                .then_inc(S["hT"].sem, 1)



def attention_signals(J):
    return dict(score=J, negmax=J, exp=J, turnedP=(J, 2), evac=J, evac2=(J // 2, 1),
                pv=(J, 2), recip=J, norm=(J, 2))


def keys(j):
    return (j % TT + 1) * P


def att_tensor(pe, turn, S, J, q_of, k_of, v_of, W, vcols, ident, identb, causal, S2, TR, O, Pt, PT):
    def score(j):
        n, qt = keys(j), j % TT
        if j >= 2:
            pe.wait_ge(S["exp"].sem, S["exp"].at(turn, j - 1))
        for n0 in range(0, n, HALF):
            n1 = min(n, n0 + HALF)
            diagonal = n1 == n
            if diagonal:
                pe.matmul(S2[j % 2][:, n - P:n], identb[:, :], causal[:, :], start=True, stop=False,
                          skip_group_check=True)
            for k in range(W):
                mm = pe.matmul(S2[j % 2][:, n0:n1], q_of(j, k, qt), k_of(j, k, n0, n1),
                               start=(k == 0 and not diagonal), stop=(k == W - 1),
                               skip_group_check=diagonal)
        mm.then_inc(S["score"].sem, 1)

    def turn_p(j):
        n = keys(j)
        pe.wait_ge(S["exp"].sem, S["exp"].at(turn, j + 1))
        for i in range(n // P):
            mm = pe.transpose(TR[i // 4][:, (i % 4) * P:(i % 4 + 1) * P],
                              Pt[:, j % 2, i * P:(i + 1) * P], ident[:, :])
        mm.then_inc(S["turnedP"].sem, 1)

    def pv(j):
        n = keys(j)
        pe.wait_ge(S["evac"].sem, S["evac"].at(turn, j + 1))
        if n > HALF:
            big = (j // TT) * (TT // 2) + (j % TT - TT // 2) + 1
            pe.wait_ge(S["evac2"].sem, S["evac2"].at(turn, big))
        pe.wait_ge(S["norm"].sem, S["norm"].at(turn, j - 1))
        for i in range(n // P):
            mm = pe.matmul(O[j % 2][:, 0:vcols], PT[:, j % 2, i, :], v_of(j, i),
                           start=(i == 0), stop=(i == n // P - 1))
        mm.then_inc(S["pv"].sem, 1)

    score(0)
    for j in range(J):
        if j + 1 < J:
            score(j + 1)
        if j >= 1:
            pv(j - 1)
        turn_p(j)
    pv(J - 1)


def att_scalar(a, turn, S, J, S2, TR, Pt, PT, negmax, sums):
    def exp(j):
        n = keys(j)
        a.wait_ge(S["negmax"].sem, S["negmax"].at(turn, j + 1))
        a.wait_ge(S["turnedP"].sem, S["turnedP"].at(turn, j - 1))
        a.activation(Pt[:, j % 2, 0:n], S2[j % 2][:, 0:n], ACT.Exp, bias=negmax[:, j:j + 1],
                     accum_out=sums[:, j:j + 1]).then_inc(S["exp"].sem, 1)

    def evac(j):
        n = min(keys(j), HALF)
        a.wait_ge(S["turnedP"].sem, S["turnedP"].at(turn, j + 1))
        a.wait_ge(S["pv"].sem, S["pv"].at(turn, j - 1))
        a.activation(PT[:, j % 2, 0:n // P, :], TR[0][:, 0:n].rearrange("p (i q) -> p i q", q=P),
                     ACT.Copy).then_inc(S["evac"].sem, 1)

    a.wait_ge(S["norm"].sem, S["norm"].at(turn, 0))
    exp(0)
    for j in range(J):
        if j + 1 < J:
            exp(j + 1)
        evac(j)


def att_vector(v, turn, S, J, S2, TR, PT, O, negmax, sums, rs, vcols, y_of):
    def rowmax(j):
        v.wait_ge(S["score"].sem, S["score"].at(turn, j + 1))
        v.tensor_reduce(negmax[:, j:j + 1], S2[j % 2][:, 0:keys(j)], AX.X, ALU.max, negate=True)\
            .then_inc(S["negmax"].sem, 1)

    def evac2(j):
        n = keys(j)
        if n > HALF:
            v.wait_ge(S["turnedP"].sem, S["turnedP"].at(turn, j + 1))
            v.wait_ge(S["pv"].sem, S["pv"].at(turn, j - 1))
            v.tensor_copy(PT[:, j % 2, 4:n // P, :],
                          TR[1][:, 0:n - HALF].rearrange("p (i q) -> p i q", q=P))\
                .then_inc(S["evac2"].sem, 1)

    def norm(j):
        v.wait_ge(S["exp"].sem, S["exp"].at(turn, j + 1))
        v.reciprocal(rs[:, j:j + 1], sums[:, j:j + 1]).then_inc(S["recip"].sem, 1)
        v.wait_ge(S["recip"].sem, S["recip"].at(turn, j + 1))
        v.wait_ge(S["pv"].sem, S["pv"].at(turn, j + 1))
        v.tensor_scalar(y_of(j), O[j % 2][:, 0:vcols], rs[:, j:j + 1], None, ALU.mult)\
            .then_inc(S["norm"].sem, 1)

    rowmax(0)
    for j in range(J):
        if j + 1 < J:
            rowmax(j + 1)
        evac2(j)
        if j >= 1:
            norm(j - 1)
    norm(J - 1)


def modulation(nc, cT, wmod, MODT, ROWSd):
    rows = [(0, GA), (0, GB), (0, CB), (0, SB), (1, GA), (1, GB)]
    with ExitStack() as sems, ExitStack() as ctx:
        c_sb = ctx.enter_context(nc.sbuf_tensor("m_c", [P, 2, KC, B], F32))
        sc = ctx.enter_context(nc.sbuf_tensor("m_silu", [P, 2, KC, B], F32))
        wm = ctx.enter_context(nc.sbuf_tensor("m_w", [P, 2, KC, 6 * C], F32))
        scb = ctx.enter_context(nc.sbuf_tensor("m_silub", [P, 2, KC, B, P], F32))
        ROWS = ctx.enter_context(nc.sbuf_tensor("m_rows", [P, len(rows), B, C], F32))
        sign = ctx.enter_context(nc.sbuf_tensor("m_sign", [P, 4 * B * C], F32))
        mag = ctx.enter_context(nc.sbuf_tensor("m_mag", [P, 4 * B * C], F32))
        banks = [ctx.enter_context(nc.psum_tensor(f"m_ps{i}", [P, HALF], F32)) for i in range(4)]
        loaded = sems.enter_context(nc.semaphore("m_loaded"))
        silu = sems.enter_context(nc.semaphore("m_silu_ready"))
        spread = sems.enter_context(nc.semaphore("m_spread"))
        product = sems.enter_context(nc.semaphore("m_product"))
        copied = sems.enter_context(nc.semaphore("m_copied"))
        chain = sems.enter_context(nc.semaphore("m_chain"))
        stored = sems.enter_context(nc.semaphore("m_stored"))
        used = (loaded, silu, spread, product, copied, chain, stored)
        ctx.enter_context(cleared_after(nc, used))
        block = ctx.enter_context(nc.Block())
        njobs = 2 + len(rows) * 2

        @block.sync
        def _(sp):
            for l in range(2):
                sp.dma_start(c_sb[:, l], cT[l]).then_inc(loaded, 16)
                sp.dma_start(wm[:, l], wmod[l]).then_inc(loaded, 16)
            sp.wait_ge(chain, 13)
            sp.dma_start(ROWSd, ROWS[:, :, :, :]).then_inc(stored, 16)
            sp.wait_ge(stored, 16)

        @block.scalar
        def _(a):
            a.wait_ge(loaded, 64)
            a.activation(sc[:, :, :, :], c_sb[:, :, :, :], ACT.Silu).then_inc(silu, 1)

        @block.tensor
        def _(pe):
            pe.wait_ge(silu, 1)
            for l in range(2):
                for j in range(12):
                    for k in range(KC):
                        mm = pe.matmul(banks[l][:, j * B:(j + 1) * B], wm[:, l, k, j * P:(j + 1) * P],
                                       sc[:, l, k, :], start=(k == 0), stop=(k == KC - 1))
                mm.then_inc(product, 1)
            pe.wait_ge(spread, 1)
            for n in range(len(rows) * 2):
                l, r = rows[n // 2]
                pe.wait_ge(copied, n + 1)
                for i in range(2):
                    b = 2 * (n % 2) + i
                    for k in range(KC):
                        mm = pe.matmul(banks[2 + n % 2][:, i * C:(i + 1) * C], scb[:, l, k, b, :],
                                       wm[:, l, k, r * C:(r + 1) * C], start=(k == 0), stop=(k == KC - 1))
                mm.then_inc(product, 1)

        @block.vector
        def _(v):
            v.wait_ge(silu, 1)
            v.tensor_copy(scb[:, :, :, :, :].rearrange("p l k b m -> p (l k b) m"),
                          sc[:, :, :, :].rearrange("p l k b -> p (l k b)")[:, :, None]
                          .broadcast_to([P, 2 * KC * B, P])).then_inc(spread, 1)
            for l in range(2):
                v.wait_ge(product, l + 1)
                v.tensor_copy(MODT[:, l, :, :], banks[l][:, 0:12 * B].rearrange("p (j b) -> p b j", b=B))\
                    .then_inc(copied, 1)
            for n in range(len(rows) * 2):
                r, half = n // 2, n % 2
                v.wait_ge(product, n + 3)
                v.tensor_copy(ROWS[:, r, 2 * half:2 * half + 2, :],
                              banks[2 + n % 2][:, :].rearrange("p (b c) -> p b c", b=2)).then_inc(copied, 1)
            v.wait_ge(copied, njobs)
            for n, j in enumerate((CA, CB)):
                v.tensor_scalar(MODT[:, :, :, 2 * j:2 * j + 2], MODT[:, :, :, 2 * j:2 * j + 2], 1.0,
                                None, ALU.add).then_inc(chain, 1)
            v.tensor_scalar(ROWS[:, 2], ROWS[:, 2], 1.0, None, ALU.add).then_inc(chain, 1)
            at = 3
            for lo in (0, 4):
                n = 2 * B * C
                g = ROWS[:, lo:lo + 2].rearrange("p r b c -> p (r b c)")
                if at > 3:
                    v.wait_ge(chain, at)
                v.tensor_scalar(sign[:, 0:n], g, 0.0, 2.0, ALU.is_ge, ALU.mult).then_inc(chain, 1)
                v.tensor_scalar(mag[:, 0:n], g, -1.0, None, ALU.mult).then_inc(chain, 1)
                v.wait_ge(chain, at + 2)
                v.tensor_tensor(mag[:, 0:n], mag[:, 0:n], g, ALU.max).then_inc(chain, 1)
                v.wait_ge(chain, at + 3)
                v.tensor_scalar(mag[:, 0:n], mag[:, 0:n], 0.25, None, ALU.max).then_inc(chain, 1)
                v.wait_ge(chain, at + 4)
                v.scalar_tensor_tensor(g, sign[:, 0:n], -1.0, mag[:, 0:n], ALU.add, ALU.mult)\
                    .then_inc(chain, 1)
                at += 5


def windowed_attention(nc, sems, X, MODT, ROWS, ident, identb, eps, W, K):
    with ExitStack() as ctx:
        def sb(name, shape, dt=F32):
            return ctx.enter_context(nc.sbuf_tensor("w_" + name, shape, dt))

        wq, wk, wv, wo = (sb(n, [P, KC, C]) for n in ("wq", "wk", "wv", "wo"))
        bo = sb("bo", [P, C])
        band = sb("band", [P, P])
        bandb = sb("bandb", [P, P], BF16)
        hmask = sb("hmask", [P, A_HEADS])
        own = sb("own", [P, 2])
        sel = sb("sel", [P, WINDOW])
        xb = sb("xb", [P, TT, C])
        mod = sb("mod", [P, 12])
        gate = sb("gate", [P, C])
        xn = sb("xn", [P, TT, C])
        st, mv = sb("st", [P, TT, 6]), sb("mv", [P, TT, 2])
        std, rstd = sb("std", [P, TT]), sb("rstd", [P, TT])
        hT = sb("hT", [P, KC, T + 2 * PAD])
        qT = sb("qT", [P, KC, T])
        kT = sb("kT", [P, KC, T + 2 * PAD])
        qm = sb("qm", [P, NWIN, A_HEADS, WINDOW])
        V = sb("V", [P, NWIN, PAIRS, 34])
        D = qT
        PTs = sb("PT", [P, 2, PAIRS * P])
        m = sb("m", [P, 2, PAIRS])
        r = sb("r", [P, 2, PAIRS])
        rm = sb("rm", [P, 2, PAIRS, 2])
        Yn = sb("Yn", [P, 2, PAIRS, 2, A_DH])
        yT = xn[:, :, :].rearrange("p t c -> p (t c)").rearrange("p (k t) -> p k t", k=KC)
        tmp = sb("tmp", [P, 2, C])
        banks = [ctx.enter_context(nc.psum_tensor(f"w_ps{i}", [P, HALF], F32)) for i in range(8)]
        S = signals(sems, nc, "w", dict(LN_SIGNALS) | dict(
            qk=8, qkout=8, qm=A_HEADS, vproj=8, vout=8, score=2 * NWIN, max=2 * NWIN,
            sub=2 * NWIN, exp=NWIN, turnedP=(2 * NWIN, 3), ptout=2 * NWIN, pv=(NWIN, 2),
            recip=2 * NWIN, yn=NWIN, ymm=(NWIN, 2), yout=NWIN, proj=TT, biased=TT,
            mul=TT, added=(TT, 2)))
        wload = sems.enter_context(nc.semaphore("w_wload"))
        consts = sems.enter_context(nc.semaphore("w_consts"))
        xload = sems.enter_context(nc.semaphore("w_xload"))
        xstore = sems.enter_context(nc.semaphore("w_xstore"))
        block = ctx.enter_context(nc.Block())

        @block.sync
        def _(sp):
            for dst, src in ((wq, W["a_wq"]), (wk, W["a_wk"]), (wv, W["a_wv"]), (wo, W["a_wo"])):
                sp.dma_start(dst[:, :, :], src).then_inc(wload, 16)
            sp.dma_start(bo[:, :], W["a_bo"].partition_broadcast(P)).then_inc(wload, 16)
            for dst, src in ((band, K["band"]), (hmask, K["hmask"]), (own, K["own"]), (sel, K["sel64"])):
                sp.dma_start(dst[:, :], src).then_inc(wload, 16)
            with sp.Fori(0, B) as b:
                sp.wait_ge(S["added"].sem, S["added"].at(b, 0))
                sp.wait_ge(xstore, b * 16 + 1)
                sp.dma_start(xb[:, :, :], X[:, bass.ds(b * TT, TT), :]).then_inc(xload, 16)
                sp.dma_start(mod[:, :], MODT[:, 0, bass.ds(b, 1), :]).then_inc(xload, 16)
                sp.dma_start(gate[:, :], ROWS[:, 0, bass.ds(b, 1), :]).then_inc(xload, 16)
                sp.wait_ge(S["added"].sem, S["added"].at(b, TT))
                sp.dma_start(X[:, bass.ds(b * TT, TT), :], xb[:, :, :]).then_inc(xstore, 16)
            sp.wait_ge(xstore, B * 16 + 1)

        @block.vector
        def _(v):
            for name in ("stats", "rstd", "xn", "qm", "max", "sub", "recip", "yn", "yout", "biased"):
                S[name].open(v)
            v.wait_ge(wload, 9 * 16)
            v.tensor_copy(bandb[:, :], band[:, :]).then_inc(consts, 1)
            for buf in (hT, kT):
                v.memset(buf[:, :, 0:PAD], 0.0).then_inc(consts, 1)
                v.memset(buf[:, :, PAD + T:], 0.0).then_inc(consts, 1)
            v.memset(V[:, :, :, 32:34], 1.0).then_inc(consts, 1)
            with v.Fori(0, B) as b:
                v.wait_ge(xload, b * 48 + 48)
                ln_vector(v, b, S, xb, st, mv, std, rstd, xn, S["turned"])
                for n in range(KC):
                    v.wait_ge(S["qkout"].sem, S["qkout"].at(b, 2 * n + 2))
                    for h in range(n * A_HEADS // KC, (n + 1) * A_HEADS // KC):
                        v.tensor_scalar(qm[:, :, h, :], qT[:, n, :].rearrange("p (w q) -> p w q", q=WINDOW),
                                        hmask[:, h:h + 1], None, ALU.mult)\
                            .then_inc(S["qm"].sem, 1)

                def softmax(w):
                    for g in range(2):
                        u = 2 * w + g
                        v.wait_ge(S["score"].sem, S["score"].at(b, u + 1))
                        s3 = banks[2 * (w % 2) + g][:, :].rearrange("p (n k) -> p n k", k=P)
                        mx = m[:, w % 2, 4 * g:4 * g + 4]
                        v.tensor_reduce(mx, s3, AX.X, ALU.max).then_inc(S["max"].sem, 1)
                        v.wait_ge(S["max"].sem, S["max"].at(b, u + 1))
                        v.wait_ge(S["turnedP"].sem, S["turnedP"].at(b, 2 * w - 2))
                        v.tensor_tensor(
                            D[:, w % 2, g * HALF:(g + 1) * HALF].rearrange("p (n k) -> p n k", k=P),
                            s3, mx[:, :, None].broadcast_to([P, 4, P]), ALU.subtract)\
                            .then_inc(S["sub"].sem, 1)

                def weigh(w):
                    o3 = banks[6][:, 0:PAIRS * 34].rearrange("p (n d) -> p n d", d=34)
                    v.wait_ge(S["pv"].sem, S["pv"].at(b, w + 1))
                    v.reciprocal(r[:, w % 2, :], o3[:, :, 32]).then_inc(S["recip"].sem, 1)
                    v.wait_ge(S["recip"].sem, S["recip"].at(b, 2 * w + 1))
                    v.tensor_tensor(rm[:, w % 2], r[:, w % 2, :, None].broadcast_to([P, PAIRS, 2]),
                                    own[:, None, :].broadcast_to([P, PAIRS, 2]), ALU.mult)\
                        .then_inc(S["recip"].sem, 1)
                    v.wait_ge(S["recip"].sem, S["recip"].at(b, 2 * w + 2))
                    v.wait_ge(S["ymm"].sem, S["ymm"].at(b, w - 1))
                    v.tensor_tensor(
                        Yn[:, w % 2], o3[:, :, 0:32].rearrange("p n (h d) -> p n h d", h=2),
                        rm[:, w % 2, :, :, None].broadcast_to([P, PAIRS, 2, A_DH]), ALU.mult)\
                        .then_inc(S["yn"].sem, 1)

                def y_out(w):
                    v.wait_ge(S["ymm"].sem, S["ymm"].at(b, w + 1))
                    v.tensor_copy(yT[:, :, w * WINDOW:(w + 1) * WINDOW],
                                  banks[7][:, 0:KC * WINDOW].rearrange("p (k q) -> p k q", k=KC))\
                        .then_inc(S["yout"].sem, 1)

                softmax(0)
                for w in range(NWIN):
                    if w + 1 < NWIN:
                        softmax(w + 1)
                    weigh(w)
                    y_out(w)
                for t in range(TT):
                    v.wait_ge(S["proj"].sem, S["proj"].at(b, t + 1))
                    v.wait_ge(S["added"].sem, S["added"].at(b, t - 1))
                    v.tensor_tensor(tmp[:, t % 2, :], banks[t % 2][:, 0:C], bo[:, :], ALU.add)\
                        .then_inc(S["biased"].sem, 1)

        @block.gpsimd
        def _(g):
            for name in ("mul", "added"):
                S[name].open(g)
            g.sem_inc(xstore, 1)
            with g.Fori(0, B) as b:
                for t in range(TT):
                    g.wait_ge(S["biased"].sem, S["biased"].at(b, t + 1))
                    g.tensor_tensor(tmp[:, t % 2, :], tmp[:, t % 2, :], gate[:, :], ALU.mult)\
                        .then_inc(S["mul"].sem, 1)
                    g.wait_ge(S["mul"].sem, S["mul"].at(b, t + 1))
                    g.tensor_tensor(xb[:, t, :], xb[:, t, :], tmp[:, t % 2, :], ALU.add)\
                        .then_inc(S["added"].sem, 1)

        @block.scalar
        def _(a):
            for name in ("std", "hT", "qkout", "vout", "exp", "ptout"):
                S[name].open(a)
            a.wait_ge(consts, 6)
            with a.Fori(0, B) as b:
                ln_scalar_std(a, b, S, mv, std, eps)
                ln_scalar_out(a, b, S, hT, PAD, banks, lambda k: mod[:, 2 * CA + k:2 * CA + k + 1],
                              lambda k: mod[:, 2 * SA + k:2 * SA + k + 1])
                for u in range(8):
                    et, half = (u % 4) // 2, u % 2
                    dst = qT[:, et, half * HALF:(half + 1) * HALF] if u < 4 else \
                        kT[:, et, PAD + half * HALF:PAD + (half + 1) * HALF]
                    a.wait_ge(S["qk"].sem, S["qk"].at(b, u + 1))
                    a.activation(dst, banks[u][:, :], ACT.Copy).then_inc(S["qkout"].sem, 1)
                for u in range(NWIN // 2):
                    a.wait_ge(S["vproj"].sem, S["vproj"].at(b, u + 1))
                    a.activation(V[:, 2 * u:2 * u + 2, :, 0:32],
                                 banks[u][:, :].rearrange("p (w n d) -> p w n d", w=2, d=32), ACT.Copy)\
                        .then_inc(S["vout"].sem, 1)

                def exp(w):
                    a.wait_ge(S["sub"].sem, S["sub"].at(b, 2 * w + 2))
                    a.activation(D[:, w % 2, :], D[:, w % 2, :], ACT.Exp, scale=A_DH ** -0.5)\
                        .then_inc(S["exp"].sem, 1)

                exp(0)
                for w in range(NWIN):
                    if w + 1 < NWIN:
                        exp(w + 1)
                    for g in range(2):
                        a.wait_ge(S["turnedP"].sem, S["turnedP"].at(b, 2 * w + g + 1))
                        if g == 0:
                            a.wait_ge(S["pv"].sem, S["pv"].at(b, w - 1))
                        a.activation(PTs[:, w % 2, g * HALF:(g + 1) * HALF], banks[4 + g][:, :], ACT.Copy)\
                            .then_inc(S["ptout"].sem, 1)

        @block.tensor
        def _(pe):
            for name in ("turned", "qk", "vproj", "score", "turnedP", "pv", "ymm", "proj"):
                S[name].open(pe)
            pe.wait_ge(consts, 6)
            with pe.Fori(0, B) as b:
                pe.wait_ge(S["biased"].sem, S["biased"].at(b, 0))
                ln_tensor(pe, b, S, xn, ident, banks)
                pe.wait_ge(S["hT"].sem, S["hT"].at(b, 2 * KC))
                for u in range(8):
                    w, et, half = (wq, wk)[u // 4], (u % 4) // 2, u % 2
                    for k in range(KC):
                        mm = pe.matmul(banks[u][:, :], w[:, k, et * P:(et + 1) * P],
                                       hT[:, k, PAD + half * HALF:PAD + (half + 1) * HALF],
                                       start=(k == 0), stop=(k == KC - 1))
                    mm.then_inc(S["qk"].sem, 1)
                for u in range(NWIN // 2):
                    pe.wait_ge(S["qkout"].sem, S["qkout"].at(b, u + 1))
                    for i in range(2):
                        w0 = (2 * u + i) * WINDOW
                        for k in range(KC):
                            mm = pe.matmul(banks[u][:, i * C:(i + 1) * C], hT[:, k, w0:w0 + P],
                                           wv[:, k, :], start=(k == 0), stop=(k == KC - 1))
                    mm.then_inc(S["vproj"].sem, 1)

                def score(w):
                    if w >= 2:
                        pe.wait_ge(S["sub"].sem, S["sub"].at(b, 2 * w - 2))
                    for g in range(2):
                        bank = banks[2 * (w % 2) + g]
                        pe.matmul(bank[:, :].rearrange("p (n k) -> p n k", k=P), identb[:, :],
                                  bandb[:, None, :].broadcast_to([P, 4, P]), start=True, stop=False,
                                  skip_group_check=True)
                        for i in range(4):
                            h = 2 * (4 * g + i)
                            mm = pe.matmul(bank[:, i * P:(i + 1) * P],
                                           qm[:, w, h:h + 2, :].rearrange("p h q -> p (h q)"),
                                           kT[:, g, w * WINDOW:w * WINDOW + P],
                                           start=False, stop=(i == 3), skip_group_check=True)
                        mm.then_inc(S["score"].sem, 1)

                def turn_p(w):
                    pe.wait_ge(S["exp"].sem, S["exp"].at(b, w + 1))
                    for g in range(2):
                        if w >= 1:
                            pe.wait_ge(S["ptout"].sem, S["ptout"].at(b, 2 * w - 1 + g))
                        for i in range(4):
                            n = 4 * g + i
                            mm = pe.transpose(banks[4 + g][:, i * P:(i + 1) * P],
                                              D[:, w % 2, n * P:(n + 1) * P], ident[:, :])
                        mm.then_inc(S["turnedP"].sem, 1)

                def pv(w):
                    pe.wait_ge(S["ptout"].sem, S["ptout"].at(b, 2 * w + 2))
                    if w >= 1:
                        pe.wait_ge(S["yn"].sem, S["yn"].at(b, w))
                    for n in range(PAIRS):
                        mm = pe.matmul(banks[6][:, n * 34:(n + 1) * 34], PTs[:, w % 2, n * P:(n + 1) * P],
                                       V[:, w, n, :], start=True, stop=True)
                    mm.then_inc(S["pv"].sem, 1)

                def y_mm(w):
                    pe.wait_ge(S["yn"].sem, S["yn"].at(b, w + 1))
                    if w >= 1:
                        pe.wait_ge(S["yout"].sem, S["yout"].at(b, w))
                    for k in range(KC):
                        mm = pe.matmul(banks[7][:, k * WINDOW:(k + 1) * WINDOW],
                                       Yn[:, w % 2, 4 * k:4 * k + 4].rearrange("p n h d -> p (n h d)"),
                                       sel[:, :], start=True, stop=True)
                    mm.then_inc(S["ymm"].sem, 1)

                pe.wait_ge(S["qm"].sem, S["qm"].at(b, A_HEADS))
                pe.wait_ge(S["qkout"].sem, S["qkout"].at(b, 8))
                pe.wait_ge(S["vout"].sem, S["vout"].at(b, 8))
                score(0)
                for w in range(NWIN):
                    if w + 1 < NWIN:
                        score(w + 1)
                    turn_p(w)
                    if w >= 1:
                        y_mm(w - 1)
                    pv(w)
                y_mm(NWIN - 1)
                pe.wait_ge(S["yout"].sem, S["yout"].at(b, NWIN))
                for t in range(TT):
                    if t >= 2:
                        pe.wait_ge(S["biased"].sem, S["biased"].at(b, t - 1))
                    for k in range(KC):
                        mm = pe.matmul(banks[t % 2][:, 0:C], yT[:, k, t * P:(t + 1) * P], wo[:, k, :],
                                       start=(k == 0), stop=(k == KC - 1))
                    mm.then_inc(S["proj"].sem, 1)



class LatentJobs:
    J = 4 * TT
    SETS = L_PAIRS + 1
    K0, K1, Q0, Q1, VAL = range(5)
    PE_AT = {1: K0, 3: K1, 5: Q0, 8: Q1, 10: VAL}
    HI_AT = {1: K0, 3: K1, 7: Q0, 11: Q1, 12: VAL}
    QLO_AT = {7: 0, 12: 1}
    FREE_AT = {1: K0, 3: K1, 5: Q0, 8: Q1, 12: VAL}

    def __init__(self):
        self.units, self.before = [], []
        for j in range(self.J):
            self.before.append(len(self.units))
            n = self.qt(j) + 1
            self.units.append((j, 0, min(n, 4)))
            if n > 4:
                self.units.append((j, 4, n - 4))
        self.NU = len(self.units)

    def pair(self, j):
        return j // 16

    def head(self, j):
        return j // 2 % 2

    def qt(self, j):
        return 2 * (j % 16 // 4) + j % 2

    def n(self, j):
        return (self.qt(j) + 1) * P

    def of(self, j):
        end = self.before[j + 1] if j + 1 < self.J else self.NU
        return range(self.before[j], end)


def latent_attention(nc, sems, X, Ud, ROWSd, ident, identb, causal, eps, W, K):
    L = LatentJobs()
    J, NU, SETS = L.J, L.NU, L.SETS
    NQ = L_PAIRS // 2
    with ExitStack() as ctx:
        def sb(name, shape, dt=F32):
            return ctx.enter_context(nc.sbuf_tensor("l_" + name, shape, dt))

        wkva, wo = sb("wkva", [P, KC, 64]), sb("wo", [P, L_PAIRS, C])
        wq, wkp = sb("wq", [P, KC, P]), sb("wkp", [64, P])
        w_ln = sb("w_ln", [P, KC])
        cos, sin = sb("cos", [P, T]), sb("sin", [P, T])
        xn, ub = sb("xn", [P, TT, C]), sb("ub", [P, TT, C])
        cb, sbias = sb("cb", [P, C]), sb("sb", [P, C])
        st, mv = sb("st", [P, TT, 6]), sb("mv", [P, TT, 2])
        std, rstd = sb("std", [P, TT]), sb("rstd", [P, TT])
        rT = sb("rT", [P, KC, T])
        kvr = sb("kvr", [64, T])
        rot, shuf = sb("rot", [P, HALF]), sb("shuf", [P, HALF])
        qhi, qlo = sb("qhi", [P, 2, T], F32R), sb("qlo", [P, 2, T], F32R)
        khi, klo = sb("khi", [P, 2, T], F32R), sb("klo", [P, 2, T], F32R)
        val = sb("val", [P, 2, TT, 192], F32R)
        Pt = sb("Pt", [P, 2, T])
        PThi, PTlo = sb("PThi", [P, 2, TT, 2 * P], F32R), sb("PTlo", [P, 2, TT, 2 * P], F32R)
        negmax, sums = sb("negmax", [P, J]), sb("sums", [P, J])
        allsums, tile_of = sb("allsums", [P, P]), sb("tile_of", [P, TT])
        placed = Pt[:, 0, :].rearrange("p (t q) -> p t q", q=P)
        heads = sb("heads", [P, L_PAIRS, P])
        YT = sb("YT", [P, L_PAIRS, T])
        xb = YT[:, 6:8, :].rearrange("p n (t c) -> p (n t) c", c=C)
        S2 = [ctx.enter_context(nc.psum_tensor(f"l_s{i}", [P, 2 * HALF], F32)) for i in range(2)]
        TR = [ctx.enter_context(nc.psum_tensor(f"l_t{i}", [P, HALF], F32)) for i in range(2)]
        O = ctx.enter_context(nc.psum_tensor("l_o", [P, HALF], F32))
        PJ = ctx.enter_context(nc.psum_tensor("l_pj", [P, HALF], F32))
        pbanks = [S2[0][:, 0:HALF], S2[0][:, HALF:], S2[1][:, 0:HALF], S2[1][:, HALF:]]
        N1 = signals(sems, nc, "l_n1", dict(stats=2 * TT, std=1, rstd=1, xn=TT))
        S = signals(sems, nc, "l", dict(LN_SIGNALS) | dict(
            sq=2, scaled=TT, u=TT, ckv=1, shufk=1, ropek=3, proj=TT, added=TT,
            pj=5 * SETS, hi=5 * SETS, free=5 * SETS, cosq=2 * SETS, sinq=2 * SETS, ropeq=2 * SETS,
            qlo=2 * SETS, recip=1, sumsT=1, placed=1, spread=NH * L_PAIRS, divided=NH * L_PAIRS))
        A = signals(sems, nc, "la", dict(
            score=J, negmax=J, exp=J, turnedP=(NU, 2), pthi=NU, ptlo=(NU, 2),
            pv=(J // 2, 2), yout=J // 4, kept=1))
        wload = sems.enter_context(nc.semaphore("l_wload"))
        pload = sems.enter_context(nc.semaphore("l_pload"))
        xload = sems.enter_context(nc.semaphore("l_xload"))
        ustore = sems.enter_context(nc.semaphore("l_ustore"))
        consts = sems.enter_context(nc.semaphore("l_consts"))
        block = ctx.enter_context(nc.Block())

        @block.sync
        def _(sp):
            for dst, src in ((wkva, W["l_wkva"]), (wo, W["l_wo"])):
                sp.dma_start(dst[:, :, :], src).then_inc(wload, 16)
            for dst, src in ((w_ln, W["l_ln1"]), (cos, K["lcos"]), (sin, K["lsin"]),
                             (tile_of, K["l_tile"])):
                sp.dma_start(dst[:, :], src).then_inc(wload, 16)
            sp.dma_start(heads[:, :, :], K["l_heads"]).then_inc(wload, 16)
            sp.dma_start(wq[:, :, :], W["l_wq"][0:1]).then_inc(pload, 16)
            sp.dma_start(wkp[:, :], W["l_wkp"][0:1]).then_inc(pload, 16)
            with sp.Fori(0, B) as b:
                sp.wait_ge(S["proj"].sem, S["proj"].at(b, 0))
                sp.dma_start(xb, X[:, bass.ds(b * TT, TT), :]).then_inc(xload, 16)
                sp.dma_start(cb[:, :], ROWSd[:, 2, bass.ds(b, 1), :]).then_inc(xload, 16)
                sp.dma_start(sbias[:, :], ROWSd[:, 3, bass.ds(b, 1), :]).then_inc(xload, 16)
            sp.wait_ge(ustore, B * 16 + 1)
            sp.wait_ge(pload, (B * SETS + 1) * 32)

        @block.vector
        def _(v):
            for sig in (N1["stats"], N1["rstd"], N1["xn"]):
                sig.open(v)
            for name in ("stats", "sq", "rstd", "xn", "shufk", "ropek", "added", "free", "cosq", "qlo",
                         "recip", "placed", "divided"):
                S[name].open(v)
            for name in ("negmax", "ptlo", "kept"):
                A[name].open(v)
            v.memset(val[:, :, :, :].bitcast(F32), 0.0).then_inc(consts, 1)
            v.wait_ge(wload, 7 * 16)
            v.wait_ge(consts, 1)
            swap = [i ^ 1 for i in range(32)]

            def project(b, s, par, unit):
                v.wait_ge(S["pj"].sem, S["pj"].at(b, s * 5 + unit + 1))
                if unit in (L.K0, L.K1):
                    cols = slice((unit - L.K0) * HALF, (unit - L.K0 + 1) * HALF)
                    v.wait_ge(S["hi"].sem, S["hi"].at(b, s * 5 + unit + 1))
                    v.scalar_tensor_tensor(klo[:, par, cols], PJ[:, :], L_D ** -0.5,
                                           khi[:, par, cols].bitcast(F32), ALU.mult, ALU.subtract)\
                        .then_inc(S["free"].sem, 1)
                elif unit in (L.Q0, L.Q1):
                    h = unit - L.Q0
                    v.wait_ge(S["qlo"].sem, S["qlo"].at(b, s * 2 + h))
                    v.tensor_tensor(rot[:, :], PJ[:, :], cos[:, h * HALF:(h + 1) * HALF], ALU.mult)\
                        .then_inc(S["cosq"].sem, 1)
                    v.stream_shuffle(shuf[:, :], PJ[:, :], swap).then_inc(S["free"].sem, 1)
                else:
                    v.wait_ge(S["hi"].sem, S["hi"].at(b, s * 5 + unit + 1))
                    pj4 = PJ[:, :].rearrange("p (t h d) -> p t h d", h=2, d=NOPE)
                    v.tensor_tensor(hi_lo(par, 1), pj4, hi_lo(par, 0).bitcast(F32), ALU.subtract)\
                        .then_inc(S["free"].sem, 1)

            def hi_lo(par, part):
                return val[:, par].rearrange("p t (a n d) -> p t a n d", a=3, n=2)[:, :, 0:3:2, part, :]

            def qlow(b, s, par, h):
                v.wait_ge(S["hi"].sem, S["hi"].at(b, s * 5 + L.Q0 + h + 1))
                cols = slice(h * HALF, (h + 1) * HALF)
                v.tensor_tensor(qlo[:, par, cols], rot[:, :], qhi[:, par, cols].bitcast(F32),
                                ALU.subtract).then_inc(S["qlo"].sem, 1)

            with v.Fori(0, B) as b:
                v.wait_ge(xload, b * 48 + 48)
                ln_vector(v, b, N1, xb, st, mv, std, rstd, xn, S["u"])
                v.wait_ge(S["u"].sem, S["u"].at(b, TT))
                ln_vector(v, b, S, ub, st, mv, std, rstd, xn, S["turned"], rms=True)
                v.wait_ge(S["ckv"].sem, S["ckv"].at(b, 1))
                sh = YT[0:64, 0, :]
                v.tensor_tensor(kvr[:, :], S2[0][0:64, :], cos[0:64, :], ALU.mult).then_inc(S["ropek"].sem, 1)
                v.stream_shuffle(sh, S2[0][0:64, :], swap).then_inc(S["shufk"].sem, 1)
                v.wait_ge(S["shufk"].sem, S["shufk"].at(b, 1))
                v.tensor_tensor(sh, sh, sin[0:64, :], ALU.mult).then_inc(S["ropek"].sem, 1)
                v.wait_ge(S["ropek"].sem, S["ropek"].at(b, 2))
                v.tensor_tensor(kvr[:, :], kvr[:, :], sh, ALU.add).then_inc(S["ropek"].sem, 1)
                for unit in range(5):
                    project(b, 0, 0, unit)
                    if unit in (L.Q0, L.Q1):
                        qlow(b, 0, 0, unit - L.Q0)
                with v.Fori(0, NQ) as m:
                    turn = b * NQ + m

                    def rowmax(j):
                        v.wait_ge(A["score"].sem, A["score"].at(turn, j + 1))
                        v.tensor_reduce(negmax[:, j:j + 1], S2[j % 2][:, 0:L.n(j)], AX.X, ALU.max,
                                        negate=True).then_inc(A["negmax"].sem, 1)

                    def low(j):
                        for u in L.of(j):
                            _, k0, nb = L.units[u]
                            at = (slice(None), j // 2 % 2, slice(k0, k0 + nb), slice(j % 2 * P, j % 2 * P + P))
                            v.wait_ge(A["pthi"].sem, A["pthi"].at(turn, u + 1))
                            v.tensor_tensor(PTlo[at], TR[u % 2][:, 0:nb * P].rearrange("p (k q) -> p k q", q=P),
                                            PThi[at].bitcast(F32), ALU.subtract).then_inc(A["ptlo"].sem, 1)

                    rowmax(0)
                    rowmax(1)
                    for j in range(J):
                        s, pr = j % 16, L.pair(j)
                        if j + 2 < J:
                            rowmax(j + 2)
                        if s in L.FREE_AT:
                            project(b, 2 * m + 1 + pr, 1 - pr, L.FREE_AT[s])
                        if s in L.QLO_AT:
                            qlow(b, 2 * m + 1 + pr, 1 - pr, L.QLO_AT[s])
                        low(j)
                    v.wait_ge(A["exp"].sem, A["exp"].at(turn, J))
                    v.tensor_scalar(allsums[:, bass.ds(J * m, J)], sums[:, :], 1.0, None, ALU.mult)\
                        .then_inc(A["kept"].sem, 1)
                v.wait_ge(A["kept"].sem, A["kept"].at(b * NQ + (NQ - 1), 1))
                v.reciprocal(allsums[:, :], allsums[:, :]).then_inc(S["recip"].sem, 1)
                v.wait_ge(S["sumsT"].sem, S["sumsT"].at(b, 1))
                v.tensor_tensor(placed, PJ[:, None, 0:P].broadcast_to([P, TT, P]),
                                tile_of[:, :, None].broadcast_to([P, TT, P]), ALU.mult)\
                    .then_inc(S["placed"].sem, 1)
                for n in range(NH * L_PAIRS):
                    half, pair = n // L_PAIRS, n % L_PAIRS
                    y = YT[:, pair, half * HALF:(half + 1) * HALF]
                    v.wait_ge(S["spread"].sem, S["spread"].at(b, n + 1))
                    v.tensor_tensor(y, y, pbanks[n % 4], ALU.mult).then_inc(S["divided"].sem, 1)
                for t in range(TT):
                    v.wait_ge(S["proj"].sem, S["proj"].at(b, t + 1))
                    v.tensor_tensor(ub[:, t, :], ub[:, t, :], pbanks[t % 4][:, 0:C], ALU.add)\
                        .then_inc(S["added"].sem, 1)

        @block.gpsimd
        def _(g):
            for name in ("scaled", "u", "sinq", "ropeq"):
                S[name].open(g)
            g.sem_inc(ustore, 1)

            def rope(b, s, h):
                g.wait_ge(S["free"].sem, S["free"].at(b, s * 5 + L.Q0 + h + 1))
                g.tensor_tensor(shuf[:, :], shuf[:, :], sin[:, h * HALF:(h + 1) * HALF], ALU.mult)\
                    .then_inc(S["sinq"].sem, 1)
                g.wait_ge(S["sinq"].sem, S["sinq"].at(b, s * 2 + h + 1))
                g.tensor_tensor(rot[:, :], rot[:, :], shuf[:, :], ALU.add)\
                    .then_inc(S["ropeq"].sem, 1)

            with g.Fori(0, B) as b:
                g.wait_ge(ustore, b * 16 + 1)
                for t in range(TT):
                    g.wait_ge(N1["xn"].sem, N1["xn"].at(b, t + 1))
                    g.tensor_tensor(ub[:, t, :], xn[:, t, :], cb[:, :], ALU.mult)\
                        .then_inc(S["scaled"].sem, 1)
                    g.wait_ge(S["scaled"].sem, S["scaled"].at(b, t + 1))
                    g.tensor_tensor(ub[:, t, :], ub[:, t, :], sbias[:, :], ALU.add)\
                        .then_inc(S["u"].sem, 1)
                for h in range(2):
                    rope(b, 0, h)
                with g.Fori(0, NQ) as m:
                    for pr in range(2):
                        for h in range(2):
                            rope(b, 2 * m + 1 + pr, h)

        @block.scalar
        def _(a):
            for sig in (N1["std"], S["std"], S["hT"], S["hi"], A["exp"], A["pthi"], A["yout"]):
                sig.open(a)

            def high(b, s, par, unit):
                cols = slice(unit % 2 * HALF, (unit % 2 + 1) * HALF)
                if unit in (L.Q0, L.Q1):
                    a.wait_ge(S["ropeq"].sem, S["ropeq"].at(b, s * 2 + unit - L.Q0 + 1))
                    a.activation(qhi[:, par, cols], rot[:, :], ACT.Copy)\
                        .then_inc(S["hi"].sem, 1)
                    return
                a.wait_ge(S["pj"].sem, S["pj"].at(b, s * 5 + unit + 1))
                if unit == L.VAL:
                    out = val[:, par].rearrange("p t (a n d) -> p t a n d", a=3, n=2)[:, :, 0:3:2, 0, :]
                    a.activation(out, PJ[:, :].rearrange("p (t h d) -> p t h d", h=2, d=NOPE), ACT.Copy)\
                        .then_inc(S["hi"].sem, 1)
                else:
                    a.activation(khi[:, par, cols], PJ[:, :], ACT.Copy, scale=L_D ** -0.5)\
                        .then_inc(S["hi"].sem, 1)

            with a.Fori(0, B) as b:
                ln_scalar_std(a, b, N1, mv, std, eps)
                ln_scalar_std(a, b, S, mv, std, eps, rms=True)
                ln_scalar_out(a, b, S, rT, 0, pbanks, lambda k: w_ln[:, k:k + 1], None)
                for unit in range(5):
                    high(b, 0, 0, unit)
                a.dma_start(wq[:, :, :], W["l_wq"][1:2]).then_inc(pload, 16)
                a.dma_start(wkp[:, :], W["l_wkp"][1:2]).then_inc(pload, 16)
                with a.Fori(0, NQ) as m:
                    turn = b * NQ + m

                    def exp(j):
                        a.wait_ge(A["turnedP"].sem, A["turnedP"].at(turn, L.before[j - 1] if j else
                                                                    L.before[-1] - NU))
                        a.wait_ge(A["negmax"].sem, A["negmax"].at(turn, j + 1))
                        a.activation(Pt[:, j % 2, 0:L.n(j)], S2[j % 2][:, 0:L.n(j)], ACT.Exp,
                                     bias=negmax[:, j:j + 1], accum_out=sums[:, j:j + 1])\
                            .then_inc(A["exp"].sem, 1)

                    def pt_high(j):
                        for u in L.of(j):
                            _, k0, nb = L.units[u]
                            at = (slice(None), j // 2 % 2, slice(k0, k0 + nb), slice(j % 2 * P, j % 2 * P + P))
                            a.wait_ge(A["pv"].sem, A["pv"].at(turn, j // 2 - 1))
                            a.wait_ge(A["turnedP"].sem, A["turnedP"].at(turn, u + 1))
                            a.activation(PThi[at], TR[u % 2][:, 0:nb * P].rearrange("p (k q) -> p k q", q=P),
                                         ACT.Copy).then_inc(A["pthi"].sem, 1)

                    def y_out(g):
                        a.wait_ge(A["pv"].sem, A["pv"].at(turn, 2 * g + 2))
                        a.activation(YT[:, bass.ds(2 * m + g // 4, 1), (g % 4) * 2 * P:(g % 4 + 1) * 2 * P],
                                     O[:, None, 0:2 * P], ACT.Copy).then_inc(A["yout"].sem, 1)

                    a.wait_ge(A["kept"].sem, A["kept"].at(turn, 0))
                    exp(0)
                    for j in range(J):
                        s, pr = j % 16, L.pair(j)
                        if j + 1 < J:
                            exp(j + 1)
                        if j >= 6 and (j - 6) % 4 == 0:
                            y_out((j - 6) // 4)
                        if s in L.HI_AT:
                            high(b, 2 * m + 1 + pr, 1 - pr, L.HI_AT[s])
                        if s == 12:
                            a.dma_start(wq[:, :, :], W["l_wq"][bass.ds(2 * m + 2 + pr, 1)]).then_inc(pload, 16)
                            a.dma_start(wkp[:, :], W["l_wkp"][bass.ds(2 * m + 2 + pr, 1)]).then_inc(pload, 16)
                        pt_high(j)
                    y_out(J // 4 - 1)
                a.wait_ge(S["added"].sem, S["added"].at(b, TT))
                a.dma_start(Ud[:, bass.ds(b * TT, TT), :], ub[:, :, :]).then_inc(ustore, 16)

        @block.tensor
        def _(pe):
            for name in ("turned", "ckv", "pj", "proj", "sumsT", "spread"):
                S[name].open(pe)
            for name in ("score", "turnedP", "pv"):
                A[name].open(pe)
            pe.wait_ge(wload, 7 * 16)

            def project(b, s, par, unit):
                pe.wait_ge(S["free"].sem, S["free"].at(b, s * 5 + unit))
                cols = slice(unit % 2 * HALF, (unit % 2 + 1) * HALF)
                if unit in (L.K0, L.K1):
                    mm = pe.matmul(PJ[:, :], wkp[:, :], kvr[:, cols], start=True, stop=True)
                elif unit in (L.Q0, L.Q1):
                    for k in range(KC):
                        mm = pe.matmul(PJ[:, :], wq[:, k, :], rT[:, k, cols],
                                       start=(k == 0), stop=(k == KC - 1))
                else:
                    wv = wkp[0:LATENT, :].rearrange("r (h d) -> r h d", h=2)[:, :, 0:NOPE]
                    for t in range(TT):
                        mm = pe.matmul(PJ[:, t * 64:(t + 1) * 64].rearrange("p (h d) -> p h d", h=2),
                                       kvr[0:LATENT, t * P:(t + 1) * P], wv, start=True, stop=True)
                mm.then_inc(S["pj"].sem, 1)

            with pe.Fori(0, B) as b:
                pe.wait_ge(S["added"].sem, S["added"].at(b, 0))
                ln_tensor(pe, b, S, xn, ident, pbanks)
                pe.wait_ge(S["hT"].sem, S["hT"].at(b, 2 * KC))
                for half in range(NH):
                    for k in range(KC):
                        mm = pe.matmul(S2[0][0:64, half * HALF:(half + 1) * HALF], wkva[:, k, :],
                                       rT[:, k, half * HALF:(half + 1) * HALF],
                                       start=(k == 0), stop=(k == KC - 1))
                mm.then_inc(S["ckv"].sem, 1)
                pe.wait_ge(S["ropek"].sem, S["ropek"].at(b, 3))
                pe.wait_ge(pload, b * (SETS * 32) + 32)
                for unit in range(5):
                    project(b, 0, 0, unit)
                with pe.Fori(0, NQ) as m:
                    turn = b * NQ + m

                    def score(j):
                        n, qt, par = L.n(j), L.qt(j), L.pair(j)
                        rows = slice(64 * L.head(j), 64 * L.head(j) + 64)
                        s = 2 * m + par
                        if j % 16 == 0:
                            pe.wait_ge(S["qlo"].sem, S["qlo"].at(b, s * 2 + 2))
                            pe.wait_ge(S["free"].sem, S["free"].at(b, s * 5 + 5))
                        if j >= 2:
                            pe.wait_ge(A["exp"].sem, A["exp"].at(turn, j - 1))
                        for n0 in range(0, n, HALF):
                            n1 = min(n, n0 + HALF)
                            diagonal = n1 == n
                            if diagonal:
                                pe.matmul(S2[j % 2][:, n - P:n], identb[:, :], causal[:, :], start=True,
                                          stop=False, skip_group_check=True)
                            for i, (q, k) in enumerate(((qhi, khi), (qhi, klo), (qlo, khi))):
                                mm = pe.matmul(S2[j % 2][:, n0:n1], q[rows, par, qt * P:(qt + 1) * P],
                                               k[rows, par, n0:n1], start=(i == 0 and not diagonal),
                                               stop=(i == 2), skip_group_check=diagonal)
                        mm.then_inc(A["score"].sem, 1)

                    def turn_p(j):
                        pe.wait_ge(A["exp"].sem, A["exp"].at(turn, j + 1))
                        for u in L.of(j):
                            _, k0, nb = L.units[u]
                            pe.wait_ge(A["ptlo"].sem, A["ptlo"].at(turn, u - 1))
                            for i in range(nb):
                                mm = pe.transpose(TR[u % 2][:, i * P:(i + 1) * P],
                                                  Pt[:, j % 2, (k0 + i) * P:(k0 + i + 1) * P], ident[:, :])
                            mm.then_inc(A["turnedP"].sem, 1)

                    def pv(x):
                        g, h, par = x // 2 % 4, x % 2, x // 8
                        last = 2 * g + 1
                        pe.wait_ge(A["ptlo"].sem, A["ptlo"].at(turn, L.of(2 * x + 1)[-1] + 1))
                        if h == 0:
                            pe.wait_ge(A["yout"].sem, A["yout"].at(turn, x // 2))
                        order = [0, last, *range(1, last)]
                        parts = [(PThi, kt) for kt in order] + [(PTlo, kt) for kt in order[1:] + [0]]
                        for n, (src, kt) in enumerate(parts):
                            c0 = P if kt == last else 0
                            mm = pe.matmul(O[:, c0:2 * P], val[:, par, kt, 64 * h:64 * h + P],
                                           src[:, x % 2, kt, c0:], start=(h == 0 and n == 0),
                                           stop=(h == 1 and n == len(parts) - 1), skip_group_check=True)
                        mm.then_inc(A["pv"].sem, 1)

                    score(0)
                    score(1)
                    for j in range(J):
                        s, pr = j % 16, L.pair(j)
                        if j + 2 < J:
                            score(j + 2)
                        if s in L.PE_AT:
                            if s == min(L.PE_AT):
                                pe.wait_ge(pload, b * (SETS * 32) + (2 * m + 2 + pr) * 32)
                            project(b, 2 * m + 1 + pr, 1 - pr, L.PE_AT[s])
                        if j >= 3 and j % 2 == 1:
                            pv((j - 3) // 2)
                        turn_p(j)
                    pv(J // 2 - 1)
                pe.wait_ge(A["yout"].sem, A["yout"].at(b * NQ + (NQ - 1), J // 4))
                pe.wait_ge(S["recip"].sem, S["recip"].at(b, 1))
                pe.transpose(PJ[:, 0:P], allsums[:, :], ident[:, :]).then_inc(S["sumsT"].sem, 1)
                pe.wait_ge(S["placed"].sem, S["placed"].at(b, 1))
                for n in range(NH * L_PAIRS):
                    half, pair = n // L_PAIRS, n % L_PAIRS
                    if n >= 4:
                        pe.wait_ge(S["divided"].sem, S["divided"].at(b, n - 3))
                    pe.matmul(pbanks[n % 4], heads[:, pair, :], Pt[:, 0, half * HALF:(half + 1) * HALF],
                              start=True, stop=True).then_inc(S["spread"].sem, 1)
                for t in range(TT):
                    if t == 0:
                        pe.wait_ge(S["divided"].sem, S["divided"].at(b, NH * L_PAIRS))
                    if t >= 4:
                        pe.wait_ge(S["added"].sem, S["added"].at(b, t - 3))
                    for k in range(L_PAIRS):
                        mm = pe.matmul(pbanks[t % 4][:, 0:C], YT[:, k, t * P:(t + 1) * P], wo[:, k, :],
                                       start=(k == 0), stop=(k == L_PAIRS - 1))
                    mm.then_inc(S["proj"].sem, 1)


def rope_attention(nc, sems, X, MODT, ROWS, ident, identb, causal, eps, W, K):
    J = TT
    with ExitStack() as ctx:
        def sb(name, shape, dt=F32):
            return ctx.enter_context(nc.sbuf_tensor("r_" + name, shape, dt))

        wq, wk, wv = (sb(n, [P, KC, C]) for n in ("wq", "wk", "wv"))
        cos, sin = sb("cos", [P, KC, T]), sb("sin", [P, KC, T])
        xb = sb("xb", [P, TT, C])
        mod, gate = sb("mod", [P, 12]), sb("gate", [P, C])
        xn = sb("xn", [P, TT, C])
        st, mv = sb("st", [P, TT, 6]), sb("mv", [P, TT, 2])
        std, rstd = sb("std", [P, TT]), sb("rstd", [P, TT])
        hT = sb("hT", [P, KC, T])
        shuf = sb("shuf", [P, 2 * KC, T])
        qk = sb("qk", [P, 2 * KC, T])
        V = sb("V", [P, TT, C])
        Pt, PT = sb("Pt", [P, 2, T]), sb("PT", [P, 2, TT, P])
        negmax, sums, rs = sb("negmax", [P, J]), sb("sums", [P, J]), sb("rs", [P, J])
        tmp = sb("tmp", [P, TT, C])
        S2 = [ctx.enter_context(nc.psum_tensor(f"r_s{i}", [P, 2 * HALF], F32)) for i in range(2)]
        TR = [ctx.enter_context(nc.psum_tensor(f"r_t{i}", [P, HALF], F32)) for i in range(2)]
        O = [ctx.enter_context(nc.psum_tensor(f"r_o{i}", [P, HALF], F32)) for i in range(2)]
        banks = [TR[0][:, :], TR[1][:, :], O[0][:, :], O[1][:, :]]
        S = signals(sems, nc, "r", dict(LN_SIGNALS) | attention_signals(J) | dict(
            proj=4, shufd=4, cosd=4, sind=4, rope=4, vproj=4, vout=4, gated=TT, added=TT))
        wload = sems.enter_context(nc.semaphore("r_wload"))
        xload = sems.enter_context(nc.semaphore("r_xload"))
        xstore = sems.enter_context(nc.semaphore("r_xstore"))
        block = ctx.enter_context(nc.Block())

        @block.sync
        def _(sp):
            for dst, src in ((wq, W["r_wq"]), (wk, W["r_wk"]), (wv, W["r_wv"]), (cos, K["rcos"]),
                             (sin, K["rsin"])):
                sp.dma_start(dst[:, :, :], src).then_inc(wload, 16)
            with sp.Fori(0, B) as b:
                sp.wait_ge(S["added"].sem, S["added"].at(b, 0))
                sp.wait_ge(xstore, b * 16 + 1)
                sp.dma_start(xb[:, :, :], X[:, bass.ds(b * TT, TT), :]).then_inc(xload, 16)
                sp.dma_start(mod[:, :], MODT[:, 1, bass.ds(b, 1), :]).then_inc(xload, 16)
                sp.dma_start(gate[:, :], ROWS[:, 4, bass.ds(b, 1), :]).then_inc(xload, 16)
                sp.wait_ge(S["added"].sem, S["added"].at(b, TT))
                sp.dma_start(X[:, bass.ds(b * TT, TT), :], xb[:, :, :]).then_inc(xstore, 16)
            sp.wait_ge(xstore, B * 16 + 1)

        @block.vector
        def _(v):
            for name in ("stats", "rstd", "xn", "shufd", "cosd", "negmax", "evac2", "recip", "norm"):
                S[name].open(v)
            v.wait_ge(wload, 5 * 16)
            swap = [i ^ 1 for i in range(32)]
            with v.Fori(0, B) as b:
                v.wait_ge(xload, b * 48 + 48)
                ln_vector(v, b, S, xb, st, mv, std, rstd, xn, S["turned"])
                for u in range(4):
                    v.wait_ge(S["proj"].sem, S["proj"].at(b, u + 1))
                    v.tensor_tensor(qk[:, u, :], S2[u % 2][:, :], cos[:, u % KC, :], ALU.mult)\
                        .then_inc(S["cosd"].sem, 1)
                    v.stream_shuffle(shuf[:, u, :], S2[u % 2][:, :], swap).then_inc(S["shufd"].sem, 1)
                att_vector(v, b, S, J, S2, TR, PT, O, negmax, sums, rs, C, lambda j: tmp[:, j, :])

        @block.gpsimd
        def _(g):
            for name in ("sind", "rope", "gated", "added"):
                S[name].open(g)
            g.sem_inc(xstore, 1)
            with g.Fori(0, B) as b:
                for u in range(4):
                    g.wait_ge(S["shufd"].sem, S["shufd"].at(b, u + 1))
                    g.tensor_tensor(shuf[:, u, :], shuf[:, u, :], sin[:, u % KC, :], ALU.mult)\
                        .then_inc(S["sind"].sem, 1)
                    g.wait_ge(S["sind"].sem, S["sind"].at(b, u + 1))
                    g.wait_ge(S["cosd"].sem, S["cosd"].at(b, u + 1))
                    g.tensor_tensor(qk[:, u, :], qk[:, u, :], shuf[:, u, :], ALU.add)\
                        .then_inc(S["rope"].sem, 1)
                for t in range(TT):
                    g.wait_ge(S["norm"].sem, S["norm"].at(b, t + 1))
                    g.tensor_tensor(tmp[:, t, :], tmp[:, t, :], gate[:, :], ALU.mult)\
                        .then_inc(S["gated"].sem, 1)
                    g.wait_ge(S["gated"].sem, S["gated"].at(b, t + 1))
                    g.tensor_tensor(xb[:, t, :], xb[:, t, :], tmp[:, t, :], ALU.add)\
                        .then_inc(S["added"].sem, 1)

        @block.scalar
        def _(a):
            for name in ("std", "hT", "vout", "exp", "evac"):
                S[name].open(a)
            with a.Fori(0, B) as b:
                ln_scalar_std(a, b, S, mv, std, eps)
                ln_scalar_out(a, b, S, hT, 0, banks, lambda k: mod[:, 2 * CA + k:2 * CA + k + 1],
                              lambda k: mod[:, 2 * SA + k:2 * SA + k + 1])
                for u in range(4):
                    a.wait_ge(S["vproj"].sem, S["vproj"].at(b, u + 1))
                    a.activation(V[:, 2 * u:2 * u + 2, :],
                                 banks[u].rearrange("p (t c) -> p t c", t=2), ACT.Copy)\
                        .then_inc(S["vout"].sem, 1)
                att_scalar(a, b, S, J, S2, TR, Pt, PT, negmax, sums)

        @block.tensor
        def _(pe):
            for name in ("turned", "proj", "vproj", "score", "turnedP", "pv"):
                S[name].open(pe)
            pe.wait_ge(wload, 5 * 16)
            with pe.Fori(0, B) as b:
                pe.wait_ge(S["norm"].sem, S["norm"].at(b, 0))
                ln_tensor(pe, b, S, xn, ident, banks)
                pe.wait_ge(S["hT"].sem, S["hT"].at(b, 2 * KC))
                for u in range(4):
                    w, et = (wq, wk)[u // KC], u % KC
                    if u >= 2:
                        pe.wait_ge(S["shufd"].sem, S["shufd"].at(b, u - 1))
                    for half in range(NH):
                        for k in range(KC):
                            mm = pe.matmul(S2[u % 2][:, half * HALF:(half + 1) * HALF],
                                           w[:, k, et * P:(et + 1) * P],
                                           hT[:, k, half * HALF:(half + 1) * HALF],
                                           start=(k == 0), stop=(k == KC - 1))
                    mm.then_inc(S["proj"].sem, 1)
                for u in range(4):
                    for i in range(2):
                        t = 2 * u + i
                        for k in range(KC):
                            mm = pe.matmul(banks[u][:, i * C:(i + 1) * C], hT[:, k, t * P:(t + 1) * P],
                                           wv[:, k, :], start=(k == 0), stop=(k == KC - 1))
                    mm.then_inc(S["vproj"].sem, 1)
                pe.wait_ge(S["rope"].sem, S["rope"].at(b, 4))
                pe.wait_ge(S["vout"].sem, S["vout"].at(b, 4))
                att_tensor(pe, b, S, J,
                           lambda j, k, qt: qk[:, k, qt * P:(qt + 1) * P],
                           lambda j, k, n0, n1: qk[:, KC + k, n0:n1],
                           lambda j, i: V[:, i, :],
                           KC, C, ident, identb, causal, S2, TR, O, Pt, PT)


def experts(nc, sems, name, X, U, MODT, ROWS, ident, identb, eps, W, K, out):
    first = U is not None
    M = MOE0 if first else MOE1
    E, NS = M["experts"], M["shared"]
    NT = NS + M["routed"]
    G = 4
    with ExitStack() as ctx:
        def sb(nm, shape, dt=F32):
            return ctx.enter_context(nc.sbuf_tensor(f"{name}_{nm}", shape, dt))

        wg, wu = sb("wg", [P, NT, KC, P]), sb("wu", [P, NT, KC, P])
        wd = sb("wd", [P, NT, C])
        wr = sb("wr", [P, KC, E])
        rbias = sb("rbias", [P, E])
        lower = sb("lower", [P, E, E])
        selb = sb("selb", [P, M["routed"], P], BF16)
        w_ln = sb("w_ln", [P, KC])
        xb = sb("xb", [P, TT, C])
        ub = sb("ub", [P, TT, C]) if first else None
        mod, gate = sb("mod", [P, 12]), sb("gate", [P, C])
        xn = sb("xn", [P, TT, C])
        st, mv = sb("st", [P, TT, 6]), sb("mv", [P, TT, 2])
        std, rstd = sb("std", [P, TT]), sb("rstd", [P, TT])
        hT = sb("hT", [P, KC, T])
        score, key = sb("score", [P, TT, E]), sb("key", [P, TT, E])
        red = sb("red", [P, TT])
        r1, r2 = sb("r1", [P, TT * E * E]), sb("r2", [P, TT * E * E])
        rank, comb = sb("rank", [P, TT, E]), sb("comb", [P, TT, E])
        gA, gB, gC, gD = (sb(n, [P, TT * G]) for n in ("gA", "gB", "gC", "gD"))
        comb3 = sb("comb3", [P, TT, P], BF16)
        combT = sb("combT", [P, T], BF16)
        sg, hid = sb("sg", [P, 2, HALF]), sb("hid", [P, 2, HALF])
        tmp = sb("tmp", [P, 2, C])
        Gb = [ctx.enter_context(nc.psum_tensor(f"{name}_g{i}", [P, HALF], F32)) for i in range(2)]
        Ub = [ctx.enter_context(nc.psum_tensor(f"{name}_u{i}", [P, HALF], F32)) for i in range(2)]
        Cb = [ctx.enter_context(nc.psum_tensor(f"{name}_c{i}", [P, HALF], F32)) for i in range(2)]
        acc = [ctx.enter_context(nc.psum_tensor(f"{name}_a{i}", [P, HALF], F32)) for i in range(2)]
        CHAIN = 17 if first else 33
        NJ = NH * NT
        NR = NH * M["routed"]
        S = signals(sems, nc, name, dict(LN_SIGNALS) | dict(
            sq=2, logits=1, act=1, chain=(CHAIN, 0), comb=1, combP=1, combT=1, gate=NJ, up=NJ, cb=NR, silu=NJ,
            mul=NJ, hid=NR, down=(NJ, 2), y=TT, gated=TT, added=(TT, 2)))
        wload = sems.enter_context(nc.semaphore(name + "_wload"))
        xload = sems.enter_context(nc.semaphore(name + "_xload"))
        xstore = sems.enter_context(nc.semaphore(name + "_xstore"))
        consts = sems.enter_context(nc.semaphore(name + "_consts"))
        block = ctx.enter_context(nc.Block())
        loads = 48 + 16 * first

        def routed(n):
            return n // NT * M["routed"] + max(0, n % NT - NS)

        @block.sync
        def _(sp):
            sp.dma_start(wr[:, :, :], W[name + "_wr"]).then_inc(wload, 16)
            sp.dma_start(rbias[:, :], W[name + "_rb"].partition_broadcast(P)).then_inc(wload, 16)
            sp.dma_start(lower[:, :, :], K[name + "_lower"]).then_inc(wload, 16)
            sp.dma_start(w_ln[:, :], W["m0_ln"]).then_inc(wload, 16)
            sp.dma_start(r1[:, 0:M["routed"] * P].rearrange("p (j m) -> p j m", m=P) if not first else
                         wg[:, 0:4].rearrange("p a k m -> p (a k) m"), K[name + "_sel"]).then_inc(wload, 16)
            sp.wait_ge(consts, 2)
            for dst, src in ((wg, W[name + "_wg"]), (wu, W[name + "_wu"])):
                sp.dma_start(dst[:, :, :, :], src).then_inc(wload, 16)
            sp.dma_start(wd[:, :, :], W[name + "_wd"]).then_inc(wload, 16)
            with sp.Fori(0, B) as b:
                sp.wait_ge(S["added"].sem, S["added"].at(b, 0))
                sp.wait_ge(xstore, b * 16 + 1)
                sp.dma_start(xb[:, :, :], X[:, bass.ds(b * TT, TT), :]).then_inc(xload, 16)
                if first:
                    sp.dma_start(ub[:, :, :], U[:, bass.ds(b * TT, TT), :]).then_inc(xload, 16)
                sp.dma_start(mod[:, :], MODT[:, 1, bass.ds(b, 1), :]).then_inc(xload, 16)
                sp.dma_start(gate[:, :], ROWS[:, 1 if first else 5, bass.ds(b, 1), :]).then_inc(xload, 16)
                sp.wait_ge(S["added"].sem, S["added"].at(b, TT))
                if first:
                    sp.dma_start(X[:, bass.ds(b * TT, TT), :], xb[:, :, :]).then_inc(xstore, 16)
                else:
                    sp.dma_start(out[bass.ds(b, 1)].rearrange("b (t p) c -> p (b t) c", p=P), xb[:, :, :])\
                        .then_inc(xstore, 16)
            sp.wait_ge(xstore, B * 16 + 1)

        @block.vector
        def _(v):
            for nm in ("stats", "sq", "rstd", "xn", "comb", "combT", "mul", "hid", "y"):
                S[nm].open(v)
            v.wait_ge(wload, 5 * 16)
            v.tensor_copy(selb[:, :, :], (wg[:, 0:4].rearrange("p a k m -> p (a k) m") if first else
                          r1[:, 0:M["routed"] * P].rearrange("p (j m) -> p j m", m=P))).then_inc(consts, 1)
            v.memset(comb3[:, :, :], 0.0).then_inc(consts, 1)
            v.wait_ge(consts, 2)
            with v.Fori(0, B) as b:
                v.wait_ge(xload, b * loads + loads)
                ln_vector(v, b, S, ub if first else xb, st, mv, std, rstd, xn, S["turned"], rms=first)

                steps = [0]

                def link(ins):
                    steps[0] += 1
                    ins.then_inc(S["chain"].sem, 1)
                    v.wait_ge(S["chain"].sem, b * CHAIN + steps[0])

                def over(x):
                    return x[:, :, None].broadcast_to([P, TT, E])

                lg = Gb[0][:, 0:TT * E].rearrange("p (t e) -> p t e", e=E)
                bias = rbias[:, None, :].broadcast_to([P, TT, E])

                def ranks(x, n, e, low, dst):
                    size = n * e * e
                    a3 = r1[:, 0:size].rearrange("p (t i j) -> p t i j", i=e, j=e)
                    b3 = r2[:, 0:size].rearrange("p (t i j) -> p t i j", i=e, j=e)
                    other = x[:, :, None, :].broadcast_to([P, n, e, e])
                    mine = x[:, :, :, None].broadcast_to([P, n, e, e])
                    link(v.tensor_tensor(a3, other, mine, ALU.is_gt))
                    link(v.tensor_tensor(b3, other, mine, ALU.is_equal))
                    link(v.tensor_tensor(b3, b3, low[:, None, :, :].broadcast_to([P, n, e, e]), ALU.mult))
                    link(v.tensor_tensor(r1[:, 0:size], r1[:, 0:size], r2[:, 0:size], ALU.add))
                    link(v.tensor_reduce(dst, r1[:, 0:size].rearrange("p (t j) -> p t j", j=e), AX.X, ALU.add))

                v.wait_ge(S["logits"].sem, S["logits"].at(b, 1))
                if first:
                    link(v.tensor_tensor(key[:, :, :], lg, bias, ALU.add))
                    link(v.tensor_reduce(red[:, :], key[:, :, :], AX.X, ALU.max))
                    v.tensor_tensor(key[:, :, :], key[:, :, :], over(red), ALU.subtract)\
                        .then_inc(S["comb"].sem, 1)
                    v.wait_ge(S["act"].sem, S["act"].at(b, 1))
                    ranks(score[:, :, :], TT, E, lower[:, :, :], rank[:, :, :].rearrange("p t e -> p (t e)"))
                    keep = 2
                else:
                    v.wait_ge(S["act"].sem, S["act"].at(b, 1))
                    link(v.tensor_tensor(key[:, :, :], score[:, :, :], bias, ALU.add))
                    g4 = key[:, :, :].rearrange("p t (g i) -> p (t g) i", i=4)
                    link(v.tensor_tensor(gA[:, :], g4[:, :, 0], g4[:, :, 1], ALU.max))
                    link(v.tensor_tensor(gB[:, :], g4[:, :, 0], g4[:, :, 1], ALU.min))
                    link(v.tensor_tensor(gC[:, :], g4[:, :, 2], g4[:, :, 3], ALU.max))
                    link(v.tensor_tensor(gD[:, :], g4[:, :, 2], g4[:, :, 3], ALU.min))
                    link(v.tensor_tensor(gB[:, :], gB[:, :], gD[:, :], ALU.max))
                    link(v.tensor_tensor(gD[:, :], gA[:, :], gC[:, :], ALU.min))
                    link(v.tensor_tensor(gB[:, :], gB[:, :], gD[:, :], ALU.max))
                    link(v.tensor_tensor(gA[:, :], gA[:, :], gC[:, :], ALU.max))
                    link(v.tensor_tensor(gA[:, :], gA[:, :], gB[:, :], ALU.add))
                    ranks(gA[:, :].rearrange("p (t g) -> p t g", g=G), TT, G, lower[:, 0:G, 0:G], gC[:, :])
                    link(v.tensor_scalar(gC[:, :], gC[:, :], 2.0, MASKED, ALU.is_ge, ALU.mult))
                    link(v.tensor_tensor(g4, g4, gC[:, :, None].broadcast_to([P, TT * G, 4]), ALU.add))
                    ranks(key[:, :, :], TT, E, lower[:, :, :], rank[:, :, :].rearrange("p t e -> p (t e)"))
                    keep = 4
                link(v.tensor_scalar(rank[:, :, :], rank[:, :, :], float(keep), None, ALU.is_lt))
                link(v.tensor_tensor(comb[:, :, :], score[:, :, :], rank[:, :, :], ALU.mult))
                link(v.tensor_reduce(red[:, :], comb[:, :, :], AX.X, ALU.add))
                if not first:
                    link(v.tensor_scalar(red[:, :], red[:, :], 1e-20, None, ALU.add))
                link(v.reciprocal(red[:, :], red[:, :]))
                link(v.tensor_tensor(comb[:, :, :], comb[:, :, :], over(red), ALU.mult))
                v.wait_ge(S["combP"].sem, S["combP"].at(b, 0))
                for s in range(3):
                    link(v.tensor_copy(comb3[:, :, s * E:(s + 1) * E], comb[:, :, :]))
                    if s < 2:
                        link(v.tensor_tensor(comb[:, :, :], comb[:, :, :], comb3[:, :, s * E:(s + 1) * E],
                                             ALU.subtract))
                assert steps[0] == CHAIN

                def hidden(c, j):
                    n = c * NT + j
                    v.wait_ge(S["silu"].sem, S["silu"].at(b, n + 1))
                    v.wait_ge(S["up"].sem, S["up"].at(b, n + 1))
                    v.wait_ge(S["down"].sem, S["down"].at(b, n - 1))
                    v.tensor_tensor(hid[:, n % 2, :], Ub[n % 2][:, :], sg[:, n % 2, :], ALU.mult)\
                        .then_inc(S["mul"].sem, 1)
                    if j >= NS:
                        v.wait_ge(S["mul"].sem, S["mul"].at(b, n + 1))
                        v.wait_ge(S["cb"].sem, S["cb"].at(b, routed(n + 1)))
                        v.tensor_tensor(hid[:, n % 2, :], hid[:, n % 2, :], Cb[n % 2][:, :], ALU.mult)\
                            .then_inc(S["hid"].sem, 1)

                def split():
                    v.wait_ge(S["combP"].sem, S["combP"].at(b, 1))
                    v.tensor_copy(combT[:, :], Cb[1][:, :].bitcast(BF16)).then_inc(S["combT"].sem, 1)

                split()
                for c in range(NH):
                    for j in range(NT):
                        hidden(c, j)
                    for i in range(4):
                        t = 4 * c + i
                        v.wait_ge(S["down"].sem, S["down"].at(b, (c + 1) * NT))
                        v.wait_ge(S["added"].sem, S["added"].at(b, t - 1))
                        src = acc[i // 2][:, (i % 2) * C:(i % 2 + 1) * C]
                        v.tensor_tensor(tmp[:, t % 2, :], src, ub[:, t, :] if first else gate[:, :],
                                        ALU.add if first else ALU.mult).then_inc(S["y"].sem, 1)

        @block.gpsimd
        def _(g):
            for nm in ("gated", "added"):
                S[nm].open(g)
            g.sem_inc(xstore, 1)
            with g.Fori(0, B) as b:
                for t in range(TT):
                    g.wait_ge(S["y"].sem, S["y"].at(b, t + 1))
                    if first:
                        g.tensor_tensor(tmp[:, t % 2, :], tmp[:, t % 2, :], gate[:, :], ALU.mult)\
                            .then_inc(S["gated"].sem, 1)
                        g.wait_ge(S["gated"].sem, S["gated"].at(b, t + 1))
                    g.tensor_tensor(xb[:, t, :], xb[:, t, :], tmp[:, t % 2, :], ALU.add)\
                        .then_inc(S["added"].sem, 1)

        @block.scalar
        def _(a):
            for nm in ("std", "hT", "act", "silu"):
                S[nm].open(a)
            with a.Fori(0, B) as b:
                ln_scalar_std(a, b, S, mv, std, eps, rms=first)
                banks = [Ub[0][:, :], Ub[1][:, :], acc[0][:, :], acc[1][:, :]]
                if first:
                    ln_scalar_out(a, b, S, hT, 0, banks, lambda k: w_ln[:, k:k + 1], None)
                    a.wait_ge(S["comb"].sem, S["comb"].at(b, 1))
                    a.activation(score[:, :, :], key[:, :, :], ACT.Exp).then_inc(S["act"].sem, 1)
                else:
                    ln_scalar_out(a, b, S, hT, 0, banks, lambda k: mod[:, 2 * CB + k:2 * CB + k + 1],
                                  lambda k: mod[:, 2 * SB + k:2 * SB + k + 1])
                    a.wait_ge(S["logits"].sem, S["logits"].at(b, 1))
                    a.activation(score[:, :, :], Gb[0][:, 0:TT * E].rearrange("p (t e) -> p t e", e=E),
                                 ACT.Sigmoid).then_inc(S["act"].sem, 1)
                for n in range(NJ):
                    a.wait_ge(S["gate"].sem, S["gate"].at(b, n + 1))
                    if n >= 2:
                        a.wait_ge(S["mul"].sem, S["mul"].at(b, n - 1))
                    a.activation(sg[:, n % 2, :], Gb[n % 2][:, :], ACT.Silu).then_inc(S["silu"].sem, 1)

        @block.tensor
        def _(pe):
            for nm in ("turned", "logits", "combP", "gate", "up", "cb", "down"):
                S[nm].open(pe)
            pe.wait_ge(wload, 8 * 16)
            with pe.Fori(0, B) as b:
                pe.wait_ge(S["y"].sem, S["y"].at(b, 0))
                ln_tensor(pe, b, S, xn, ident, [Ub[0][:, :], Ub[1][:, :], acc[0][:, :], acc[1][:, :]])
                pe.wait_ge(S["hT"].sem, S["hT"].at(b, 2 * KC))
                for t in range(TT):
                    for k in range(KC):
                        mm = pe.matmul(Gb[0][:, t * E:(t + 1) * E], hT[:, k, t * P:(t + 1) * P],
                                       wr[:, k, :], start=(k == 0), stop=(k == KC - 1))
                mm.then_inc(S["logits"].sem, 1)
                pe.wait_ge(S["chain"].sem, b * CHAIN + CHAIN)
                for t in range(TT):
                    mm = pe.transpose(Cb[1][:, :].bitcast(BF16)[:, t * P:(t + 1) * P], comb3[:, t, :],
                                      identb[:, :])
                mm.then_inc(S["combP"].sem, 1)
                pe.wait_ge(S["combT"].sem, S["combT"].at(b, 1))

                def up(c, j):
                    n = c * NT + j
                    cols = slice(c * HALF, (c + 1) * HALF)
                    if n >= 2:
                        pe.wait_ge(S["silu"].sem, S["silu"].at(b, n - 1))
                    for k in range(KC):
                        mm = pe.matmul(Gb[n % 2][:, :], wg[:, j, k, :], hT[:, k, cols],
                                       start=(k == 0), stop=(k == KC - 1))
                    mm.then_inc(S["gate"].sem, 1)
                    if n >= 2:
                        pe.wait_ge(S["mul"].sem, S["mul"].at(b, n - 1))
                        if routed(n - 1):
                            pe.wait_ge(S["hid"].sem, S["hid"].at(b, routed(n - 1)))
                    for k in range(KC):
                        mm = pe.matmul(Ub[n % 2][:, :], wu[:, j, k, :], hT[:, k, cols],
                                       start=(k == 0), stop=(k == KC - 1))
                    mm.then_inc(S["up"].sem, 1)
                    if j >= NS:
                        pe.matmul(Cb[n % 2][:, :], selb[:, j - NS, :], combT[:, cols],
                                  start=True, stop=True).then_inc(S["cb"].sem, 1)

                def down(c, j):
                    n = c * NT + j
                    if j < NS:
                        pe.wait_ge(S["mul"].sem, S["mul"].at(b, n + 1))
                    else:
                        pe.wait_ge(S["hid"].sem, S["hid"].at(b, routed(n + 1)))
                    if c >= 1 and j == 0:
                        pe.wait_ge(S["y"].sem, S["y"].at(b, 4 * c))
                    for i in range(4):
                        mm = pe.matmul(acc[i // 2][:, (i % 2) * C:(i % 2 + 1) * C],
                                       hid[:, n % 2, i * P:(i + 1) * P], wd[:, j, :],
                                       start=(j == 0 and i % 2 == 0), stop=(j == NT - 1),
                                       skip_group_check=True)
                    mm.then_inc(S["down"].sem, 1)

                order = [(c, j) for c in range(NH) for j in range(NT)]
                up(*order[0])
                for n, cj in enumerate(order):
                    if n + 1 < len(order):
                        up(*order[n + 1])
                    down(*cj)


def build(nc, w, k, out, upto=5):
    with ExitStack() as ctx:
        def sb(name, shape, dt=F32):
            return ctx.enter_context(nc.sbuf_tensor(name, shape, dt))

        X = sb("X", [P, B * TT, C])
        MODT = sb("MODT", [P, 2, B, 12])
        ROWS = nc.dram_tensor("rows", (P, 6, B, C), F32, kind="Internal").ap()
        U = nc.dram_tensor("u", (P, B * TT, C), F32, kind="Internal").ap()
        ident, identb = sb("ident", [P, P]), sb("identb", [P, P], BF16)
        causal, eps = sb("causal", [P, P], BF16), sb("eps", [P, 1])
        mask = sb("mask", [P, P])
        loaded = ctx.enter_context(nc.semaphore("loaded"))
        ready = ctx.enter_context(nc.semaphore("ready"))
        with nc.Block() as block:
            @block.sync
            def _(sp):
                sp.dma_start(ident[:, :], k["ident"]).then_inc(loaded, 16)
                sp.dma_start(mask[:, :], k["causal"]).then_inc(loaded, 16)
                for b in range(B):
                    sp.dma_start(X[:, b * TT:(b + 1) * TT, :],
                                 w["x"][b].rearrange("(t p) c -> p t c", p=P)).then_inc(loaded, 16)
                sp.wait_ge(loaded, (2 + B) * 16)

            @block.vector
            def _(v):
                v.memset(eps[:, :], EPS).then_inc(ready, 1)
                v.wait_ge(loaded, (2 + B) * 16)
                v.tensor_copy(identb[:, :], ident[:, :]).then_inc(ready, 1)
                v.tensor_copy(causal[:, :], mask[:, :]).then_inc(ready, 1)

        modulation(nc, w["cT"], w["wmod"], MODT, ROWS)
        if upto >= 1:
            windowed_attention(nc, ctx, X, MODT, ROWS, ident, identb, eps, w, k)
        if upto >= 2:
            latent_attention(nc, ctx, X, U, ROWS, ident, identb, causal, eps, w, k)
        if upto >= 3:
            experts(nc, ctx, "m0", X, U, MODT, ROWS, ident, identb, eps, w, k, None)
        if upto >= 4:
            rope_attention(nc, ctx, X, MODT, ROWS, ident, identb, causal, eps, w, k)
        if upto >= 5:
            experts(nc, ctx, "m1", X, None, MODT, ROWS, ident, identb, eps, w, k, out)
        else:
            st = ctx.enter_context(nc.semaphore("dbg"))
            with nc.Block() as block:
                @block.sync
                def _(sp):
                    for b in range(B):
                        sp.dma_start(out[b].rearrange("(t p) c -> p t c", p=P),
                                     (U if upto == 2 else X)[:, b * TT:(b + 1) * TT, :]).then_inc(st, 16)
                    sp.wait_ge(st, 16 * B)


def tables():
    f = np.float32
    i = np.arange(P)
    k = {"ident": np.eye(P, dtype=f)}
    k["causal"] = np.where(i[None, :] <= i[:, None], 0, MASKED).astype(f)
    q = i % WINDOW
    off = i[None, :] - q[:, None]
    k["band"] = np.where((off >= 0) & (off < WINDOW), 0, MASKED).astype(f)
    heads = np.arange(A_HEADS)
    k["hmask"] = (i[:, None] // A_DH == heads[None, :] % (P // A_DH)).astype(f)
    k["own"] = (i[:, None] // WINDOW == np.arange(2)[None, :]).astype(f)
    k["sel64"] = (q[:, None] == np.arange(WINDOW)[None, :]).astype(f)
    job = np.arange(P)
    k["l_tile"] = (2 * (job % 16 // 4) + job % 2)[:, None] == np.arange(TT)[None, :]
    k["l_tile"] = k["l_tile"].astype(f)
    k["l_heads"] = ((job // 16)[:, None, None] == np.arange(L_PAIRS)[None, :, None]) & \
        ((job // 2 % 2)[:, None, None] == (i // 64)[None, None, :])
    k["l_heads"] = k["l_heads"].astype(f)
    t = np.arange(T, dtype=f)

    def angles(theta, d):
        freqs = (1.0 / f(theta) ** (np.arange(0, d, 2, dtype=f) / f(d))).astype(f)
        a = np.repeat(freqs, 2)[:, None] * t[None, :]
        sign = np.where(np.arange(d) % 2 == 0, -1, 1)[:, None]
        return np.cos(a.astype(np.float64)), np.sin(a.astype(np.float64)) * sign

    c, s = angles(100000.0, ROPE)
    kc = np.concatenate([np.ones((NOPE, T)), c])
    ks = np.concatenate([np.zeros((NOPE, T)), s])
    k["lcos"], k["lsin"] = np.tile(kc, (2, 1)).astype(f), np.tile(ks, (2, 1)).astype(f)
    c, s = angles(10000.0, C)
    scale = C ** -0.25
    km = lambda a: np.ascontiguousarray((a * scale).astype(f).reshape(KC, P, T).transpose(1, 0, 2))
    k["rcos"], k["rsin"] = km(c), km(s)
    for name, M in (("m0", MOE0), ("m1", MOE1)):
        E, R = M["experts"], M["routed"]
        e = np.arange(E)
        k[name + "_lower"] = np.broadcast_to((e[None, :] < e[:, None]).astype(f), (P, E, E)).copy()
        sel = np.zeros((P, R, P), f)
        for part in range(3):
            for j in range(R):
                for m in range(P):
                    sel[part * E + (j if E == R else 2 * j + m // 64), j, m] = 1
        k[name + "_sel"] = sel
    return k


def layouts(a):
    def km(w):
        return w.reshape(-1, P, w.shape[-1]).transpose(1, 0, 2)

    w = {"x": a["L0_attn_x"]}
    w["cT"] = np.stack([km(a[f"L{l}_c"].T) for l in range(2)])
    w["wmod"] = np.stack([km(a[f"L{l}_wmod"]) for l in range(2)])
    for n in "qkvo":
        w["a_w" + n] = km(a["L0_attn_W" + n].T)
    w["a_bo"] = a["L0_attn_bo"]
    w["l_wkva"] = km(a["L0_ffn_Wkva"])
    w["l_wq"] = a["L0_ffn_Wq"].reshape(KC, P, L_PAIRS, P).transpose(2, 1, 0, 3)
    w["l_wq"] = np.concatenate([w["l_wq"], w["l_wq"][0:1], w["l_wq"][0:1]])
    wkp = np.zeros((L_PAIRS, 64, 2, 64), np.float32)
    wkp[:, 0:32, :, 0:32] = a["L0_ffn_Wkvb"].reshape(32, L_PAIRS, 2, 32).transpose(1, 0, 2, 3)
    wkp[:, 32:64, :, 32:64] = np.eye(32, dtype=np.float32)[:, None, :]
    wkp = wkp.reshape(L_PAIRS, 64, P)
    w["l_wkp"] = np.concatenate([wkp, wkp[0:1], wkp[0:1]])
    wo = a["L0_ffn_Wo"].reshape(L_PAIRS, 2, 1, L_D, C)[:, :, :, :NOPE]
    w["l_wo"] = np.broadcast_to(wo, (L_PAIRS, 2, 2, NOPE, C)).reshape(L_PAIRS, P, C).transpose(1, 0, 2)
    w["l_ln1"] = a["L0_ffn_w_ln1"].reshape(KC, P).T
    w["m0_ln"] = a["L0_ffn_w_ln2"].reshape(KC, P).T

    def up(shared, each):
        return np.concatenate([shared, each]).reshape(-1, KC, P, P).transpose(2, 0, 1, 3)

    w["m0_wg"] = up(a["L0_ffn_sWg"], a["L0_ffn_Wg"])
    w["m0_wu"] = up(a["L0_ffn_sWu"], a["L0_ffn_Wu"])
    w["m0_wd"] = np.concatenate([a["L0_ffn_sWd"], a["L0_ffn_Wd"]]).transpose(1, 0, 2)
    w["m0_wr"] = km(a["L0_ffn_Wgate"])
    w["m0_rb"] = a["L0_ffn_expert_bias"]
    for n in "qkv":
        w["r_w" + n] = km(a["L1_attn_w" + n].T)
    two = lambda x: x.reshape(8, 2, C, 64).transpose(0, 2, 1, 3).reshape(8, C, P)
    tiles = lambda x: x.T.reshape(C, 4, P).transpose(1, 0, 2)
    w["m1_wg"] = up(tiles(a["L1_ffn_shared_gate_w"]), two(a["L1_ffn_gate_w"]))
    w["m1_wu"] = up(tiles(a["L1_ffn_shared_up_w"]), two(a["L1_ffn_up_w"]))
    w["m1_wd"] = np.concatenate([a["L1_ffn_shared_down_w"].T.reshape(4, P, C),
                                 a["L1_ffn_down_w"].reshape(8, P, C)]).transpose(1, 0, 2)
    w["m1_wr"] = km(a["L1_ffn_router_w"].T)
    w["m1_rb"] = a["L1_ffn_correction_bias"]
    return {n: np.ascontiguousarray(x) for n, x in w.items()}


def kernel(**inputs):
    import concourse.bacc as bacc
    from concourse.bass_utils import run_bass_kernel_spmd

    nc = bacc.Bacc("TRN2", target_bir_lowering=False, num_devices=1)
    arrays = {n: np.asarray(a) for n, a in inputs.items()}
    w, k = layouts(arrays), tables()
    feed = {}

    def declare(group):
        aps = {}
        for n, a in group.items():
            feed["in_" + n] = a
            aps[n] = nc.dram_tensor("in_" + n, a.shape, F32, kind="ExternalInput").ap()
        return aps

    out = nc.dram_tensor("out", (B, T, C), F32, kind="ExternalOutput").ap()
    build(nc, declare(w), declare(k), out)
    r = run_bass_kernel_spmd(nc, [feed], core_ids=[0])
    return r.results[0]["out"]
```

```python
from contextlib import ExitStack, contextmanager

import numpy as np

import concourse.bass as bass
from concourse import mybir

F32 = mybir.dt.float32
BF16 = mybir.dt.bfloat16
F32R = mybir.dt.float32r
ALU = mybir.AluOpType
ACT = mybir.ActivationFunctionType
AX = mybir.AxisListType

P = 128
B, T, C = 4, 1024, 256
TT = T // P
KC = C // P
HALF = 512
NH = T // HALF
EPS = 1e-5
MASKED = -1e30
SA, CA, GA, SB, CB, GB = range(6)

A_HEADS, WINDOW = 16, 64
A_DH = C // A_HEADS
PAD = WINDOW // 2
NWIN = T // WINDOW
PAIRS = A_HEADS // 2

L_HEADS, L_D, LATENT, ROPE = 16, 64, 32, 32
NOPE = L_D - ROPE
L_PAIRS = L_HEADS // 2

MOE0 = dict(experts=8, shared=1, routed=8)
MOE1 = dict(experts=16, shared=4, routed=8)


class Signal:

    def __init__(self, ctx, nc, name, per, credit=1):
        self.sem = ctx.enter_context(nc.semaphore(name))
        self.per, self.credit = per, credit

    def at(self, turn, n):
        return turn * self.per + (self.credit + n)

    def open(self, engine):
        if self.credit:
            engine.sem_inc(self.sem, self.credit)


def signals(ctx, nc, phase, table):
    return {name: Signal(ctx, nc, f"{phase}_{name}", *((v,) if isinstance(v, int) else v))
            for name, v in table.items()}


@contextmanager
def cleared_after(nc, used):
    yield
    with nc.Block() as block:
        @block.sync
        def _(sp):
            for sem in used:
                sp.sem_clear(sem)


class Semaphores(ExitStack):

    def __init__(self):
        super().__init__()
        self.used = []

    def enter_context(self, semaphore):
        self.used.append(super().enter_context(semaphore))
        return self.used[-1]



LN_SIGNALS = dict(stats=2 * TT, std=1, rstd=1, xn=TT, turned=2 * KC, hT=2 * KC)


def ln_vector(*args, **kwargs):
    for _ in ln_pieces(*args, **kwargs):
        pass


def ln_pieces(v, turn, S, src, st, mv, std, rstd, xn, free, rms=False):
    for t in range(TT):
        v.bn_stats(st[:, t, :], src[:, t, :]).then_inc(S["stats"].sem, 1)
    yield
    v.wait_ge(S["stats"].sem, S["stats"].at(turn, TT))
    v.memset(std[:, 0:1], 0.0)
    for t in range(TT):
        v.bn_aggr(mv[:, t, :], st[:, t, :]).then_inc(S["stats"].sem, 1)
    if rms:
        v.wait_ge(S["stats"].sem, S["stats"].at(turn, 2 * TT))
        v.tensor_tensor(st[:, :, 0], mv[:, :, 0], mv[:, :, 0], ALU.mult).then_inc(S["sq"].sem, 1)
        v.wait_ge(S["sq"].sem, S["sq"].at(turn, 1))
        v.tensor_tensor(mv[:, :, 1], mv[:, :, 1], st[:, :, 0], ALU.add).then_inc(S["sq"].sem, 1)
    yield
    v.wait_ge(S["std"].sem, S["std"].at(turn, 1))
    v.reciprocal(rstd[:, :], std[:, :]).then_inc(S["rstd"].sem, 1)
    v.wait_ge(S["rstd"].sem, S["rstd"].at(turn, 1))
    v.wait_ge(free.sem, free.at(turn, 0))
    for t in range(TT):
        if t == TT // 2:
            yield
        if rms:
            v.tensor_scalar(xn[:, t, :], src[:, t, :], rstd[:, t:t + 1], None, ALU.mult)\
                .then_inc(S["xn"].sem, 1)
        else:
            v.tensor_scalar(xn[:, t, :], src[:, t, :], mv[:, t, 0:1], rstd[:, t:t + 1],
                            ALU.subtract, ALU.mult).then_inc(S["xn"].sem, 1)


def ln_scalar_std(a, turn, S, mv, std, eps, rms=False):
    if rms:
        a.wait_ge(S["sq"].sem, S["sq"].at(turn, 2))
    else:
        a.wait_ge(S["stats"].sem, S["stats"].at(turn, 2 * TT))
    a.activation(std[:, :], mv[:, :, 1], ACT.Sqrt, bias=eps[:, 0:1]).then_inc(S["std"].sem, 1)


def ln_tensor(pe, turn, S, xn, ident, banks):
    for u in range(2 * KC):
        k, half = u // 2, u % 2
        if k == 0:
            pe.wait_ge(S["xn"].sem, S["xn"].at(turn, 4 * half + 4))
        for i in range(4):
            mm = pe.transpose(banks[u][:, i * P:(i + 1) * P],
                              xn[:, 4 * half + i, k * P:(k + 1) * P], ident[:, :])
        mm.then_inc(S["turned"].sem, 1)


def ln_scalar_out(a, turn, S, hT, off, banks, scale, shift):
    for u in range(2 * KC):
        k, half = u // 2, u % 2
        a.wait_ge(S["turned"].sem, S["turned"].at(turn, u + 1))
        out = hT[:, k, off + half * HALF:off + (half + 1) * HALF]
        if shift is None:
            a.activation(out, banks[u][:, :], ACT.Copy, scale=scale(k)).then_inc(S["hT"].sem, 1)
        else:
            a.activation(out, banks[u][:, :], ACT.Identity, scale=scale(k), bias=shift(k))\
                .then_inc(S["hT"].sem, 1)



def attention_signals(J):
    return dict(score=J, negmax=J, exp=J, turnedP=(J, 2), evac=J, evac2=(J // 2, 1),
                pv=(J, 2), recip=J, norm=(J, 2))


def keys(j):
    return (j % TT + 1) * P


def att_tensor(pe, turn, S, J, q_of, k_of, v_of, W, vcols, ident, identb, causal, S2, TR, O, Pt, PT):
    def score(j):
        n, qt = keys(j), j % TT
        if j >= 2:
            pe.wait_ge(S["exp"].sem, S["exp"].at(turn, j - 1))
        for n0 in range(0, n, HALF):
            n1 = min(n, n0 + HALF)
            diagonal = n1 == n
            if diagonal:
                pe.matmul(S2[j % 2][:, n - P:n], identb[:, :], causal[:, :], start=True, stop=False,
                          skip_group_check=True)
            for k in range(W):
                mm = pe.matmul(S2[j % 2][:, n0:n1], q_of(j, k, qt), k_of(j, k, n0, n1),
                               start=(k == 0 and not diagonal), stop=(k == W - 1),
                               skip_group_check=diagonal)
        mm.then_inc(S["score"].sem, 1)

    def second(j):
        return j // TT * (TT // 2) + max(0, j % TT - TT // 2 + 1)

    def turn_p(j):
        n = keys(j)
        pe.wait_ge(S["exp"].sem, S["exp"].at(turn, j + 1))
        if j >= 1:
            pe.wait_ge(S["evac"].sem, S["evac"].at(turn, j))
            if second(j - 1):
                pe.wait_ge(S["evac2"].sem, S["evac2"].at(turn, second(j - 1)))
        for i in range(n // P):
            mm = pe.transpose(TR[i // 4][:, (i % 4) * P:(i % 4 + 1) * P],
                              Pt[:, j % 2, i * P:(i + 1) * P], ident[:, :])
        mm.then_inc(S["turnedP"].sem, 1)

    def pv(j):
        n = keys(j)
        pe.wait_ge(S["evac"].sem, S["evac"].at(turn, j + 1))
        if n > HALF:
            pe.wait_ge(S["evac2"].sem, S["evac2"].at(turn, second(j)))
        pe.wait_ge(S["norm"].sem, S["norm"].at(turn, j - 1))
        for i in range(n // P):
            mm = pe.matmul(O[j % 2][:, 0:vcols], PT[:, j % 2, i, :], v_of(j, i),
                           start=(i == 0), stop=(i == n // P - 1))
        mm.then_inc(S["pv"].sem, 1)

    score(0)
    score(1)
    for j in range(J):
        turn_p(j)
        if j + 2 < J:
            score(j + 2)
        if j >= 1:
            pv(j - 1)
    pv(J - 1)


def att_scalar(a, turn, S, J, S2, TR, Pt, PT, negmax, sums):
    def exp(j):
        n = keys(j)
        a.wait_ge(S["negmax"].sem, S["negmax"].at(turn, j + 1))
        a.wait_ge(S["turnedP"].sem, S["turnedP"].at(turn, j - 1))
        a.activation(Pt[:, j % 2, 0:n], S2[j % 2][:, 0:n], ACT.Exp, bias=negmax[:, j:j + 1],
                     accum_out=sums[:, j:j + 1]).then_inc(S["exp"].sem, 1)

    def evac(j):
        n = min(keys(j), HALF)
        a.wait_ge(S["turnedP"].sem, S["turnedP"].at(turn, j + 1))
        a.wait_ge(S["pv"].sem, S["pv"].at(turn, j - 1))
        a.activation(PT[:, j % 2, 0:n // P, :], TR[0][:, 0:n].rearrange("p (i q) -> p i q", q=P),
                     ACT.Copy).then_inc(S["evac"].sem, 1)

    a.wait_ge(S["norm"].sem, S["norm"].at(turn, 0))
    exp(0)
    for j in range(J):
        evac(j)
        if j + 1 < J:
            exp(j + 1)


def att_vector(v, turn, S, J, S2, TR, PT, O, negmax, sums, rs, vcols, y_of):
    def rowmax(j):
        v.wait_ge(S["score"].sem, S["score"].at(turn, j + 1))
        v.tensor_reduce(negmax[:, j:j + 1], S2[j % 2][:, 0:keys(j)], AX.X, ALU.max, negate=True)\
            .then_inc(S["negmax"].sem, 1)

    def evac2(j):
        n = keys(j)
        if n > HALF:
            v.wait_ge(S["turnedP"].sem, S["turnedP"].at(turn, j + 1))
            v.wait_ge(S["pv"].sem, S["pv"].at(turn, j - 1))
            v.tensor_copy(PT[:, j % 2, 4:n // P, :],
                          TR[1][:, 0:n - HALF].rearrange("p (i q) -> p i q", q=P))\
                .then_inc(S["evac2"].sem, 1)

    def norm(j):
        v.wait_ge(S["exp"].sem, S["exp"].at(turn, j + 1))
        v.reciprocal(rs[:, j:j + 1], sums[:, j:j + 1]).then_inc(S["recip"].sem, 1)
        v.wait_ge(S["recip"].sem, S["recip"].at(turn, j + 1))
        v.wait_ge(S["pv"].sem, S["pv"].at(turn, j + 1))
        v.tensor_scalar(y_of(j), O[j % 2][:, 0:vcols], rs[:, j:j + 1], None, ALU.mult)\
            .then_inc(S["norm"].sem, 1)

    rowmax(0)
    rowmax(1)
    for j in range(J):
        evac2(j)
        if j + 2 < J:
            rowmax(j + 2)
        if j >= 1:
            norm(j - 1)
    norm(J - 1)


def modulation(nc, cT, wmod, x, MODT, ROWSd, X, U):
    rows = [(0, GA), (0, GB), (0, CB), (0, SB), (1, GA), (1, GB)]
    with ExitStack() as sems, ExitStack() as ctx:
        c_sb = ctx.enter_context(nc.sbuf_tensor("m_c", [P, 2, KC, B], F32))
        sc = ctx.enter_context(nc.sbuf_tensor("m_silu", [P, 2, KC, B], F32))
        wm = ctx.enter_context(nc.sbuf_tensor("m_w", [P, 2, KC, 6 * C], F32))
        scb = ctx.enter_context(nc.sbuf_tensor("m_silub", [P, 2, KC, B, P], F32))
        ROWS = ctx.enter_context(nc.sbuf_tensor("m_rows", [P, len(rows), B, C], F32))
        sign = ctx.enter_context(nc.sbuf_tensor("m_sign", [P, 4 * B * C], F32))
        mag = ctx.enter_context(nc.sbuf_tensor("m_mag", [P, 4 * B * C], F32))
        banks = [ctx.enter_context(nc.psum_tensor(f"m_ps{i}", [P, HALF], F32)) for i in range(4)]
        loaded = sems.enter_context(nc.semaphore("m_loaded"))
        silu = sems.enter_context(nc.semaphore("m_silu_ready"))
        spread = sems.enter_context(nc.semaphore("m_spread"))
        product = sems.enter_context(nc.semaphore("m_product"))
        copied = sems.enter_context(nc.semaphore("m_copied"))
        chain = sems.enter_context(nc.semaphore("m_chain"))
        stored = sems.enter_context(nc.semaphore("m_stored"))
        used = (loaded, silu, spread, product, copied, chain, stored)
        ctx.enter_context(cleared_after(nc, used))
        block = ctx.enter_context(nc.Block())
        njobs = 2 + len(rows) * 2

        @block.sync
        def _(sp):
            for l in range(2):
                sp.dma_start(c_sb[:, l], cT[l]).then_inc(loaded, 16)
                sp.dma_start(wm[:, l], wmod[l]).then_inc(loaded, 16)
            for behind in (X, U):
                sp.dma_start(behind[:, B * TT:, :], x[0].rearrange("(t p) c -> p t c", p=P))\
                    .then_inc(stored, 16)
            sp.wait_ge(chain, 13)
            sp.dma_start(ROWSd[:, :, 0:B, :], ROWS[:, :, :, :]).then_inc(stored, 16)
            sp.dma_start(ROWSd[:, :, B, :], ROWS[:, :, 0, :]).then_inc(stored, 16)
            sp.wait_ge(stored, 64)

        @block.scalar
        def _(a):
            a.wait_ge(loaded, 64)
            a.activation(sc[:, :, :, :], c_sb[:, :, :, :], ACT.Silu).then_inc(silu, 1)

        @block.tensor
        def _(pe):
            pe.wait_ge(silu, 1)
            for l in range(2):
                for j in (range(4), (0, 1, 2, 3, 6, 7, 8, 9))[l]:
                    for k in range(KC):
                        mm = pe.matmul(banks[l][:, j * B:(j + 1) * B], wm[:, l, k, j * P:(j + 1) * P],
                                       sc[:, l, k, :], start=(k == 0), stop=(k == KC - 1))
                mm.then_inc(product, 1)
            pe.wait_ge(spread, 1)
            for n in range(len(rows) * 2):
                l, r = rows[n // 2]
                pe.wait_ge(copied, n + 1)
                for i in range(2):
                    b = 2 * (n % 2) + i
                    for k in range(KC):
                        mm = pe.matmul(banks[2 + n % 2][:, i * C:(i + 1) * C], scb[:, l, k, b, :],
                                       wm[:, l, k, r * C:(r + 1) * C], start=(k == 0), stop=(k == KC - 1))
                mm.then_inc(product, 1)

        @block.vector
        def _(v):
            v.wait_ge(silu, 1)
            v.tensor_copy(scb[:, :, :, :, :].rearrange("p l k b m -> p (l k b) m"),
                          sc[:, :, :, :].rearrange("p l k b -> p (l k b)")[:, :, None]
                          .broadcast_to([P, 2 * KC * B, P])).then_inc(spread, 1)
            for l in range(2):
                v.wait_ge(product, l + 1)
                for j in ((0,), (0, 6))[l]:
                    copy = v.tensor_copy(MODT[:, l, 0:B, j:j + 4],
                                       banks[l][:, j * B:(j + 4) * B].rearrange("p (j b) -> p b j", b=B))
                copy.then_inc(copied, 1)
            for n in range(len(rows) * 2):
                r, half = n // 2, n % 2
                v.wait_ge(product, n + 3)
                v.tensor_copy(ROWS[:, r, 2 * half:2 * half + 2, :],
                              banks[2 + n % 2][:, :].rearrange("p (b c) -> p b c", b=2)).then_inc(copied, 1)
            v.wait_ge(copied, njobs)
            for n, j in enumerate((CA, CB)):
                v.tensor_scalar(MODT[:, :, 0:B, 2 * j:2 * j + 2], MODT[:, :, 0:B, 2 * j:2 * j + 2], 1.0,
                                None, ALU.add).then_inc(chain, 1)
            v.tensor_scalar(ROWS[:, 2], ROWS[:, 2], 1.0, None, ALU.add).then_inc(chain, 1)
            at = 3
            for lo in (0, 4):
                n = 2 * B * C
                g = ROWS[:, lo:lo + 2].rearrange("p r b c -> p (r b c)")
                if at > 3:
                    v.wait_ge(chain, at)
                v.tensor_scalar(sign[:, 0:n], g, 0.0, 2.0, ALU.is_ge, ALU.mult).then_inc(chain, 1)
                v.tensor_scalar(mag[:, 0:n], g, -1.0, None, ALU.mult).then_inc(chain, 1)
                v.wait_ge(chain, at + 2)
                v.tensor_tensor(mag[:, 0:n], mag[:, 0:n], g, ALU.max).then_inc(chain, 1)
                v.wait_ge(chain, at + 3)
                v.tensor_scalar(mag[:, 0:n], mag[:, 0:n], 0.25, None, ALU.max).then_inc(chain, 1)
                v.wait_ge(chain, at + 4)
                v.scalar_tensor_tensor(g, sign[:, 0:n], -1.0, mag[:, 0:n], ALU.add, ALU.mult)\
                    .then_inc(chain, 1)
                at += 5


def windowed_attention(nc, sems, X, MODT, ROWS, ident, identb, eps, W, K):
    with ExitStack() as ctx:
        def sb(name, shape, dt=F32):
            return ctx.enter_context(nc.sbuf_tensor("w_" + name, shape, dt))

        wq, wk, wv, wo = (sb(n, [P, KC, C]) for n in ("wq", "wk", "wv", "wo"))
        bo = sb("bo", [P, C])
        band = sb("band", [P, P])
        bandb = sb("bandb", [P, P], BF16)
        hmask = sb("hmask", [P, A_HEADS])
        own = sb("own", [P, 2])
        sel = sb("sel", [P, WINDOW])
        xb = sb("xb", [P, TT, C])
        mod = sb("mod", [P, 12])
        gate = sb("gate", [P, C])
        xn = sb("xn", [P, TT, C])
        st, mv = sb("st", [P, TT, 6]), sb("mv", [P, TT, 2])
        std, rstd = sb("std", [P, TT]), sb("rstd", [P, TT])
        hT = sb("hT", [P, KC, T + 2 * PAD])
        qT = sb("qT", [P, KC, T])
        kT = sb("kT", [P, KC, T + 2 * PAD])
        qm = sb("qm", [P, NWIN, A_HEADS, WINDOW])
        V = sb("V", [P, NWIN, PAIRS, 34])
        D = qT
        PTs = sb("PT", [P, 2, PAIRS * P])
        m = sb("m", [P, 2, PAIRS])
        r = sb("r", [P, 2, PAIRS])
        rm = sb("rm", [P, 2, PAIRS, 2])
        Yn = sb("Yn", [P, 2, PAIRS, 2, A_DH])
        yT = xn[:, :, :].rearrange("p t c -> p (t c)").rearrange("p (k t) -> p k t", k=KC)
        tmp = sb("tmp", [P, 2, C])
        banks = [ctx.enter_context(nc.psum_tensor(f"w_ps{i}", [P, HALF], F32)) for i in range(8)]
        S = signals(sems, nc, "w", dict(LN_SIGNALS) | dict(
            qk=8, qkout=8, qm=A_HEADS, vproj=8, vout=8, score=2 * NWIN, max=2 * NWIN,
            sub=2 * NWIN, exp=NWIN, turnedP=(2 * NWIN, 3), ptout=2 * NWIN, pv=(NWIN, 2),
            recip=2 * NWIN, yn=NWIN, ymm=(NWIN, 2), yout=NWIN, proj=TT, biased=TT,
            mul=TT, added=(TT, 2)))
        wload = sems.enter_context(nc.semaphore("w_wload"))
        consts = sems.enter_context(nc.semaphore("w_consts"))
        xload = sems.enter_context(nc.semaphore("w_xload"))
        xstore = sems.enter_context(nc.semaphore("w_xstore"))
        block = ctx.enter_context(nc.Block())

        @block.sync
        def _(sp):
            for dst, src in ((wq, W["a_wq"]), (wk, W["a_wk"]), (wv, W["a_wv"]), (wo, W["a_wo"])):
                sp.dma_start(dst[:, :, :], src).then_inc(wload, 16)
            sp.dma_start(bo[:, :], W["a_bo"].partition_broadcast(P)).then_inc(wload, 16)
            for dst, src in ((band, K["band"]), (hmask, K["hmask"]), (own, K["own"]), (sel, K["sel64"])):
                sp.dma_start(dst[:, :], src).then_inc(wload, 16)
            with sp.Fori(0, B) as b:
                sp.wait_ge(S["added"].sem, S["added"].at(b, 0))
                sp.wait_ge(xstore, b * 16 + 1)
                sp.dma_start(xb[:, :, :], W["x"][bass.ds(b, 1)].rearrange("b (t p) c -> p (b t) c", p=P))\
                    .then_inc(xload, 16)
                sp.dma_start(mod[:, :], MODT[:, 0, bass.ds(b, 1), :]).then_inc(xload, 16)
                sp.dma_start(gate[:, :], ROWS[:, 0, bass.ds(b, 1), :]).then_inc(xload, 16)
                sp.wait_ge(S["added"].sem, S["added"].at(b, TT))
                sp.dma_start(X[:, bass.ds(b * TT, TT), :], xb[:, :, :]).then_inc(xstore, 16)
            sp.wait_ge(xstore, B * 16 + 1)

        @block.vector
        def _(v):
            for name in ("stats", "rstd", "xn", "qm", "max", "sub", "recip", "yn", "yout", "biased"):
                S[name].open(v)
            v.wait_ge(wload, 9 * 16)
            v.tensor_copy(bandb[:, :], band[:, :]).then_inc(consts, 1)
            for buf in (hT, kT):
                v.memset(buf[:, :, 0:PAD], 0.0).then_inc(consts, 1)
                v.memset(buf[:, :, PAD + T:], 0.0).then_inc(consts, 1)
            v.memset(V[:, :, :, 32:34], 1.0).then_inc(consts, 1)
            with v.Fori(0, B) as b:
                v.wait_ge(xload, b * 48 + 48)
                ln_vector(v, b, S, xb, st, mv, std, rstd, xn, S["turned"])
                for n in range(KC):
                    v.wait_ge(S["qkout"].sem, S["qkout"].at(b, 2 * n + 2))
                    for h in range(n * A_HEADS // KC, (n + 1) * A_HEADS // KC):
                        v.tensor_scalar(qm[:, :, h, :], qT[:, n, :].rearrange("p (w q) -> p w q", q=WINDOW),
                                        hmask[:, h:h + 1], None, ALU.mult)\
                            .then_inc(S["qm"].sem, 1)

                def softmax(w):
                    for g in range(2):
                        u = 2 * w + g
                        v.wait_ge(S["score"].sem, S["score"].at(b, u + 1))
                        s3 = banks[2 * (w % 2) + g][:, :].rearrange("p (n k) -> p n k", k=P)
                        mx = m[:, w % 2, 4 * g:4 * g + 4]
                        v.tensor_reduce(mx, s3, AX.X, ALU.max).then_inc(S["max"].sem, 1)
                        v.wait_ge(S["max"].sem, S["max"].at(b, u + 1))
                        v.wait_ge(S["turnedP"].sem, S["turnedP"].at(b, 2 * w - 2))
                        v.tensor_tensor(
                            D[:, w % 2, g * HALF:(g + 1) * HALF].rearrange("p (n k) -> p n k", k=P),
                            s3, mx[:, :, None].broadcast_to([P, 4, P]), ALU.subtract)\
                            .then_inc(S["sub"].sem, 1)

                def weigh(w):
                    o3 = banks[6][:, 0:PAIRS * 34].rearrange("p (n d) -> p n d", d=34)
                    v.wait_ge(S["pv"].sem, S["pv"].at(b, w + 1))
                    v.reciprocal(r[:, w % 2, :], o3[:, :, 32]).then_inc(S["recip"].sem, 1)
                    v.wait_ge(S["recip"].sem, S["recip"].at(b, 2 * w + 1))
                    v.tensor_tensor(rm[:, w % 2], r[:, w % 2, :, None].broadcast_to([P, PAIRS, 2]),
                                    own[:, None, :].broadcast_to([P, PAIRS, 2]), ALU.mult)\
                        .then_inc(S["recip"].sem, 1)
                    v.wait_ge(S["recip"].sem, S["recip"].at(b, 2 * w + 2))
                    v.wait_ge(S["ymm"].sem, S["ymm"].at(b, w - 1))
                    v.tensor_tensor(
                        Yn[:, w % 2], o3[:, :, 0:32].rearrange("p n (h d) -> p n h d", h=2),
                        rm[:, w % 2, :, :, None].broadcast_to([P, PAIRS, 2, A_DH]), ALU.mult)\
                        .then_inc(S["yn"].sem, 1)

                def y_out(w):
                    v.wait_ge(S["ymm"].sem, S["ymm"].at(b, w + 1))
                    v.tensor_copy(yT[:, :, w * WINDOW:(w + 1) * WINDOW],
                                  banks[7][:, 0:KC * WINDOW].rearrange("p (k q) -> p k q", k=KC))\
                        .then_inc(S["yout"].sem, 1)

                softmax(0)
                softmax(1)
                for w in range(NWIN + 2):
                    if w + 2 < NWIN:
                        softmax(w + 2)
                    if 1 <= w <= NWIN:
                        weigh(w - 1)
                    if w >= 2:
                        y_out(w - 2)
                for t in range(TT):
                    v.wait_ge(S["proj"].sem, S["proj"].at(b, t + 1))
                    v.wait_ge(S["added"].sem, S["added"].at(b, t - 1))
                    v.tensor_tensor(tmp[:, t % 2, :], banks[t % 2][:, 0:C], bo[:, :], ALU.add)\
                        .then_inc(S["biased"].sem, 1)

        @block.gpsimd
        def _(g):
            for name in ("mul", "added"):
                S[name].open(g)
            g.sem_inc(xstore, 1)
            with g.Fori(0, B) as b:
                for t in range(TT):
                    g.wait_ge(S["biased"].sem, S["biased"].at(b, t + 1))
                    g.tensor_tensor(tmp[:, t % 2, :], tmp[:, t % 2, :], gate[:, :], ALU.mult)\
                        .then_inc(S["mul"].sem, 1)
                    g.wait_ge(S["mul"].sem, S["mul"].at(b, t + 1))
                    g.tensor_tensor(xb[:, t, :], xb[:, t, :], tmp[:, t % 2, :], ALU.add)\
                        .then_inc(S["added"].sem, 1)

        @block.scalar
        def _(a):
            for name in ("std", "hT", "qkout", "vout", "exp", "ptout"):
                S[name].open(a)
            a.wait_ge(consts, 6)
            with a.Fori(0, B) as b:
                ln_scalar_std(a, b, S, mv, std, eps)
                ln_scalar_out(a, b, S, hT, PAD, banks, lambda k: mod[:, 2 * CA + k:2 * CA + k + 1],
                              lambda k: mod[:, 2 * SA + k:2 * SA + k + 1])
                for u in range(8):
                    et, half = (u % 4) // 2, u % 2
                    dst = qT[:, et, half * HALF:(half + 1) * HALF] if u < 4 else \
                        kT[:, et, PAD + half * HALF:PAD + (half + 1) * HALF]
                    a.wait_ge(S["qk"].sem, S["qk"].at(b, u + 1))
                    a.activation(dst, banks[u][:, :], ACT.Copy).then_inc(S["qkout"].sem, 1)
                for u in range(NWIN // 2):
                    a.wait_ge(S["vproj"].sem, S["vproj"].at(b, u + 1))
                    a.activation(V[:, 2 * u:2 * u + 2, :, 0:32],
                                 banks[u][:, :].rearrange("p (w n d) -> p w n d", w=2, d=32), ACT.Copy)\
                        .then_inc(S["vout"].sem, 1)

                def exp(w):
                    a.wait_ge(S["sub"].sem, S["sub"].at(b, 2 * w + 2))
                    a.activation(D[:, w % 2, :], D[:, w % 2, :], ACT.Exp, scale=A_DH ** -0.5)\
                        .then_inc(S["exp"].sem, 1)

                exp(0)
                for w in range(NWIN):
                    for g in range(2):
                        a.wait_ge(S["turnedP"].sem, S["turnedP"].at(b, 2 * w + g + 1))
                        if g == 0:
                            a.wait_ge(S["pv"].sem, S["pv"].at(b, w - 1))
                        a.activation(PTs[:, w % 2, g * HALF:(g + 1) * HALF], banks[4 + g][:, :], ACT.Copy)\
                            .then_inc(S["ptout"].sem, 1)
                    if w + 1 < NWIN:
                        exp(w + 1)

        @block.tensor
        def _(pe):
            for name in ("turned", "qk", "vproj", "score", "turnedP", "pv", "ymm", "proj"):
                S[name].open(pe)
            pe.wait_ge(consts, 6)
            with pe.Fori(0, B) as b:
                pe.wait_ge(S["biased"].sem, S["biased"].at(b, 0))
                ln_tensor(pe, b, S, xn, ident, banks)
                pe.wait_ge(S["hT"].sem, S["hT"].at(b, 2 * KC))
                for u in range(8):
                    w, et, half = (wq, wk)[u // 4], (u % 4) // 2, u % 2
                    for k in range(KC):
                        mm = pe.matmul(banks[u][:, :], w[:, k, et * P:(et + 1) * P],
                                       hT[:, k, PAD + half * HALF:PAD + (half + 1) * HALF],
                                       start=(k == 0), stop=(k == KC - 1))
                    mm.then_inc(S["qk"].sem, 1)
                for u in range(NWIN // 2):
                    pe.wait_ge(S["qkout"].sem, S["qkout"].at(b, u + 1))
                    for i in range(2):
                        w0 = (2 * u + i) * WINDOW
                        for k in range(KC):
                            mm = pe.matmul(banks[u][:, i * C:(i + 1) * C], hT[:, k, w0:w0 + P],
                                           wv[:, k, :], start=(k == 0), stop=(k == KC - 1))
                    mm.then_inc(S["vproj"].sem, 1)

                def score(w):
                    if w >= 2:
                        pe.wait_ge(S["sub"].sem, S["sub"].at(b, 2 * w - 2))
                    for g in range(2):
                        bank = banks[2 * (w % 2) + g]
                        pe.matmul(bank[:, :].rearrange("p (n k) -> p n k", k=P), identb[:, :],
                                  bandb[:, None, :].broadcast_to([P, 4, P]), start=True, stop=False,
                                  skip_group_check=True)
                        for i in range(4):
                            h = 2 * (4 * g + i)
                            mm = pe.matmul(bank[:, i * P:(i + 1) * P],
                                           qm[:, w, h:h + 2, :].rearrange("p h q -> p (h q)"),
                                           kT[:, g, w * WINDOW:w * WINDOW + P],
                                           start=False, stop=(i == 3), skip_group_check=True)
                        mm.then_inc(S["score"].sem, 1)

                def turn_p(w):
                    pe.wait_ge(S["exp"].sem, S["exp"].at(b, w + 1))
                    for g in range(2):
                        if w >= 1:
                            pe.wait_ge(S["ptout"].sem, S["ptout"].at(b, 2 * w - 1 + g))
                        for i in range(4):
                            n = 4 * g + i
                            mm = pe.transpose(banks[4 + g][:, i * P:(i + 1) * P],
                                              D[:, w % 2, n * P:(n + 1) * P], ident[:, :])
                        mm.then_inc(S["turnedP"].sem, 1)

                def pv(w):
                    pe.wait_ge(S["ptout"].sem, S["ptout"].at(b, 2 * w + 2))
                    if w >= 1:
                        pe.wait_ge(S["yn"].sem, S["yn"].at(b, w))
                    for n in range(PAIRS):
                        mm = pe.matmul(banks[6][:, n * 34:(n + 1) * 34], PTs[:, w % 2, n * P:(n + 1) * P],
                                       V[:, w, n, :], start=True, stop=True)
                    mm.then_inc(S["pv"].sem, 1)

                def y_mm(w):
                    pe.wait_ge(S["yn"].sem, S["yn"].at(b, w + 1))
                    if w >= 1:
                        pe.wait_ge(S["yout"].sem, S["yout"].at(b, w))
                    for k in range(KC):
                        mm = pe.matmul(banks[7][:, k * WINDOW:(k + 1) * WINDOW],
                                       Yn[:, w % 2, 4 * k:4 * k + 4].rearrange("p n h d -> p (n h d)"),
                                       sel[:, :], start=True, stop=True)
                    mm.then_inc(S["ymm"].sem, 1)

                pe.wait_ge(S["qm"].sem, S["qm"].at(b, A_HEADS))
                pe.wait_ge(S["qkout"].sem, S["qkout"].at(b, 8))
                pe.wait_ge(S["vout"].sem, S["vout"].at(b, 8))
                score(0)
                score(1)
                for w in range(NWIN + 2):
                    if w < NWIN:
                        turn_p(w)
                    if w + 2 < NWIN:
                        score(w + 2)
                    if 1 <= w <= NWIN:
                        pv(w - 1)
                    if w >= 2:
                        y_mm(w - 2)
                pe.wait_ge(S["yout"].sem, S["yout"].at(b, NWIN))
                for t in range(TT):
                    if t >= 2:
                        pe.wait_ge(S["biased"].sem, S["biased"].at(b, t - 1))
                    for k in range(KC):
                        mm = pe.matmul(banks[t % 2][:, 0:C], yT[:, k, t * P:(t + 1) * P], wo[:, k, :],
                                       start=(k == 0), stop=(k == KC - 1))
                    mm.then_inc(S["proj"].sem, 1)



class LatentJobs:
    J = 4 * TT
    SETS = L_PAIRS + 1
    K0, K1, Q0, Q1, VAL = range(5)
    PE_AT = {1: K0, 3: K1, 5: Q0, 8: Q1, 10: VAL}
    HI_AT = {1: K0, 3: K1, 7: Q0, 11: Q1, 12: VAL}
    QLO_AT = {7: 0, 12: 1}
    FREE_AT = {1: K0, 3: K1, 5: Q0, 8: Q1, 12: VAL}

    def __init__(self):
        self.units, self.before = [], []
        for j in range(self.J):
            self.before.append(len(self.units))
            n = self.qt(j) + 1
            self.units.append((j, 0, min(n, 4)))
            if n > 4:
                self.units.append((j, 4, n - 4))
        self.NU = len(self.units)

    def pair(self, j):
        return j // 16

    def head(self, j):
        return j // 2 % 2

    def qt(self, j):
        return 2 * (j % 16 // 4) + j % 2

    def n(self, j):
        return (self.qt(j) + 1) * P

    def of(self, j):
        end = self.before[j + 1] if j + 1 < self.J else self.NU
        return range(self.before[j], end)


def latent_attention(nc, sems, X, Ud, ROWSd, ident, identb, causal, eps, W, K):
    L = LatentJobs()
    J, NU, SETS = L.J, L.NU, L.SETS
    NQ = L_PAIRS // 2
    with ExitStack() as ctx:
        def sb(name, shape, dt=F32):
            return ctx.enter_context(nc.sbuf_tensor("l_" + name, shape, dt))

        wkva, wo = sb("wkva", [P, KC, 64]), sb("wo", [P, L_PAIRS, C])
        wq, wkp = sb("wq", [P, KC, P]), sb("wkp", [64, P])
        w_ln = sb("w_ln", [P, KC])
        cos, sin = sb("cos", [P, T]), sb("sin", [P, T])
        xn, ub = sb("xn", [P, TT, C]), sb("ub", [P, TT, C])
        cb, sbias = sb("cb", [P, C]), sb("sb", [P, C])
        st, mv = sb("st", [P, TT, 6]), sb("mv", [P, TT, 2])
        std, rstd = sb("std", [P, TT]), sb("rstd", [P, TT])
        rT = sb("rT", [P, KC, T])
        kvr = sb("kvr", [64, T])
        rot, shuf = sb("rot", [P, HALF]), sb("shuf", [P, HALF])
        qhi, qlo = sb("qhi", [P, 2, T], F32R), sb("qlo", [P, 2, T], F32R)
        khi, klo = sb("khi", [P, 2, T], F32R), sb("klo", [P, 2, T], F32R)
        val = sb("val", [P, 2, TT, 192], F32R)
        Pt = sb("Pt", [P, 2, T])
        PThi, PTlo = sb("PThi", [P, 2, TT, 2 * P], F32R), sb("PTlo", [P, 2, TT, 2 * P], F32R)
        negmax, sums = sb("negmax", [P, J]), sb("sums", [P, J])
        allsums, tile_of = sb("allsums", [P, P]), sb("tile_of", [P, TT])
        placed = Pt[:, 0, :].rearrange("p (t q) -> p t q", q=P)
        heads = sb("heads", [P, L_PAIRS, P])
        YT = sb("YT", [P, L_PAIRS, T])
        xb = YT[:, 6:8, :].rearrange("p n (t c) -> p (n t) c", c=C)
        S2 = [ctx.enter_context(nc.psum_tensor(f"l_s{i}", [P, 2 * HALF], F32)) for i in range(2)]
        TR = [ctx.enter_context(nc.psum_tensor(f"l_t{i}", [P, HALF], F32)) for i in range(2)]
        O = ctx.enter_context(nc.psum_tensor("l_o", [P, HALF], F32))
        PJ = ctx.enter_context(nc.psum_tensor("l_pj", [P, HALF], F32))
        pbanks = [S2[0][:, 0:HALF], S2[0][:, HALF:], S2[1][:, 0:HALF], S2[1][:, HALF:]]
        N1 = signals(sems, nc, "l_n1", dict(stats=2 * TT, std=1, rstd=1, xn=TT))
        S = signals(sems, nc, "l", dict(LN_SIGNALS) | dict(
            sq=2, scaled=TT, u=TT, ckv=1, shufk=1, ropek=3, proj=TT, added=TT,
            pj=5 * SETS, hi=5 * SETS, free=5 * SETS, cosq=2 * SETS, sinq=2 * SETS, ropeq=2 * SETS,
            qlo=2 * SETS, recip=1, sumsT=1, placed=1, spread=NH * L_PAIRS, divided=NH * L_PAIRS))
        A = signals(sems, nc, "la", dict(
            score=J, negmax=J, exp=J, turnedP=(NU, 2), pthi=NU, ptlo=(NU, 2),
            pv=(J // 2, 2), yout=J // 4, kept=1))
        wload = sems.enter_context(nc.semaphore("l_wload"))
        pload = sems.enter_context(nc.semaphore("l_pload"))
        xload = sems.enter_context(nc.semaphore("l_xload"))
        ustore = sems.enter_context(nc.semaphore("l_ustore"))
        consts = sems.enter_context(nc.semaphore("l_consts"))
        block = ctx.enter_context(nc.Block())

        @block.sync
        def _(sp):
            for dst, src in ((wkva, W["l_wkva"]), (wo, W["l_wo"])):
                sp.dma_start(dst[:, :, :], src).then_inc(wload, 16)
            for dst, src in ((w_ln, W["l_ln1"]), (cos, K["lcos"]), (sin, K["lsin"]),
                             (tile_of, K["l_tile"])):
                sp.dma_start(dst[:, :], src).then_inc(wload, 16)
            sp.dma_start(heads[:, :, :], K["l_heads"]).then_inc(wload, 16)
            sp.dma_start(wq[:, :, :], W["l_wq"][0:1]).then_inc(pload, 16)
            sp.dma_start(wkp[:, :], W["l_wkp"][0:1]).then_inc(pload, 16)
            with sp.Fori(0, B) as b:
                sp.wait_ge(S["proj"].sem, S["proj"].at(b, 0))
                sp.dma_start(xb, X[:, bass.ds(b * TT, TT), :]).then_inc(xload, 16)
                sp.dma_start(cb[:, :], ROWSd[:, 2, bass.ds(b, 1), :]).then_inc(xload, 16)
                sp.dma_start(sbias[:, :], ROWSd[:, 3, bass.ds(b, 1), :]).then_inc(xload, 16)
            sp.wait_ge(ustore, B * 16 + 1)
            sp.wait_ge(pload, (B * SETS + 1) * 32)

        @block.vector
        def _(v):
            for sig in (N1["stats"], N1["rstd"], N1["xn"]):
                sig.open(v)
            for name in ("stats", "sq", "rstd", "xn", "shufk", "ropek", "added", "free", "cosq", "qlo",
                         "recip", "placed", "divided"):
                S[name].open(v)
            for name in ("negmax", "ptlo", "kept"):
                A[name].open(v)
            v.memset(val[:, :, :, :].bitcast(F32), 0.0).then_inc(consts, 1)
            v.wait_ge(wload, 7 * 16)
            v.wait_ge(consts, 1)
            swap = [i ^ 1 for i in range(32)]

            def project(b, s, par, unit):
                v.wait_ge(S["pj"].sem, S["pj"].at(b, s * 5 + unit + 1))
                if unit in (L.K0, L.K1):
                    cols = slice((unit - L.K0) * HALF, (unit - L.K0 + 1) * HALF)
                    v.wait_ge(S["hi"].sem, S["hi"].at(b, s * 5 + unit + 1))
                    v.scalar_tensor_tensor(klo[:, par, cols], PJ[:, :], L_D ** -0.5,
                                           khi[:, par, cols].bitcast(F32), ALU.mult, ALU.subtract)\
                        .then_inc(S["free"].sem, 1)
                elif unit in (L.Q0, L.Q1):
                    h = unit - L.Q0
                    v.wait_ge(S["qlo"].sem, S["qlo"].at(b, s * 2 + h))
                    v.tensor_tensor(rot[:, :], PJ[:, :], cos[:, h * HALF:(h + 1) * HALF], ALU.mult)\
                        .then_inc(S["cosq"].sem, 1)
                    v.stream_shuffle(shuf[:, :], PJ[:, :], swap).then_inc(S["free"].sem, 1)
                else:
                    v.wait_ge(S["hi"].sem, S["hi"].at(b, s * 5 + unit + 1))
                    pj4 = PJ[:, :].rearrange("p (t h d) -> p t h d", h=2, d=NOPE)
                    v.tensor_tensor(hi_lo(par, 1), pj4, hi_lo(par, 0).bitcast(F32), ALU.subtract)\
                        .then_inc(S["free"].sem, 1)

            def hi_lo(par, part):
                return val[:, par].rearrange("p t (a n d) -> p t a n d", a=3, n=2)[:, :, 0:3:2, part, :]

            def qlow(b, s, par, h):
                v.wait_ge(S["hi"].sem, S["hi"].at(b, s * 5 + L.Q0 + h + 1))
                cols = slice(h * HALF, (h + 1) * HALF)
                v.tensor_tensor(qlo[:, par, cols], rot[:, :], qhi[:, par, cols].bitcast(F32),
                                ALU.subtract).then_inc(S["qlo"].sem, 1)

            with v.Fori(0, B) as b:
                v.wait_ge(xload, b * 48 + 48)
                ln_vector(v, b, N1, xb, st, mv, std, rstd, xn, S["u"])
                v.wait_ge(S["u"].sem, S["u"].at(b, TT))
                ln_vector(v, b, S, ub, st, mv, std, rstd, xn, S["turned"], rms=True)
                v.wait_ge(S["ckv"].sem, S["ckv"].at(b, 1))
                sh = YT[0:64, 0, :]
                v.tensor_tensor(kvr[:, :], S2[0][0:64, :], cos[0:64, :], ALU.mult).then_inc(S["ropek"].sem, 1)
                v.stream_shuffle(sh, S2[0][0:64, :], swap).then_inc(S["shufk"].sem, 1)
                v.wait_ge(S["shufk"].sem, S["shufk"].at(b, 1))
                v.tensor_tensor(sh, sh, sin[0:64, :], ALU.mult).then_inc(S["ropek"].sem, 1)
                v.wait_ge(S["ropek"].sem, S["ropek"].at(b, 2))
                v.tensor_tensor(kvr[:, :], kvr[:, :], sh, ALU.add).then_inc(S["ropek"].sem, 1)
                for unit in range(5):
                    project(b, 0, 0, unit)
                    if unit in (L.Q0, L.Q1):
                        qlow(b, 0, 0, unit - L.Q0)
                with v.Fori(0, NQ) as m:
                    turn = b * NQ + m

                    def rowmax(j):
                        v.wait_ge(A["score"].sem, A["score"].at(turn, j + 1))
                        v.tensor_reduce(negmax[:, j:j + 1], S2[j % 2][:, 0:L.n(j)], AX.X, ALU.max,
                                        negate=True).then_inc(A["negmax"].sem, 1)

                    def low(j):
                        for u in L.of(j):
                            _, k0, nb = L.units[u]
                            at = (slice(None), j // 2 % 2, slice(k0, k0 + nb), slice(j % 2 * P, j % 2 * P + P))
                            v.wait_ge(A["pthi"].sem, A["pthi"].at(turn, u + 1))
                            v.tensor_tensor(PTlo[at], TR[u % 2][:, 0:nb * P].rearrange("p (k q) -> p k q", q=P),
                                            PThi[at].bitcast(F32), ALU.subtract).then_inc(A["ptlo"].sem, 1)

                    rowmax(0)
                    rowmax(1)
                    for j in range(J):
                        s, pr = j % 16, L.pair(j)
                        if j + 2 < J:
                            rowmax(j + 2)
                        if s in L.FREE_AT:
                            project(b, 2 * m + 1 + pr, 1 - pr, L.FREE_AT[s])
                        if s in L.QLO_AT:
                            qlow(b, 2 * m + 1 + pr, 1 - pr, L.QLO_AT[s])
                        low(j)
                    v.wait_ge(A["exp"].sem, A["exp"].at(turn, J))
                    v.tensor_scalar(allsums[:, bass.ds(J * m, J)], sums[:, :], 1.0, None, ALU.mult)\
                        .then_inc(A["kept"].sem, 1)
                v.wait_ge(A["kept"].sem, A["kept"].at(b * NQ + (NQ - 1), 1))
                v.reciprocal(allsums[:, :], allsums[:, :]).then_inc(S["recip"].sem, 1)
                v.wait_ge(S["sumsT"].sem, S["sumsT"].at(b, 1))
                v.tensor_tensor(placed, PJ[:, None, 0:P].broadcast_to([P, TT, P]),
                                tile_of[:, :, None].broadcast_to([P, TT, P]), ALU.mult)\
                    .then_inc(S["placed"].sem, 1)
                for n in range(NH * L_PAIRS):
                    half, pair = n // L_PAIRS, n % L_PAIRS
                    y = YT[:, pair, half * HALF:(half + 1) * HALF]
                    v.wait_ge(S["spread"].sem, S["spread"].at(b, n + 1))
                    v.tensor_tensor(y, y, pbanks[n % 4], ALU.mult).then_inc(S["divided"].sem, 1)
                for t in range(TT):
                    v.wait_ge(S["proj"].sem, S["proj"].at(b, t + 1))
                    v.tensor_tensor(ub[:, t, :], ub[:, t, :], pbanks[t % 4][:, 0:C], ALU.add)\
                        .then_inc(S["added"].sem, 1)

        @block.gpsimd
        def _(g):
            for name in ("scaled", "u", "sinq", "ropeq"):
                S[name].open(g)
            g.sem_inc(ustore, 1)

            def rope(b, s, h):
                g.wait_ge(S["free"].sem, S["free"].at(b, s * 5 + L.Q0 + h + 1))
                g.tensor_tensor(shuf[:, :], shuf[:, :], sin[:, h * HALF:(h + 1) * HALF], ALU.mult)\
                    .then_inc(S["sinq"].sem, 1)
                g.wait_ge(S["sinq"].sem, S["sinq"].at(b, s * 2 + h + 1))
                g.tensor_tensor(rot[:, :], rot[:, :], shuf[:, :], ALU.add)\
                    .then_inc(S["ropeq"].sem, 1)

            with g.Fori(0, B) as b:
                g.wait_ge(ustore, b * 16 + 1)
                for t in range(TT):
                    g.wait_ge(N1["xn"].sem, N1["xn"].at(b, t + 1))
                    g.tensor_tensor(ub[:, t, :], xn[:, t, :], cb[:, :], ALU.mult)\
                        .then_inc(S["scaled"].sem, 1)
                    g.wait_ge(S["scaled"].sem, S["scaled"].at(b, t + 1))
                    g.tensor_tensor(ub[:, t, :], ub[:, t, :], sbias[:, :], ALU.add)\
                        .then_inc(S["u"].sem, 1)
                for h in range(2):
                    rope(b, 0, h)
                with g.Fori(0, NQ) as m:
                    for pr in range(2):
                        for h in range(2):
                            rope(b, 2 * m + 1 + pr, h)

        @block.scalar
        def _(a):
            for sig in (N1["std"], S["std"], S["hT"], S["hi"], A["exp"], A["pthi"], A["yout"]):
                sig.open(a)

            def high(b, s, par, unit):
                cols = slice(unit % 2 * HALF, (unit % 2 + 1) * HALF)
                if unit in (L.Q0, L.Q1):
                    a.wait_ge(S["ropeq"].sem, S["ropeq"].at(b, s * 2 + unit - L.Q0 + 1))
                    a.activation(qhi[:, par, cols], rot[:, :], ACT.Copy)\
                        .then_inc(S["hi"].sem, 1)
                    return
                a.wait_ge(S["pj"].sem, S["pj"].at(b, s * 5 + unit + 1))
                if unit == L.VAL:
                    out = val[:, par].rearrange("p t (a n d) -> p t a n d", a=3, n=2)[:, :, 0:3:2, 0, :]
                    a.activation(out, PJ[:, :].rearrange("p (t h d) -> p t h d", h=2, d=NOPE), ACT.Copy)\
                        .then_inc(S["hi"].sem, 1)
                else:
                    a.activation(khi[:, par, cols], PJ[:, :], ACT.Copy, scale=L_D ** -0.5)\
                        .then_inc(S["hi"].sem, 1)

            with a.Fori(0, B) as b:
                ln_scalar_std(a, b, N1, mv, std, eps)
                ln_scalar_std(a, b, S, mv, std, eps, rms=True)
                ln_scalar_out(a, b, S, rT, 0, pbanks, lambda k: w_ln[:, k:k + 1], None)
                for unit in range(5):
                    high(b, 0, 0, unit)
                a.dma_start(wq[:, :, :], W["l_wq"][1:2]).then_inc(pload, 16)
                a.dma_start(wkp[:, :], W["l_wkp"][1:2]).then_inc(pload, 16)
                with a.Fori(0, NQ) as m:
                    turn = b * NQ + m

                    def exp(j):
                        a.wait_ge(A["turnedP"].sem, A["turnedP"].at(turn, L.before[j - 1] if j else
                                                                    L.before[-1] - NU))
                        a.wait_ge(A["negmax"].sem, A["negmax"].at(turn, j + 1))
                        a.activation(Pt[:, j % 2, 0:L.n(j)], S2[j % 2][:, 0:L.n(j)], ACT.Exp,
                                     bias=negmax[:, j:j + 1], accum_out=sums[:, j:j + 1])\
                            .then_inc(A["exp"].sem, 1)

                    def pt_high(j):
                        for u in L.of(j):
                            _, k0, nb = L.units[u]
                            at = (slice(None), j // 2 % 2, slice(k0, k0 + nb), slice(j % 2 * P, j % 2 * P + P))
                            a.wait_ge(A["pv"].sem, A["pv"].at(turn, j // 2 - 1))
                            a.wait_ge(A["turnedP"].sem, A["turnedP"].at(turn, u + 1))
                            a.activation(PThi[at], TR[u % 2][:, 0:nb * P].rearrange("p (k q) -> p k q", q=P),
                                         ACT.Copy).then_inc(A["pthi"].sem, 1)

                    def y_out(g):
                        a.wait_ge(A["pv"].sem, A["pv"].at(turn, 2 * g + 2))
                        a.activation(YT[:, bass.ds(2 * m + g // 4, 1), (g % 4) * 2 * P:(g % 4 + 1) * 2 * P],
                                     O[:, None, 0:2 * P], ACT.Copy).then_inc(A["yout"].sem, 1)

                    a.wait_ge(A["kept"].sem, A["kept"].at(turn, 0))
                    exp(0)
                    for j in range(J):
                        s, pr = j % 16, L.pair(j)
                        if j + 1 < J:
                            exp(j + 1)
                        if j >= 6 and (j - 6) % 4 == 0:
                            y_out((j - 6) // 4)
                        if s in L.HI_AT:
                            high(b, 2 * m + 1 + pr, 1 - pr, L.HI_AT[s])
                        if s == 12:
                            a.dma_start(wq[:, :, :], W["l_wq"][bass.ds(2 * m + 2 + pr, 1)]).then_inc(pload, 16)
                            a.dma_start(wkp[:, :], W["l_wkp"][bass.ds(2 * m + 2 + pr, 1)]).then_inc(pload, 16)
                        pt_high(j)
                    y_out(J // 4 - 1)
                a.wait_ge(S["added"].sem, S["added"].at(b, TT))
                a.dma_start(Ud[:, bass.ds(b * TT, TT), :], ub[:, :, :]).then_inc(ustore, 16)

        @block.tensor
        def _(pe):
            for name in ("turned", "ckv", "pj", "proj", "sumsT", "spread"):
                S[name].open(pe)
            for name in ("score", "turnedP", "pv"):
                A[name].open(pe)
            pe.wait_ge(wload, 7 * 16)

            def project(b, s, par, unit):
                pe.wait_ge(S["free"].sem, S["free"].at(b, s * 5 + unit))
                cols = slice(unit % 2 * HALF, (unit % 2 + 1) * HALF)
                if unit in (L.K0, L.K1):
                    mm = pe.matmul(PJ[:, :], wkp[:, :], kvr[:, cols], start=True, stop=True)
                elif unit in (L.Q0, L.Q1):
                    for k in range(KC):
                        mm = pe.matmul(PJ[:, :], wq[:, k, :], rT[:, k, cols],
                                       start=(k == 0), stop=(k == KC - 1))
                else:
                    wv = wkp[0:LATENT, :].rearrange("r (h d) -> r h d", h=2)[:, :, 0:NOPE]
                    for t in range(TT):
                        mm = pe.matmul(PJ[:, t * 64:(t + 1) * 64].rearrange("p (h d) -> p h d", h=2),
                                       kvr[0:LATENT, t * P:(t + 1) * P], wv, start=True, stop=True)
                mm.then_inc(S["pj"].sem, 1)

            with pe.Fori(0, B) as b:
                pe.wait_ge(S["added"].sem, S["added"].at(b, 0))
                ln_tensor(pe, b, S, xn, ident, pbanks)
                pe.wait_ge(S["hT"].sem, S["hT"].at(b, 2 * KC))
                for half in range(NH):
                    for k in range(KC):
                        mm = pe.matmul(S2[0][0:64, half * HALF:(half + 1) * HALF], wkva[:, k, :],
                                       rT[:, k, half * HALF:(half + 1) * HALF],
                                       start=(k == 0), stop=(k == KC - 1))
                mm.then_inc(S["ckv"].sem, 1)
                pe.wait_ge(S["ropek"].sem, S["ropek"].at(b, 3))
                pe.wait_ge(pload, b * (SETS * 32) + 32)
                for unit in range(5):
                    project(b, 0, 0, unit)
                with pe.Fori(0, NQ) as m:
                    turn = b * NQ + m

                    def score(j):
                        n, qt, par = L.n(j), L.qt(j), L.pair(j)
                        rows = slice(64 * L.head(j), 64 * L.head(j) + 64)
                        s = 2 * m + par
                        if j % 16 == 0:
                            pe.wait_ge(S["qlo"].sem, S["qlo"].at(b, s * 2 + 2))
                            pe.wait_ge(S["free"].sem, S["free"].at(b, s * 5 + 5))
                        if j >= 2:
                            pe.wait_ge(A["exp"].sem, A["exp"].at(turn, j - 1))
                        for n0 in range(0, n, HALF):
                            n1 = min(n, n0 + HALF)
                            diagonal = n1 == n
                            if diagonal:
                                pe.matmul(S2[j % 2][:, n - P:n], identb[:, :], causal[:, :], start=True,
                                          stop=False, skip_group_check=True)
                            for i, (q, k) in enumerate(((qhi, khi), (qhi, klo), (qlo, khi))):
                                mm = pe.matmul(S2[j % 2][:, n0:n1], q[rows, par, qt * P:(qt + 1) * P],
                                               k[rows, par, n0:n1], start=(i == 0 and not diagonal),
                                               stop=(i == 2), skip_group_check=diagonal)
                        mm.then_inc(A["score"].sem, 1)

                    def turn_p(j):
                        pe.wait_ge(A["exp"].sem, A["exp"].at(turn, j + 1))
                        for u in L.of(j):
                            _, k0, nb = L.units[u]
                            pe.wait_ge(A["ptlo"].sem, A["ptlo"].at(turn, u - 1))
                            for i in range(nb):
                                mm = pe.transpose(TR[u % 2][:, i * P:(i + 1) * P],
                                                  Pt[:, j % 2, (k0 + i) * P:(k0 + i + 1) * P], ident[:, :])
                            mm.then_inc(A["turnedP"].sem, 1)

                    def pv(x):
                        g, h, par = x // 2 % 4, x % 2, x // 8
                        last = 2 * g + 1
                        pe.wait_ge(A["ptlo"].sem, A["ptlo"].at(turn, L.of(2 * x + 1)[-1] + 1))
                        if h == 0:
                            pe.wait_ge(A["yout"].sem, A["yout"].at(turn, x // 2))
                        order = [0, last, *range(1, last)]
                        parts = [(PThi, kt) for kt in order] + [(PTlo, kt) for kt in order[1:] + [0]]
                        for n, (src, kt) in enumerate(parts):
                            c0 = P if kt == last else 0
                            mm = pe.matmul(O[:, c0:2 * P], val[:, par, kt, 64 * h:64 * h + P],
                                           src[:, x % 2, kt, c0:], start=(h == 0 and n == 0),
                                           stop=(h == 1 and n == len(parts) - 1), skip_group_check=True)
                        mm.then_inc(A["pv"].sem, 1)

                    score(0)
                    score(1)
                    for j in range(J):
                        s, pr = j % 16, L.pair(j)
                        if j + 2 < J:
                            score(j + 2)
                        if s in L.PE_AT:
                            if s == min(L.PE_AT):
                                pe.wait_ge(pload, b * (SETS * 32) + (2 * m + 2 + pr) * 32)
                            project(b, 2 * m + 1 + pr, 1 - pr, L.PE_AT[s])
                        if j >= 3 and j % 2 == 1:
                            pv((j - 3) // 2)
                        turn_p(j)
                    pv(J // 2 - 1)
                pe.wait_ge(A["yout"].sem, A["yout"].at(b * NQ + (NQ - 1), J // 4))
                pe.wait_ge(S["recip"].sem, S["recip"].at(b, 1))
                pe.transpose(PJ[:, 0:P], allsums[:, :], ident[:, :]).then_inc(S["sumsT"].sem, 1)
                pe.wait_ge(S["placed"].sem, S["placed"].at(b, 1))
                for n in range(NH * L_PAIRS):
                    half, pair = n // L_PAIRS, n % L_PAIRS
                    if n >= 4:
                        pe.wait_ge(S["divided"].sem, S["divided"].at(b, n - 3))
                    pe.matmul(pbanks[n % 4], heads[:, pair, :], Pt[:, 0, half * HALF:(half + 1) * HALF],
                              start=True, stop=True).then_inc(S["spread"].sem, 1)
                for t in range(TT):
                    if t == 0:
                        pe.wait_ge(S["divided"].sem, S["divided"].at(b, NH * L_PAIRS))
                    if t >= 4:
                        pe.wait_ge(S["added"].sem, S["added"].at(b, t - 3))
                    for k in range(L_PAIRS):
                        mm = pe.matmul(pbanks[t % 4][:, 0:C], YT[:, k, t * P:(t + 1) * P], wo[:, k, :],
                                       start=(k == 0), stop=(k == L_PAIRS - 1))
                    mm.then_inc(S["proj"].sem, 1)


def rope_attention(nc, sems, X, MODT, ROWS, ident, identb, causal, eps, W, K):
    J = TT
    with ExitStack() as ctx:
        def sb(name, shape, dt=F32):
            return ctx.enter_context(nc.sbuf_tensor("r_" + name, shape, dt))

        wq, wk, wv = (sb(n, [P, KC, C]) for n in ("wq", "wk", "wv"))
        cos, sin = sb("cos", [P, KC, T]), sb("sin", [P, KC, T])
        xb = sb("xb", [P, TT, C])
        mod, gate = sb("mod", [P, 12]), sb("gate", [P, C])
        xn = sb("xn", [P, TT, C])
        st, mv = sb("st", [P, TT, 6]), sb("mv", [P, TT, 2])
        std, rstd = sb("std", [P, TT]), sb("rstd", [P, TT])
        hT = sb("hT", [P, KC, T])
        shuf = sb("shuf", [P, 2 * KC, T])
        qk = sb("qk", [P, 2 * KC, T])
        V = sb("V", [P, TT, C])
        Pt, PT = sb("Pt", [P, 2, T]), sb("PT", [P, 2, TT, P])
        negmax, sums, rs = sb("negmax", [P, J]), sb("sums", [P, J]), sb("rs", [P, J])
        tmp = sb("tmp", [P, TT, C])
        S2 = [ctx.enter_context(nc.psum_tensor(f"r_s{i}", [P, 2 * HALF], F32)) for i in range(2)]
        TR = [ctx.enter_context(nc.psum_tensor(f"r_t{i}", [P, HALF], F32)) for i in range(2)]
        O = [ctx.enter_context(nc.psum_tensor(f"r_o{i}", [P, HALF], F32)) for i in range(2)]
        banks = [TR[0][:, :], TR[1][:, :], O[0][:, :], O[1][:, :]]
        S = signals(sems, nc, "r", dict(LN_SIGNALS) | attention_signals(J) | dict(
            proj=4, shufd=4, cosd=4, sind=4, rope=4, vproj=4, vout=4, gated=TT, added=TT))
        wload = sems.enter_context(nc.semaphore("r_wload"))
        xload = sems.enter_context(nc.semaphore("r_xload"))
        xstore = sems.enter_context(nc.semaphore("r_xstore"))
        block = ctx.enter_context(nc.Block())

        @block.sync
        def _(sp):
            for dst, src in ((wq, W["r_wq"]), (wk, W["r_wk"]), (wv, W["r_wv"]), (cos, K["rcos"]),
                             (sin, K["rsin"])):
                sp.dma_start(dst[:, :, :], src).then_inc(wload, 16)
            with sp.Fori(0, B) as b:
                sp.wait_ge(S["added"].sem, S["added"].at(b, 0))
                sp.wait_ge(xstore, b * 16 + 1)
                sp.dma_start(xb[:, :, :], X[:, bass.ds(b * TT, TT), :]).then_inc(xload, 16)
                sp.dma_start(mod[:, :], MODT[:, 1, bass.ds(b, 1), :]).then_inc(xload, 16)
                sp.dma_start(gate[:, :], ROWS[:, 4, bass.ds(b, 1), :]).then_inc(xload, 16)
                sp.wait_ge(S["added"].sem, S["added"].at(b, TT))
                sp.dma_start(X[:, bass.ds(b * TT, TT), :], xb[:, :, :]).then_inc(xstore, 16)
            sp.wait_ge(xstore, B * 16 + 1)

        @block.vector
        def _(v):
            for name in ("stats", "rstd", "xn", "shufd", "cosd", "negmax", "evac2", "recip", "norm"):
                S[name].open(v)
            v.wait_ge(wload, 5 * 16)
            swap = [i ^ 1 for i in range(32)]
            with v.Fori(0, B) as b:
                v.wait_ge(xload, b * 48 + 48)
                ln_vector(v, b, S, xb, st, mv, std, rstd, xn, S["turned"])
                for u in range(4):
                    v.wait_ge(S["proj"].sem, S["proj"].at(b, u + 1))
                    v.tensor_tensor(qk[:, u, :], S2[u % 2][:, :], cos[:, u % KC, :], ALU.mult)\
                        .then_inc(S["cosd"].sem, 1)
                    v.stream_shuffle(shuf[:, u, :], S2[u % 2][:, :], swap).then_inc(S["shufd"].sem, 1)
                att_vector(v, b, S, J, S2, TR, PT, O, negmax, sums, rs, C, lambda j: tmp[:, j, :])

        @block.gpsimd
        def _(g):
            for name in ("sind", "rope", "gated", "added"):
                S[name].open(g)
            g.sem_inc(xstore, 1)
            with g.Fori(0, B) as b:
                for u in range(4):
                    g.wait_ge(S["shufd"].sem, S["shufd"].at(b, u + 1))
                    g.tensor_tensor(shuf[:, u, :], shuf[:, u, :], sin[:, u % KC, :], ALU.mult)\
                        .then_inc(S["sind"].sem, 1)
                    g.wait_ge(S["sind"].sem, S["sind"].at(b, u + 1))
                    g.wait_ge(S["cosd"].sem, S["cosd"].at(b, u + 1))
                    g.tensor_tensor(qk[:, u, :], qk[:, u, :], shuf[:, u, :], ALU.add)\
                        .then_inc(S["rope"].sem, 1)
                for t in range(TT):
                    g.wait_ge(S["norm"].sem, S["norm"].at(b, t + 1))
                    g.tensor_tensor(tmp[:, t, :], tmp[:, t, :], gate[:, :], ALU.mult)\
                        .then_inc(S["gated"].sem, 1)
                    g.wait_ge(S["gated"].sem, S["gated"].at(b, t + 1))
                    g.tensor_tensor(xb[:, t, :], xb[:, t, :], tmp[:, t, :], ALU.add)\
                        .then_inc(S["added"].sem, 1)

        @block.scalar
        def _(a):
            for name in ("std", "hT", "vout", "exp", "evac"):
                S[name].open(a)
            with a.Fori(0, B) as b:
                ln_scalar_std(a, b, S, mv, std, eps)
                ln_scalar_out(a, b, S, hT, 0, banks, lambda k: mod[:, 2 * CA + k:2 * CA + k + 1],
                              lambda k: mod[:, 2 * SA + k:2 * SA + k + 1])
                for u in range(4):
                    a.wait_ge(S["vproj"].sem, S["vproj"].at(b, u + 1))
                    a.activation(V[:, 2 * u:2 * u + 2, :],
                                 banks[u].rearrange("p (t c) -> p t c", t=2), ACT.Copy)\
                        .then_inc(S["vout"].sem, 1)
                att_scalar(a, b, S, J, S2, TR, Pt, PT, negmax, sums)

        @block.tensor
        def _(pe):
            for name in ("turned", "proj", "vproj", "score", "turnedP", "pv"):
                S[name].open(pe)
            pe.wait_ge(wload, 5 * 16)
            with pe.Fori(0, B) as b:
                pe.wait_ge(S["norm"].sem, S["norm"].at(b, 0))
                ln_tensor(pe, b, S, xn, ident, banks)
                pe.wait_ge(S["hT"].sem, S["hT"].at(b, 2 * KC))
                for u in range(4):
                    w, et = (wq, wk)[u // KC], u % KC
                    if u >= 2:
                        pe.wait_ge(S["shufd"].sem, S["shufd"].at(b, u - 1))
                    for half in range(NH):
                        for k in range(KC):
                            mm = pe.matmul(S2[u % 2][:, half * HALF:(half + 1) * HALF],
                                           w[:, k, et * P:(et + 1) * P],
                                           hT[:, k, half * HALF:(half + 1) * HALF],
                                           start=(k == 0), stop=(k == KC - 1))
                    mm.then_inc(S["proj"].sem, 1)
                for u in range(4):
                    for i in range(2):
                        t = 2 * u + i
                        for k in range(KC):
                            mm = pe.matmul(banks[u][:, i * C:(i + 1) * C], hT[:, k, t * P:(t + 1) * P],
                                           wv[:, k, :], start=(k == 0), stop=(k == KC - 1))
                    mm.then_inc(S["vproj"].sem, 1)
                pe.wait_ge(S["rope"].sem, S["rope"].at(b, 4))
                pe.wait_ge(S["vout"].sem, S["vout"].at(b, 4))
                att_tensor(pe, b, S, J,
                           lambda j, k, qt: qk[:, k, qt * P:(qt + 1) * P],
                           lambda j, k, n0, n1: qk[:, KC + k, n0:n1],
                           lambda j, i: V[:, i, :],
                           KC, C, ident, identb, causal, S2, TR, O, Pt, PT)


def experts(nc, sems, name, X, U, MODT, ROWS, ident, identb, eps, W, K, out):
    first = U is not None
    M = MOE0 if first else MOE1
    E, NS = M["experts"], M["shared"]
    NT = NS + M["routed"]
    G = 4
    with ExitStack() as ctx:
        def sb(nm, shape, dt=F32):
            return ctx.enter_context(nc.sbuf_tensor(f"{name}_{nm}", shape, dt))

        wghi, wglo = sb("wghi", [P, NT, KC, P], F32R), sb("wglo", [P, NT, KC, P], F32R)
        wuhi, wulo = sb("wuhi", [P, NT, KC, P], F32R), sb("wulo", [P, NT, KC, P], F32R)
        wdhi, wdlo = sb("wdhi", [P, NT, C], F32R), sb("wdlo", [P, NT, C], F32R)
        staged = [sb("staged", [P, NT * C]), sb("results", [P, 3 * 2 * HALF])]
        sg, hid = (staged[1][:, n * 2 * HALF:(n + 1) * 2 * HALF].rearrange("p (i q) -> p i q", i=2)
                   for n in range(2))
        tmp = staged[1][:, 4 * HALF:].rearrange("p (t c) -> p t c", c=C)
        wr = sb("wr", [P, KC, E])
        rbias = sb("rbias", [P, E])
        lower = sb("lower", [P, E, E])
        selb = sb("selb", [P, M["routed"], P], BF16)
        w_ln = sb("w_ln", [P, KC])
        xbs = sb("xb", [P, 2, TT, C])
        ubs = sb("ub", [P, 2, TT, C]) if first else None
        mod, gates = sb("mod", [P, 12]), sb("gate", [P, 2, C])
        xn = sb("xn", [P, TT, C])
        st, mv = sb("st", [P, TT, 6]), sb("mv", [P, TT, 2])
        std, rstd = sb("std", [P, TT]), sb("rstd", [P, TT])
        hT = sb("hT", [P, KC, T])
        hThi, hTlo = sb("hThi", [P, 2, KC, T], F32R), sb("hTlo", [P, 2, KC, T], F32R)
        score, key = sb("score", [P, TT, E]), sb("key", [P, TT, E])
        red = sb("red", [P, TT])
        r1, r2 = sb("r1", [P, TT * E * E]), sb("r2", [P, TT * E * E])
        rank, comb = sb("rank", [P, TT, E]), sb("comb", [P, TT, E])
        gA, gB, gC, gD = (sb(n, [P, TT * G]) for n in ("gA", "gB", "gC", "gD"))
        comb3 = sb("comb3", [P, TT, P], BF16)
        combT = sb("combT", [P, 2, T], BF16)
        hidhi, hidlo = sb("hidhi", [P, 2, HALF], F32R), sb("hidlo", [P, 2, HALF], F32R)
        Gb = [ctx.enter_context(nc.psum_tensor(f"{name}_g{i}", [P, HALF], F32)) for i in range(2)]
        Ub = [ctx.enter_context(nc.psum_tensor(f"{name}_u{i}", [P, HALF], F32)) for i in range(2)]
        Cb = ctx.enter_context(nc.psum_tensor(f"{name}_c", [P, HALF], F32))
        Z = ctx.enter_context(nc.psum_tensor(f"{name}_z", [P, HALF], F32))
        acc = [ctx.enter_context(nc.psum_tensor(f"{name}_a{i}", [P, HALF], F32)) for i in range(2)]
        CHAIN = 17 if first else 33
        LOAD = 3
        NJ = NH * NT
        NR = NH * M["routed"]
        S = signals(sems, nc, name, dict(LN_SIGNALS) | dict(
            sq=2, logits=1, act=1, chain=(CHAIN, 0), comb=1, combP=1, combT=1, gate=NJ, up=NJ, cb=NR, silu=NJ,
            hThi=2 * KC, hTlo=2 * KC, mul=NJ, scaled=NR, high=NJ, low=NJ, down=(NJ, 2), y=TT, gated=TT, added=(TT, 4)))
        wload = sems.enter_context(nc.semaphore(name + "_wload"))
        xload = sems.enter_context(nc.semaphore(name + "_xload"))
        xstore = sems.enter_context(nc.semaphore(name + "_xstore"))
        consts = sems.enter_context(nc.semaphore(name + "_consts"))
        staging = [sems.enter_context(nc.semaphore(f"{name}_staging{i}")) for i in range(2)]
        split_hi = sems.enter_context(nc.semaphore(name + "_split_hi"))
        split_lo = sems.enter_context(nc.semaphore(name + "_split_lo"))
        block = ctx.enter_context(nc.Block())
        loads = 48 + 16 * first
        src = ubs if first else xbs

        def routed(n):
            return n // NT * M["routed"] + max(0, n % NT - NS)

        flat = lambda x: x[:, :, :, :].rearrange("p a k m -> p (a k m)")
        splits = [(flat(wghi), flat(wglo)), (flat(wuhi), flat(wulo)),
                  (wdhi[:, :, :].rearrange("p a c -> p (a c)"), wdlo[:, :, :].rearrange("p a c -> p (a c)"))]
        selector = hT[:, 0, 0:M["routed"] * P]

        def piece(ahead):
            next(ahead, None)

        @block.sync
        def _(sp):
            def load(b, par):
                sp.dma_start(xbs[:, par], X[:, bass.ds(b * TT, TT), :]).then_inc(xload, 16)
                if first:
                    sp.dma_start(ubs[:, par], U[:, bass.ds(b * TT, TT), :]).then_inc(xload, 16)
                sp.dma_start(mod[:, :], MODT[:, 1, bass.ds(b, 1), :]).then_inc(xload, 16)
                sp.dma_start(gates[:, par, :], ROWS[:, 1 if first else 5, bass.ds(b, 1), :])\
                    .then_inc(xload, 16)

            load(0, 0)
            sp.dma_start(wr[:, :, :], W[name + "_wr"]).then_inc(wload, 16)
            sp.dma_start(rbias[:, :], W[name + "_rb"].partition_broadcast(P)).then_inc(wload, 16)
            sp.dma_start(lower[:, :, :], K[name + "_lower"]).then_inc(wload, 16)
            sp.dma_start(w_ln[:, :], W["m0_ln"]).then_inc(wload, 16)
            sp.dma_start(selector.rearrange("p (j m) -> p j m", m=P), K[name + "_sel"]).then_inc(wload, 16)
            for n, wt in enumerate(("_wg", "_wu", "_wd")):
                if n == 2:
                    sp.wait_ge(split_lo, 1)
                src_w = W[name + wt]
                src_w = src_w.rearrange("p a c -> p (a c)") if n == 2 else \
                    src_w.rearrange("p a k m -> p (a k m)")
                sp.dma_start(staged[n % 2][:, 0:NT * C], src_w).then_inc(staging[n % 2], 16)
            with sp.Fori(0, B // 2) as i:
                for par in range(2):
                    b = 2 * i + par
                    used, summed = S["hThi"].at(b, 2 * KC), S["added"].at(b, 0)
                    sp.wait_ge(S["added"].sem, summed)
                    sp.wait_ge(S["hThi"].sem, used)
                    sp.wait_ge(xstore, b * 16 + 1)
                    load(b + 1, 1 - par)
                    sp.wait_ge(S["added"].sem, S["added"].at(b, TT))
                    if first:
                        sp.dma_start(X[:, bass.ds(b * TT, TT), :], xbs[:, par]).then_inc(xstore, 16)
                    else:
                        sp.dma_start(out[bass.ds(b, 1)].rearrange("b (t p) c -> p (b t) c", p=P), xbs[:, par])\
                            .then_inc(xstore, 16)
            sp.wait_ge(xload, (B + 1) * loads)
            sp.wait_ge(xstore, B * 16 + 1)

        @block.vector
        def _(v):
            for nm in ("stats", "sq", "rstd", "xn", "comb", "combT", "hTlo", "mul", "scaled",
                       "low", "y"):
                S[nm].open(v)
            v.wait_ge(wload, 5 * 16)
            v.tensor_copy(selb[:, :, :], selector.rearrange("p (j m) -> p j m", m=P)).then_inc(consts, 1)
            v.memset(comb3[:, :, :], 0.0).then_inc(consts, 1)
            v.wait_ge(consts, 2)

            def over(x):
                return x[:, :, None].broadcast_to([P, TT, E])

            lg = Z[:, 0:TT * E].rearrange("p (t e) -> p t e", e=E)
            bias = rbias[:, None, :].broadcast_to([P, TT, E])

            def ahead(b, par):
                for _ in range(LOAD):
                    yield
                v.wait_ge(xload, b * loads + loads)
                yield from ln_pieces(v, b, S, src[:, par], st, mv, std, rstd, xn, S["turned"], rms=first)
                for u in range(2 * KC):
                    yield
                    k, cols = u // 2, slice(u % 2 * HALF, (u % 2 + 1) * HALF)
                    v.wait_ge(S["hThi"].sem, S["hThi"].at(b, u + 1))
                    v.tensor_tensor(hTlo[:, par, k, cols], hT[:, k, cols],
                                    hThi[:, par, k, cols].bitcast(F32), ALU.subtract)\
                        .then_inc(S["hTlo"].sem, 1)
                yield
                steps = [0]

                def link(ins):
                    steps[0] += 1
                    ins.then_inc(S["chain"].sem, 1)
                    v.wait_ge(S["chain"].sem, b * CHAIN + steps[0])

                def ranks(x, n, e, low, dst):
                    size = n * e * e
                    a3 = r1[:, 0:size].rearrange("p (t i j) -> p t i j", i=e, j=e)
                    b3 = r2[:, 0:size].rearrange("p (t i j) -> p t i j", i=e, j=e)
                    other = x[:, :, None, :].broadcast_to([P, n, e, e])
                    mine = x[:, :, :, None].broadcast_to([P, n, e, e])
                    link(v.tensor_tensor(a3, other, mine, ALU.is_gt))
                    yield
                    link(v.tensor_tensor(b3, other, mine, ALU.is_equal))
                    yield
                    link(v.tensor_tensor(b3, b3, low[:, None, :, :].broadcast_to([P, n, e, e]), ALU.mult))
                    yield
                    link(v.tensor_tensor(r1[:, 0:size], r1[:, 0:size], r2[:, 0:size], ALU.add))
                    yield
                    link(v.tensor_reduce(dst, r1[:, 0:size].rearrange("p (t j) -> p t j", j=e), AX.X, ALU.add))
                    yield

                v.wait_ge(S["logits"].sem, S["logits"].at(b, 1))
                if first:
                    link(v.tensor_tensor(key[:, :, :], lg, bias, ALU.add))
                    link(v.tensor_reduce(red[:, :], key[:, :, :], AX.X, ALU.max))
                    v.tensor_tensor(key[:, :, :], key[:, :, :], over(red), ALU.subtract)\
                        .then_inc(S["comb"].sem, 1)
                    yield
                    v.wait_ge(S["act"].sem, S["act"].at(b, 1))
                    yield from ranks(score[:, :, :], TT, E, lower[:, :, :],
                                     rank[:, :, :].rearrange("p t e -> p (t e)"))
                    keep = 2
                else:
                    yield
                    v.wait_ge(S["act"].sem, S["act"].at(b, 1))
                    link(v.tensor_tensor(key[:, :, :], score[:, :, :], bias, ALU.add))
                    g4 = key[:, :, :].rearrange("p t (g i) -> p (t g) i", i=4)
                    link(v.tensor_tensor(gA[:, :], g4[:, :, 0], g4[:, :, 1], ALU.max))
                    link(v.tensor_tensor(gB[:, :], g4[:, :, 0], g4[:, :, 1], ALU.min))
                    link(v.tensor_tensor(gC[:, :], g4[:, :, 2], g4[:, :, 3], ALU.max))
                    link(v.tensor_tensor(gD[:, :], g4[:, :, 2], g4[:, :, 3], ALU.min))
                    link(v.tensor_tensor(gB[:, :], gB[:, :], gD[:, :], ALU.max))
                    link(v.tensor_tensor(gD[:, :], gA[:, :], gC[:, :], ALU.min))
                    link(v.tensor_tensor(gB[:, :], gB[:, :], gD[:, :], ALU.max))
                    link(v.tensor_tensor(gA[:, :], gA[:, :], gC[:, :], ALU.max))
                    link(v.tensor_tensor(gA[:, :], gA[:, :], gB[:, :], ALU.add))
                    yield
                    for _ in ranks(gA[:, :].rearrange("p (t g) -> p t g", g=G), TT, G, lower[:, 0:G, 0:G],
                                   gC[:, :]):
                        pass
                    link(v.tensor_scalar(gC[:, :], gC[:, :], 2.0, MASKED, ALU.is_ge, ALU.mult))
                    link(v.tensor_tensor(g4, g4, gC[:, :, None].broadcast_to([P, TT * G, 4]), ALU.add))
                    yield
                    yield from ranks(key[:, :, :], TT, E, lower[:, :, :],
                                     rank[:, :, :].rearrange("p t e -> p (t e)"))
                    keep = 4
                link(v.tensor_scalar(rank[:, :, :], rank[:, :, :], float(keep), None, ALU.is_lt))
                link(v.tensor_tensor(comb[:, :, :], score[:, :, :], rank[:, :, :], ALU.mult))
                link(v.tensor_reduce(red[:, :], comb[:, :, :], AX.X, ALU.add))
                if not first:
                    link(v.tensor_scalar(red[:, :], red[:, :], 1e-20, None, ALU.add))
                link(v.reciprocal(red[:, :], red[:, :]))
                link(v.tensor_tensor(comb[:, :, :], comb[:, :, :], over(red), ALU.mult))
                v.wait_ge(S["combP"].sem, S["combP"].at(b, 0))
                for s in range(3):
                    link(v.tensor_copy(comb3[:, :, s * E:(s + 1) * E], comb[:, :, :]))
                    if s < 2:
                        link(v.tensor_tensor(comb[:, :, :], comb[:, :, :], comb3[:, :, s * E:(s + 1) * E],
                                             ALU.subtract))
                assert steps[0] == CHAIN
                yield
                v.wait_ge(S["combP"].sem, S["combP"].at(b, 1))
                v.tensor_copy(combT[:, par, :], Z[:, :].bitcast(BF16)).then_inc(S["combT"].sem, 1)

            def hidden(b, c, j):
                n = c * NT + j
                s, h = sg[:, n % 2, :], hid[:, n % 2, :]
                v.wait_ge(S["silu"].sem, S["silu"].at(b, n + 1))
                if j >= NS:
                    v.wait_ge(S["cb"].sem, S["cb"].at(b, routed(n + 1)))
                    v.tensor_tensor(s, s, Cb[:, :], ALU.mult).then_inc(S["scaled"].sem, 1)
                    v.wait_ge(S["scaled"].sem, S["scaled"].at(b, routed(n + 1)))
                v.wait_ge(S["up"].sem, S["up"].at(b, n + 1))
                v.wait_ge(S["low"].sem, S["low"].at(b, n - 1))
                v.tensor_tensor(h, Ub[n % 2][:, :], s, ALU.mult).then_inc(S["mul"].sem, 1)
                v.wait_ge(S["high"].sem, S["high"].at(b, n + 1))
                v.tensor_tensor(hidlo[:, n % 2, :], h, hidhi[:, n % 2, :].bitcast(F32), ALU.subtract)\
                    .then_inc(S["low"].sem, 1)

            for _ in ahead(0, 0):
                pass
            for n, (hi, lo) in enumerate(splits):
                v.wait_ge(split_hi, n + 1)
                v.tensor_tensor(lo, staged[n % 2][:, 0:NT * C], hi.bitcast(F32), ALU.subtract)\
                    .then_inc(split_lo, 1)
            with v.Fori(0, B // 2) as i:
                for par in range(2):
                    b = 2 * i + par
                    nxt = ahead(b + 1, 1 - par)
                    for c in range(NH):
                        for j in range(NT):
                            hidden(b, c, j)
                            piece(nxt)
                        for q in range(4):
                            t = 4 * c + q
                            v.wait_ge(S["down"].sem, S["down"].at(b, (c + 1) * NT))
                            v.wait_ge(S["added"].sem, S["added"].at(b, t - 3))
                            row = acc[q // 2][:, (q % 2) * C:(q % 2 + 1) * C]
                            v.tensor_tensor(tmp[:, q, :], row,
                                            ubs[:, par, t, :] if first else gates[:, par, :],
                                            ALU.add if first else ALU.mult).then_inc(S["y"].sem, 1)
                    for _ in nxt:
                        pass

        @block.gpsimd
        def _(g):
            for nm in ("gated", "added"):
                S[nm].open(g)
            g.sem_inc(xstore, 1)
            with g.Fori(0, B // 2) as i:
                for par in range(2):
                    b = 2 * i + par
                    for t in range(TT):
                        g.wait_ge(S["y"].sem, S["y"].at(b, t + 1))
                        if first:
                            g.tensor_tensor(tmp[:, t % 4, :], tmp[:, t % 4, :], gates[:, par, :], ALU.mult)\
                                .then_inc(S["gated"].sem, 1)
                            g.wait_ge(S["gated"].sem, S["gated"].at(b, t + 1))
                        g.tensor_tensor(xbs[:, par, t, :], xbs[:, par, t, :], tmp[:, t % 4, :], ALU.add)\
                            .then_inc(S["added"].sem, 1)

        @block.scalar
        def _(a):
            for nm in ("std", "hT", "hThi", "act", "silu", "high"):
                S[nm].open(a)
            a.wait_ge(consts, 2)

            def ahead(b, par):
                for _ in range(LOAD + 1):
                    yield
                ln_scalar_std(a, b, S, mv, std, eps, rms=first)
                for u in range(2 * KC):
                    yield
                    k, half = u // 2, u % 2
                    cols = slice(half * HALF, (half + 1) * HALF)
                    a.wait_ge(S["turned"].sem, S["turned"].at(b, u + 1))
                    for dst, done in ((hT[:, k, cols], "hT"), (hThi[:, par, k, cols], "hThi")):
                        if first:
                            a.activation(dst, Z[:, :], ACT.Copy, scale=w_ln[:, k:k + 1])\
                                .then_inc(S[done].sem, 1)
                        else:
                            a.activation(dst, Z[:, :], ACT.Identity, scale=mod[:, 2 * CB + k:2 * CB + k + 1],
                                         bias=mod[:, 2 * SB + k:2 * SB + k + 1]).then_inc(S[done].sem, 1)
                for _ in range(3):
                    yield
                if first:
                    a.wait_ge(S["comb"].sem, S["comb"].at(b, 1))
                    a.activation(score[:, :, :], key[:, :, :], ACT.Exp).then_inc(S["act"].sem, 1)
                else:
                    a.wait_ge(S["logits"].sem, S["logits"].at(b, 1))
                    a.activation(score[:, :, :], Z[:, 0:TT * E].rearrange("p (t e) -> p t e", e=E),
                                 ACT.Sigmoid).then_inc(S["act"].sem, 1)

            for _ in ahead(0, 0):
                pass
            for n, (hi, _) in enumerate(splits):
                a.wait_ge(staging[n % 2], (n // 2 + 1) * 16)
                a.activation(hi, staged[n % 2][:, 0:NT * C], ACT.Copy).then_inc(split_hi, 1)
            with a.Fori(0, B // 2) as i:
                for par in range(2):
                    b = 2 * i + par
                    nxt = ahead(b + 1, 1 - par)
                    for n in range(NJ):
                        a.wait_ge(S["gate"].sem, S["gate"].at(b, n + 1))
                        a.wait_ge(S["mul"].sem, S["mul"].at(b, n - 1))
                        a.activation(sg[:, n % 2, :], Gb[n % 2][:, :], ACT.Silu).then_inc(S["silu"].sem, 1)
                        a.wait_ge(S["down"].sem, S["down"].at(b, n - 1))
                        a.wait_ge(S["mul"].sem, S["mul"].at(b, n + 1))
                        a.activation(hidhi[:, n % 2, :], hid[:, n % 2, :], ACT.Copy)\
                            .then_inc(S["high"].sem, 1)
                        if n >= 1:
                            piece(nxt)
                    for _ in nxt:
                        pass

        @block.tensor
        def _(pe):
            for nm in ("turned", "logits", "combP", "gate", "up", "cb", "down"):
                S[nm].open(pe)

            def ahead(b, par):
                for _ in range(LOAD + 2):
                    yield
                pe.wait_ge(S["combT"].sem, S["combT"].at(b, 0))
                for u in range(2 * KC):
                    k, half = u // 2, u % 2
                    if k == 0:
                        pe.wait_ge(S["xn"].sem, S["xn"].at(b, 4 * half + 4))
                    if u >= 1:
                        pe.wait_ge(S["hThi"].sem, S["hThi"].at(b, u))
                    for q in range(4):
                        mm = pe.transpose(Z[:, q * P:(q + 1) * P],
                                          xn[:, 4 * half + q, k * P:(k + 1) * P], ident[:, :])
                    mm.then_inc(S["turned"].sem, 1)
                    yield
                pe.wait_ge(S["hThi"].sem, S["hThi"].at(b, 2 * KC))
                for t in range(TT):
                    for k in range(KC):
                        mm = pe.matmul(Z[:, t * E:(t + 1) * E], hT[:, k, t * P:(t + 1) * P],
                                       wr[:, k, :], start=(k == 0), stop=(k == KC - 1))
                mm.then_inc(S["logits"].sem, 1)
                for _ in range(8 if first else 10):
                    yield
                pe.wait_ge(S["chain"].sem, b * CHAIN + CHAIN)
                for t in range(TT):
                    mm = pe.transpose(Z[:, :].bitcast(BF16)[:, t * P:(t + 1) * P], comb3[:, t, :],
                                      identb[:, :])
                mm.then_inc(S["combP"].sem, 1)

            def up(b, par, c, j):
                n = c * NT + j
                cols = slice(c * HALF, (c + 1) * HALF)
                if j >= NS:
                    if routed(n):
                        pe.wait_ge(S["scaled"].sem, S["scaled"].at(b, routed(n)))
                    pe.matmul(Cb[:, :], selb[:, j - NS, :], combT[:, par, cols],
                              start=True, stop=True).then_inc(S["cb"].sem, 1)
                for bank, whi, wlo, free, done in ((Gb, wghi, wglo, "silu", "gate"),
                                                   (Ub, wuhi, wulo, "mul", "up")):
                    if n >= 2:
                        pe.wait_ge(S[free].sem, S[free].at(b, n - 1))
                    parts = [(w, h, k) for k in range(KC)
                             for w, h in ((whi, hThi), (whi, hTlo), (wlo, hThi))]
                    for m, (w, h, k) in enumerate(parts):
                        mm = pe.matmul(bank[n % 2][:, :], w[:, j, k, :], h[:, par, k, cols],
                                       start=(m == 0), stop=(m == len(parts) - 1))
                    mm.then_inc(S[done].sem, 1)

            def down(b, c, j):
                n = c * NT + j
                pe.wait_ge(S["low"].sem, S["low"].at(b, n + 1))
                if j == 0:
                    pe.wait_ge(S["y"].sem, S["y"].at(b, 4 * c))
                for q in range(4):
                    for m, (h, w) in enumerate(((hidhi, wdhi), (hidhi, wdlo), (hidlo, wdhi))):
                        mm = pe.matmul(acc[q // 2][:, (q % 2) * C:(q % 2 + 1) * C],
                                       h[:, n % 2, q * P:(q + 1) * P], w[:, j, :],
                                       start=(j == 0 and q % 2 == 0 and m == 0),
                                       stop=(j == NT - 1 and m == 2), skip_group_check=True)
                mm.then_inc(S["down"].sem, 1)

            pe.wait_ge(wload, 5 * 16)
            for _ in ahead(0, 0):
                pass
            pe.wait_ge(split_lo, 3)
            with pe.Fori(0, B // 2) as i:
                for par in range(2):
                    b = 2 * i + par
                    nxt = ahead(b + 1, 1 - par)
                    pe.wait_ge(S["combT"].sem, S["combT"].at(b, 1))
                    order = [(c, j) for c in range(NH) for j in range(NT)]
                    up(b, par, *order[0])
                    for n, cj in enumerate(order):
                        if n + 1 < len(order):
                            up(b, par, *order[n + 1])
                        if n >= 1:
                            piece(nxt)
                        down(b, *cj)
                    for _ in nxt:
                        pass


def build(nc, w, k, out, upto=5):
    with ExitStack() as ctx:
        def sb(name, shape, dt=F32):
            return ctx.enter_context(nc.sbuf_tensor(name, shape, dt))

        MODT = sb("MODT", [P, 2, B + 1, 12])
        X = nc.dram_tensor("xs", (P, (B + 1) * TT, C), F32, kind="Internal").ap()
        ROWS = nc.dram_tensor("rows", (P, 6, B + 1, C), F32, kind="Internal").ap()
        U = nc.dram_tensor("u", (P, (B + 1) * TT, C), F32, kind="Internal").ap()
        ident, identb = sb("ident", [P, P]), sb("identb", [P, P], BF16)
        causal, eps = sb("causal", [P, P], BF16), sb("eps", [P, 1])
        mask = sb("mask", [P, P])
        loaded = ctx.enter_context(nc.semaphore("loaded"))
        ready = ctx.enter_context(nc.semaphore("ready"))
        with nc.Block() as block:
            @block.sync
            def _(sp):
                sp.dma_start(ident[:, :], k["ident"]).then_inc(loaded, 16)
                sp.dma_start(mask[:, :], k["causal"]).then_inc(loaded, 16)
                sp.wait_ge(loaded, 2 * 16)

            @block.vector
            def _(v):
                v.memset(eps[:, :], EPS).then_inc(ready, 1)
                v.memset(MODT[:, :, :, :], 0.0).then_inc(ready, 1)
                v.wait_ge(loaded, 2 * 16)
                v.tensor_copy(identb[:, :], ident[:, :]).then_inc(ready, 1)
                v.tensor_copy(causal[:, :], mask[:, :]).then_inc(ready, 1)

        modulation(nc, w["cT"], w["wmod"], w["x"], MODT, ROWS, X, U)
        phases = [
            lambda sems: windowed_attention(nc, sems, X, MODT, ROWS, ident, identb, eps, w, k),
            lambda sems: latent_attention(nc, sems, X, U, ROWS, ident, identb, causal, eps, w, k),
            lambda sems: experts(nc, sems, "m0", X, U, MODT, ROWS, ident, identb, eps, w, k, None),
            lambda sems: rope_attention(nc, sems, X, MODT, ROWS, ident, identb, causal, eps, w, k),
            lambda sems: experts(nc, sems, "m1", X, None, MODT, ROWS, ident, identb, eps, w, k, out)]
        for phase in phases[:upto]:
            with Semaphores() as sems, cleared_after(nc, sems.used):
                phase(sems)
        if upto < 5:
            st = ctx.enter_context(nc.semaphore("dbg"))
            with nc.Block() as block:
                @block.sync
                def _(sp):
                    for b in range(B):
                        sp.dma_start(out[b].rearrange("(t p) c -> p t c", p=P),
                                     (U if upto == 2 else X)[:, b * TT:(b + 1) * TT, :]).then_inc(st, 16)
                    sp.wait_ge(st, 16 * B)


def tables():
    f = np.float32
    i = np.arange(P)
    k = {"ident": np.eye(P, dtype=f)}
    k["causal"] = np.where(i[None, :] <= i[:, None], 0, MASKED).astype(f)
    q = i % WINDOW
    off = i[None, :] - q[:, None]
    k["band"] = np.where((off >= 0) & (off < WINDOW), 0, MASKED).astype(f)
    heads = np.arange(A_HEADS)
    k["hmask"] = (i[:, None] // A_DH == heads[None, :] % (P // A_DH)).astype(f)
    k["own"] = (i[:, None] // WINDOW == np.arange(2)[None, :]).astype(f)
    k["sel64"] = (q[:, None] == np.arange(WINDOW)[None, :]).astype(f)
    job = np.arange(P)
    k["l_tile"] = (2 * (job % 16 // 4) + job % 2)[:, None] == np.arange(TT)[None, :]
    k["l_tile"] = k["l_tile"].astype(f)
    k["l_heads"] = ((job // 16)[:, None, None] == np.arange(L_PAIRS)[None, :, None]) & \
        ((job // 2 % 2)[:, None, None] == (i // 64)[None, None, :])
    k["l_heads"] = k["l_heads"].astype(f)
    t = np.arange(T, dtype=f)

    def angles(theta, d):
        freqs = (1.0 / f(theta) ** (np.arange(0, d, 2, dtype=f) / f(d))).astype(f)
        a = np.repeat(freqs, 2)[:, None] * t[None, :]
        sign = np.where(np.arange(d) % 2 == 0, -1, 1)[:, None]
        return np.cos(a.astype(np.float64)), np.sin(a.astype(np.float64)) * sign

    c, s = angles(100000.0, ROPE)
    kc = np.concatenate([np.ones((NOPE, T)), c])
    ks = np.concatenate([np.zeros((NOPE, T)), s])
    k["lcos"], k["lsin"] = np.tile(kc, (2, 1)).astype(f), np.tile(ks, (2, 1)).astype(f)
    c, s = angles(10000.0, C)
    scale = C ** -0.25
    km = lambda a: np.ascontiguousarray((a * scale).astype(f).reshape(KC, P, T).transpose(1, 0, 2))
    k["rcos"], k["rsin"] = km(c), km(s)
    for name, M in (("m0", MOE0), ("m1", MOE1)):
        E, R = M["experts"], M["routed"]
        e = np.arange(E)
        k[name + "_lower"] = np.broadcast_to((e[None, :] < e[:, None]).astype(f), (P, E, E)).copy()
        sel = np.zeros((P, R, P), f)
        for part in range(3):
            for j in range(R):
                for m in range(P):
                    sel[part * E + (j if E == R else 2 * j + m // 64), j, m] = 1
        k[name + "_sel"] = sel
    return k


def layouts(a):
    def km(w):
        return w.reshape(-1, P, w.shape[-1]).transpose(1, 0, 2)

    w = {"x": a["L0_attn_x"]}
    w["cT"] = np.stack([km(a[f"L{l}_c"].T) for l in range(2)])
    w["wmod"] = np.stack([km(a[f"L{l}_wmod"]) for l in range(2)])
    for n in "qkvo":
        w["a_w" + n] = km(a["L0_attn_W" + n].T)
    w["a_bo"] = a["L0_attn_bo"]
    w["l_wkva"] = km(a["L0_ffn_Wkva"])
    w["l_wq"] = a["L0_ffn_Wq"].reshape(KC, P, L_PAIRS, P).transpose(2, 1, 0, 3)
    w["l_wq"] = np.concatenate([w["l_wq"], w["l_wq"][0:1], w["l_wq"][0:1]])
    wkp = np.zeros((L_PAIRS, 64, 2, 64), np.float32)
    wkp[:, 0:32, :, 0:32] = a["L0_ffn_Wkvb"].reshape(32, L_PAIRS, 2, 32).transpose(1, 0, 2, 3)
    wkp[:, 32:64, :, 32:64] = np.eye(32, dtype=np.float32)[:, None, :]
    wkp = wkp.reshape(L_PAIRS, 64, P)
    w["l_wkp"] = np.concatenate([wkp, wkp[0:1], wkp[0:1]])
    wo = a["L0_ffn_Wo"].reshape(L_PAIRS, 2, 1, L_D, C)[:, :, :, :NOPE]
    w["l_wo"] = np.broadcast_to(wo, (L_PAIRS, 2, 2, NOPE, C)).reshape(L_PAIRS, P, C).transpose(1, 0, 2)
    w["l_ln1"] = a["L0_ffn_w_ln1"].reshape(KC, P).T
    w["m0_ln"] = a["L0_ffn_w_ln2"].reshape(KC, P).T

    def up(shared, each):
        return np.concatenate([shared, each]).reshape(-1, KC, P, P).transpose(2, 0, 1, 3)

    w["m0_wg"] = up(a["L0_ffn_sWg"], a["L0_ffn_Wg"])
    w["m0_wu"] = up(a["L0_ffn_sWu"], a["L0_ffn_Wu"])
    w["m0_wd"] = np.concatenate([a["L0_ffn_sWd"], a["L0_ffn_Wd"]]).transpose(1, 0, 2)
    w["m0_wr"] = km(a["L0_ffn_Wgate"])
    w["m0_rb"] = a["L0_ffn_expert_bias"]
    for n in "qkv":
        w["r_w" + n] = km(a["L1_attn_w" + n].T)
    two = lambda x: x.reshape(8, 2, C, 64).transpose(0, 2, 1, 3).reshape(8, C, P)
    tiles = lambda x: x.T.reshape(C, 4, P).transpose(1, 0, 2)
    w["m1_wg"] = up(tiles(a["L1_ffn_shared_gate_w"]), two(a["L1_ffn_gate_w"]))
    w["m1_wu"] = up(tiles(a["L1_ffn_shared_up_w"]), two(a["L1_ffn_up_w"]))
    w["m1_wd"] = np.concatenate([a["L1_ffn_shared_down_w"].T.reshape(4, P, C),
                                 a["L1_ffn_down_w"].reshape(8, P, C)]).transpose(1, 0, 2)
    w["m1_wr"] = km(a["L1_ffn_router_w"].T)
    w["m1_rb"] = a["L1_ffn_correction_bias"]
    return {n: np.ascontiguousarray(x) for n, x in w.items()}


def kernel(**inputs):
    import concourse.bacc as bacc
    from concourse.bass_utils import run_bass_kernel_spmd

    nc = bacc.Bacc("TRN2", target_bir_lowering=False, num_devices=1)
    arrays = {n: np.asarray(a) for n, a in inputs.items()}
    w, k = layouts(arrays), tables()
    feed = {}

    def declare(group):
        aps = {}
        for n, a in group.items():
            feed["in_" + n] = a
            aps[n] = nc.dram_tensor("in_" + n, a.shape, F32, kind="ExternalInput").ap()
        return aps

    out = nc.dram_tensor("out", (B, T, C), F32, kind="ExternalOutput").ap()
    build(nc, declare(w), declare(k), out)
    r = run_bass_kernel_spmd(nc, [feed], core_ids=[0])
    return r.results[0]["out"]
```
